# Optimizing a Trainium2 kernel written in Bass

```python
import numpy as np
import jax
import jax.numpy as jnp

def _softmax(x, axis=-1):
    return jax.nn.softmax(x, axis=axis)

def _gelu(x):
    return jax.nn.gelu(x, approximate=True)

def _silu(x):
    return jax.nn.silu(x)

def _sigmoid(x):
    return jax.nn.sigmoid(x)

def _layernorm(x, axis=-1, eps=1e-05):
    m = jnp.mean(x, axis=axis, keepdims=True)
    v = jnp.var(x, axis=axis, keepdims=True)
    return (x - m) / jnp.sqrt(v + eps)

def _scatter_add(tgt, idx, src, axis=0):
    return tgt.at[idx].add(src)

def _segment_sum(src, seg, n):
    return jax.ops.segment_sum(src, seg, n)
kernel_name = 'mk_seq_postln_d2_jaxref_r8_f72fbc'

def setup_inputs(seed: int=0):
    np.random.seed(seed)
    _w = jnp.asarray

    def _L0_attn_setup():
        import jax, jax.numpy as jnp
        import numpy as np
        D = 256
        key = jax.random.key(seed)
        ks = jax.random.split(key, 5)
        scale = 1.0 / np.sqrt(D)
        x = jax.random.normal(ks[0], (4, 512, D), dtype=jnp.float32)
        Wq = jax.random.normal(ks[1], (D, D), dtype=jnp.float32) * scale
        Wk = jax.random.normal(ks[2], (D, D), dtype=jnp.float32) * scale
        Wv = jax.random.normal(ks[3], (D, D), dtype=jnp.float32) * scale
        Wo = jax.random.normal(ks[4], (D, D), dtype=jnp.float32) * scale
        return {'x': x, 'Wq': Wq, 'Wk': Wk, 'Wv': Wv, 'Wo': Wo}
    _L0_attn_in = _L0_attn_setup()

    def _L0_ffn_setup():
        import jax, jax.numpy as jnp
        import numpy as np
        DIM = 256
        HID = 704
        ZERO_POINT = 128.0

        def _qlinear(x, wq, scale):
            W = (wq.astype(jnp.float32) - ZERO_POINT) * scale[:, None]
            return jnp.einsum('bsd,hd->bsh', x, W)
        key = jax.random.key(seed)
        ks = jax.random.split(key, 7)
        B, S = (4, 256)
        sg = jax.random.uniform(ks[1], (HID,)) * (0.02 / np.sqrt(DIM)) + 0.0001
        su = jax.random.uniform(ks[3], (HID,)) * (0.02 / np.sqrt(DIM)) + 0.0001
        sd = jax.random.uniform(ks[5], (DIM,)) * (0.02 / np.sqrt(HID)) + 0.0001
        return {'x': jax.random.normal(ks[0], (B, S, DIM), dtype=jnp.float32), 'wq_gate': jax.random.randint(ks[2], (HID, DIM), 0, 32, dtype=jnp.int32), 's_gate': sg, 'wq_up': jax.random.randint(ks[4], (HID, DIM), 0, 32, dtype=jnp.int32), 's_up': su, 'wq_down': jax.random.randint(ks[6], (DIM, HID), 0, 32, dtype=jnp.int32), 's_down': sd}
    _L0_ffn_in = _L0_ffn_setup()

    def _L1_attn_setup():
        import jax, jax.numpy as jnp
        import numpy as np
        B_SZ, SEQ, D_MODEL = (2, 256, 256)
        D_INNER, D_XB, INTER = (512, 128, 1024)
        HEADDIM = 64
        DSTATE = 64
        NHEADS = D_INNER // HEADDIM
        N_XB = D_XB // HEADDIM
        REP = NHEADS // N_XB
        D_IN_PROJ = D_INNER + D_XB + D_XB + D_INNER + NHEADS
        EPS = 1e-05

        def _layernorm(x, w, b):
            mu = jnp.mean(x, -1, keepdims=True)
            var = jnp.mean((x - mu) ** 2, -1, keepdims=True)
            return (x - mu) * jax.lax.rsqrt(var + EPS) * w + b

        def _mamba2(hs, W_in, dt_bias, A_log, D, norm_w, W_out):
            B, L, _ = hs.shape
            zxbcdt = hs @ W_in
            splits = [D_INNER, D_INNER + D_XB, D_INNER + 2 * D_XB, D_INNER + 2 * D_XB + D_INNER]
            z, xb, Bp, Cp, dt = jnp.split(zxbcdt, splits, axis=-1)
            xh = jnp.repeat(xb.reshape(B, L, N_XB, HEADDIM), REP, axis=2)
            Bh = jnp.repeat(Bp.reshape(B, L, N_XB, DSTATE), REP, axis=2)
            Ch = Cp.reshape(B, L, NHEADS, DSTATE)
            dt = jax.nn.softplus(dt + dt_bias)
            A = -jnp.exp(A_log)
            dA = jnp.exp(dt * A)

            def step(state, inp):
                dA_t, dt_t, B_t, x_t, C_t = inp
                dBx = (dt_t[:, :, None] * x_t)[..., None] * B_t[:, :, None, :]
                state = state * dA_t[:, :, None, None] + dBx
                y_t = jnp.einsum('bhpn,bhn->bhp', state, C_t)
                return (state, y_t)
            xs = (jnp.swapaxes(dA, 0, 1), jnp.swapaxes(dt, 0, 1), jnp.swapaxes(Bh, 0, 1), jnp.swapaxes(xh, 0, 1), jnp.swapaxes(Ch, 0, 1))
            state0 = jnp.zeros((B, NHEADS, HEADDIM, DSTATE), hs.dtype)
            _, ys = jax.lax.scan(step, state0, xs)
            y = jnp.swapaxes(ys, 0, 1) + D[None, None, :, None] * xh
            y = y.reshape(B, L, D_INNER)
            yg = y * jax.nn.silu(z)
            yn = yg * jax.lax.rsqrt(jnp.mean(yg * yg, -1, keepdims=True) + EPS) * norm_w
            return yn @ W_out
        key = jax.random.key(seed)
        ks = jax.random.split(key, 10)
        s = 0.02
        return {'hidden_states': jax.random.normal(ks[0], (B_SZ, SEQ, D_MODEL), jnp.float32), 'ln_w': jnp.ones((D_MODEL,), jnp.float32), 'ln_b': jnp.zeros((D_MODEL,), jnp.float32), 'W_in': jax.random.normal(ks[1], (D_MODEL, D_IN_PROJ), jnp.float32) * s, 'dt_bias': jax.random.uniform(ks[2], (NHEADS,), jnp.float32, -4.0, -2.0), 'A_log': jnp.log(jnp.arange(1, NHEADS + 1, dtype=jnp.float32)), 'D': jnp.ones((NHEADS,), jnp.float32), 'norm_w': jnp.ones((D_INNER,), jnp.float32), 'W_out': jax.random.normal(ks[3], (D_INNER, D_MODEL), jnp.float32) * s, 'fc1_w': jax.random.normal(ks[4], (D_MODEL, INTER), jnp.float32) * s, 'fc1_b': jnp.zeros((INTER,), jnp.float32), 'fc2_w': jax.random.normal(ks[5], (INTER, D_MODEL), jnp.float32) * s, 'fc2_b': jnp.zeros((D_MODEL,), jnp.float32)}
    _L1_attn_in = _L1_attn_setup()

    def _L1_ffn_setup():
        import jax, jax.numpy as jnp
        import numpy as np
        HIDDEN = 256
        INTER = 704
        B, S = (2, 256)

        def _ternary(key, shape):
            return jax.random.randint(key, shape, -1, 2).astype(jnp.float32)
        key = jax.random.key(seed)
        ks = jax.random.split(key, 7)
        x = jax.random.normal(ks[0], (B, S, HIDDEN), dtype=jnp.float32)
        gate_w = _ternary(ks[1], (INTER, HIDDEN))
        up_w = _ternary(ks[2], (INTER, HIDDEN))
        down_w = _ternary(ks[3], (HIDDEN, INTER))
        gate_s = jax.random.uniform(ks[4], (INTER,), minval=0.01, maxval=0.1, dtype=jnp.float32)
        up_s = jax.random.uniform(ks[5], (INTER,), minval=0.01, maxval=0.1, dtype=jnp.float32)
        down_s = jax.random.uniform(ks[6], (HIDDEN,), minval=0.01, maxval=0.1, dtype=jnp.float32)
        return {'x': x, 'gate_w': gate_w, 'up_w': up_w, 'down_w': down_w, 'gate_s': gate_s, 'up_s': up_s, 'down_s': down_s}
    _L1_ffn_in = _L1_ffn_setup()
    _d = {'L0_attn_x': _L0_attn_in['x'], 'L0_attn_Wq': _L0_attn_in['Wq'], 'L0_attn_Wk': _L0_attn_in['Wk'], 'L0_attn_Wv': _L0_attn_in['Wv'], 'L0_attn_Wo': _L0_attn_in['Wo'], 'L0_ffn_wq_gate': _L0_ffn_in['wq_gate'], 'L0_ffn_s_gate': _L0_ffn_in['s_gate'], 'L0_ffn_wq_up': _L0_ffn_in['wq_up'], 'L0_ffn_s_up': _L0_ffn_in['s_up'], 'L0_ffn_wq_down': _L0_ffn_in['wq_down'], 'L0_ffn_s_down': _L0_ffn_in['s_down'], 'L1_attn_ln_w': _L1_attn_in['ln_w'], 'L1_attn_ln_b': _L1_attn_in['ln_b'], 'L1_attn_W_in': _L1_attn_in['W_in'], 'L1_attn_dt_bias': _L1_attn_in['dt_bias'], 'L1_attn_A_log': _L1_attn_in['A_log'], 'L1_attn_D': _L1_attn_in['D'], 'L1_attn_norm_w': _L1_attn_in['norm_w'], 'L1_attn_W_out': _L1_attn_in['W_out'], 'L1_attn_fc1_w': _L1_attn_in['fc1_w'], 'L1_attn_fc1_b': _L1_attn_in['fc1_b'], 'L1_attn_fc2_w': _L1_attn_in['fc2_w'], 'L1_attn_fc2_b': _L1_attn_in['fc2_b'], 'L1_ffn_gate_w': _L1_ffn_in['gate_w'], 'L1_ffn_up_w': _L1_ffn_in['up_w'], 'L1_ffn_down_w': _L1_ffn_in['down_w'], 'L1_ffn_gate_s': _L1_ffn_in['gate_s'], 'L1_ffn_up_s': _L1_ffn_in['up_s'], 'L1_ffn_down_s': _L1_ffn_in['down_s']}
    _x0 = _d['L0_attn_x']
    _d['L0_attn_x'] = jax.random.normal(jax.random.fold_in(jax.random.key(seed), 1), (8, 512, 256), dtype=_x0.dtype)
    del _x0
    return _d

def reference(L0_attn_x, L0_attn_Wq, L0_attn_Wk, L0_attn_Wv, L0_attn_Wo, L0_ffn_wq_gate, L0_ffn_s_gate, L0_ffn_wq_up, L0_ffn_s_up, L0_ffn_wq_down, L0_ffn_s_down, L1_attn_ln_w, L1_attn_ln_b, L1_attn_W_in, L1_attn_dt_bias, L1_attn_A_log, L1_attn_D, L1_attn_norm_w, L1_attn_W_out, L1_attn_fc1_w, L1_attn_fc1_b, L1_attn_fc2_w, L1_attn_fc2_b, L1_ffn_gate_w, L1_ffn_up_w, L1_ffn_down_w, L1_ffn_gate_s, L1_ffn_up_s, L1_ffn_down_s):

    def _L0_attn_ref(x, Wq, Wk, Wv, Wo):
        import jax, jax.numpy as jnp
        import numpy as np
        D = 256
        q = jnp.einsum('bsd,ed->bse', x, Wq)
        k = jnp.einsum('bsd,ed->bse', x, Wk)
        v = jnp.einsum('bsd,ed->bse', x, Wv)
        seq = x.shape[-2]
        denom = jnp.sqrt(jnp.float32(x.shape[-1])) / seq
        kvt = jnp.cumsum(k * v, axis=-2) * denom
        vhat = q * kvt
        return jnp.einsum('bse,fe->bsf', vhat, Wo)

    def _L0_ffn_ref(x, wq_gate, s_gate, wq_up, s_up, wq_down, s_down):
        import jax, jax.numpy as jnp
        import numpy as np
        DIM = 256
        HID = 704
        ZERO_POINT = 128.0

        def _qlinear(x, wq, scale):
            W = (wq.astype(jnp.float32) - ZERO_POINT) * scale[:, None]
            return jnp.einsum('bsd,hd->bsh', x, W)
        gate = _qlinear(x, wq_gate, s_gate)
        gate = jax.nn.silu(gate)
        up = _qlinear(x, wq_up, s_up)
        return _qlinear(gate * up, wq_down, s_down)

    def _L1_attn_ref(hidden_states, ln_w, ln_b, W_in, dt_bias, A_log, D, norm_w, W_out, fc1_w, fc1_b, fc2_w, fc2_b):
        import jax, jax.numpy as jnp
        import numpy as np
        B_SZ, SEQ, D_MODEL = (2, 256, 256)
        D_INNER, D_XB, INTER = (512, 128, 1024)
        HEADDIM = 64
        DSTATE = 64
        NHEADS = D_INNER // HEADDIM
        N_XB = D_XB // HEADDIM
        REP = NHEADS // N_XB
        D_IN_PROJ = D_INNER + D_XB + D_XB + D_INNER + NHEADS
        EPS = 1e-05

        def _layernorm(x, w, b):
            mu = jnp.mean(x, -1, keepdims=True)
            var = jnp.mean((x - mu) ** 2, -1, keepdims=True)
            return (x - mu) * jax.lax.rsqrt(var + EPS) * w + b

        def _mamba2(hs, W_in, dt_bias, A_log, D, norm_w, W_out):
            B, L, _ = hs.shape
            zxbcdt = hs @ W_in
            splits = [D_INNER, D_INNER + D_XB, D_INNER + 2 * D_XB, D_INNER + 2 * D_XB + D_INNER]
            z, xb, Bp, Cp, dt = jnp.split(zxbcdt, splits, axis=-1)
            xh = jnp.repeat(xb.reshape(B, L, N_XB, HEADDIM), REP, axis=2)
            Bh = jnp.repeat(Bp.reshape(B, L, N_XB, DSTATE), REP, axis=2)
            Ch = Cp.reshape(B, L, NHEADS, DSTATE)
            dt = jax.nn.softplus(dt + dt_bias)
            A = -jnp.exp(A_log)
            dA = jnp.exp(dt * A)

            def step(state, inp):
                dA_t, dt_t, B_t, x_t, C_t = inp
                dBx = (dt_t[:, :, None] * x_t)[..., None] * B_t[:, :, None, :]
                state = state * dA_t[:, :, None, None] + dBx
                y_t = jnp.einsum('bhpn,bhn->bhp', state, C_t)
                return (state, y_t)
            xs = (jnp.swapaxes(dA, 0, 1), jnp.swapaxes(dt, 0, 1), jnp.swapaxes(Bh, 0, 1), jnp.swapaxes(xh, 0, 1), jnp.swapaxes(Ch, 0, 1))
            state0 = jnp.zeros((B, NHEADS, HEADDIM, DSTATE), hs.dtype)
            _, ys = jax.lax.scan(step, state0, xs)
            y = jnp.swapaxes(ys, 0, 1) + D[None, None, :, None] * xh
            y = y.reshape(B, L, D_INNER)
            yg = y * jax.nn.silu(z)
            yn = yg * jax.lax.rsqrt(jnp.mean(yg * yg, -1, keepdims=True) + EPS) * norm_w
            return yn @ W_out
        residual = hidden_states
        hs = _layernorm(hidden_states, ln_w, ln_b)
        attn = _mamba2(hs, W_in, dt_bias, A_log, D, norm_w, W_out)
        mlp = jax.nn.gelu(hs @ fc1_w + fc1_b, approximate=True) @ fc2_w + fc2_b
        return attn + mlp + residual

    def _L1_ffn_ref(x, gate_w, up_w, down_w, gate_s, up_s, down_s):
        import jax, jax.numpy as jnp
        import numpy as np
        HIDDEN = 256
        INTER = 704
        B, S = (2, 256)

        def _ternary(key, shape):
            return jax.random.randint(key, shape, -1, 2).astype(jnp.float32)
        b, s, h = x.shape
        xf = x.reshape(b * s, h)
        g = jnp.einsum('th,ih->ti', xf, gate_w) * gate_s
        u = jnp.einsum('th,ih->ti', xf, up_w) * up_s
        hdn = jax.nn.silu(g) * u
        out = jnp.einsum('ti,hi->th', hdn, down_w) * down_s
        return out.reshape(b, s, -1)
    x = L0_attn_x
    x = _layernorm(x + _L0_attn_ref(x, L0_attn_Wq, L0_attn_Wk, L0_attn_Wv, L0_attn_Wo), axis=-1)
    x = _layernorm(x + _L0_ffn_ref(x, L0_ffn_wq_gate, L0_ffn_s_gate, L0_ffn_wq_up, L0_ffn_s_up, L0_ffn_wq_down, L0_ffn_s_down), axis=-1)
    x = _layernorm(x + _L1_attn_ref(x, L1_attn_ln_w, L1_attn_ln_b, L1_attn_W_in, L1_attn_dt_bias, L1_attn_A_log, L1_attn_D, L1_attn_norm_w, L1_attn_W_out, L1_attn_fc1_w, L1_attn_fc1_b, L1_attn_fc2_w, L1_attn_fc2_b), axis=-1)
    x = _layernorm(x + _L1_ffn_ref(x, L1_ffn_gate_w, L1_ffn_up_w, L1_ffn_down_w, L1_ffn_gate_s, L1_ffn_up_s, L1_ffn_down_s), axis=-1)
    return x

_drawn_inputs = setup_inputs


def setup_inputs(seed=0):
    import zlib

    import numpy as np

    out = dict(_drawn_inputs(seed))
    spreads = {'L1_attn_ln_w': (1.0, 0.2),
     'L1_attn_ln_b': (0.0, 0.267),
     'L1_attn_D': (1.0, 0.2),
     'L1_attn_norm_w': (1.0, 0.2),
     'L1_attn_fc1_b': (0.0, 0.449),
     'L1_attn_fc2_b': (0.0, 0.1)}
    factors = {'L0_ffn_s_gate': 8.0,
     'L0_ffn_s_up': 8.0,
     'L0_ffn_s_down': 8.0,
     'L1_attn_dt_bias': 45.84,
     'L1_attn_A_log': 30.088}
    for name, (base, spread) in spreads.items():
        noise = np.random.default_rng([zlib.crc32(name.encode()), seed]).standard_normal(out[name].shape)
        drawn = base * np.exp(spread * noise) if base else spread * noise
        out[name] = jnp.asarray(drawn.astype(out[name].dtype))
    for name, factor in factors.items():
        out[name] = (out[name] * factor).astype(out[name].dtype)
    return out
```

```python
from contextlib import ExitStack

import numpy as np

import concourse.bass as bass
from concourse import mybir

ALU = mybir.AluOpType
ACT = mybir.ActivationFunctionType
F32 = mybir.dt.float32
F16 = mybir.dt.float16
I32 = mybir.dt.int32

P = 128
NB, S, D = 8, 512, 256
KD = D // P
NT = S // P
HID = 704
NPAIR = HID // P
NMIX = NPAIR
NUP = 2 * NPAIR + 1
HALF = P // 2
DI, DXB, NH, HD = 512, 128, 8, 64
NG = 2
GH = NH // NG
INTER = 1024
KI = DI // P
KF = INTER // P
CZ, CX, CDT, CC = 0, DI, DI + 2 * DXB, DI + 2 * DXB + NH
NSMALL = 2 * DXB + NH
WIN = CC + DI
EPS = 1e-5
WS = 64.0
ZERO_POINT = 128.0
DECAY_FLOOR = -110.0
MASKED = -30000.0
SSM_DENOM = float(D) ** 0.5 / S


def at(b, per, k):
    return b * per + k


def plan(names, first):
    count, uses = [0] * 4, {}
    for i, name in enumerate(names):
        uses[name] = (first + i % 4, count[i % 4])
        count[i % 4] += 1
    return uses, {first + j: count[j] for j in range(4)}


X_USES = ([f"{w}{m}" for m in range(KD) for w in "kvq"] + [f"o{i}" for i in range(NT // 2)]
          + [f"tr{m}" for m in range(KD)] + [f"up{t}" for t in range(NUP)] + [f"dn{i}" for i in range(NT // 2)])
Y_USES = ([f"tr{m}" for m in range(KD)] + ["bt"] + [f"ct{j}" for j in range(GH)] + [f"sm{i}" for i in range(NT)]
          + ["cum"] + [f"z{i}" for i in range(NT)])


def ssm_a(c):
    return [f"seg{c}_{g}" for g in range(NG)] + [f"g{c}_{g}" for g in range(NG)]


def ssm_b(c):
    return [f"yi{c}"] + ([f"ds{c}"] if c < NT - 1 else []) + ([f"yx{c}"] if c else [])


SCHED = [("Y", "tr"), ("X", "qkv"), ("Y", "proj"), ("Y", "fc1", 0, 4), ("X", "out"), ("Y", "fc1", 4, 8), ("X", "tr"),
         ("Y", "fc2"), ("Y", "ssm_a", 0), ("X", "up", 0, 4), ("Y", "ssm_a", 1), ("Y", "ssm_b", 0), ("X", "up", 4, 6),
         ("Y", "ssm_a", 2), ("Y", "ssm_b", 1), ("Y", "ssm_c", 0), ("X", "up", 6, 8), ("Y", "ssm_a", 3),
         ("Y", "ssm_b", 2), ("Y", "ssm_c", 1), ("X", "up", 8, 11), ("Y", "ssm_b", 3), ("Y", "ssm_c", 2),
         ("Y", "ssm_c", 3), ("Y", "out"), ("X", "down"), ("Y", "tr3"), ("Y", "up", 0, 11), ("Y", "down")]
Y_PARTS = {"ssm_a": ssm_a, "ssm_b": ssm_b, "ssm_c": lambda c: [f"ty{c}"],
           "fc1": lambda a, e: [f"f{t}" for t in range(a, e)], "fc2": lambda: [f"m{i}" for i in range(NT // 2)],
           "out": lambda: [f"o{i}" for i in range(NT // 2)], "tr3": lambda: [f"tq{m}" for m in range(KD)],
           "up": lambda a, e: [f"up{t}" for t in range(a, e)], "down": lambda: [f"dn{i}" for i in range(NT // 2)]}
for ch, kind, *arg in SCHED:
    if ch == "Y" and kind in Y_PARTS:
        Y_USES += Y_PARTS[kind](*arg)
XU, XN = plan(X_USES, 0)
YU, YN = plan(Y_USES, 4)
USES = {"X": (XU, XN), "Y": (YU, YN)}

WEIGHTS = [
    ("wqkv", KD, 3 * D, False, WS), ("wo", KD, D, False, WS), ("up0", KD, NUP * P, True, 1.0),
    ("dn0", NPAIR + 1, D, True, 1.0), ("win", KD, WIN, False, WS), ("fc1", KD, INTER, False, WS),
    ("wout", KI, D, False, WS), ("fc2", KF, D, False, WS), ("up1", KD, NUP * P, False, 1.0),
    ("dn1", NPAIR + 1, D, False, 1.0)]
COLS = {"lnw": KD, "lnb": KD, "fc1b": KF, "normw": KI, "sup0": NUP, "sup1": NUP}
ROWS = {"dtb": NH, "alog": NH, "dskip": NH, "sdn0": D, "sdn1": D, "fc2b": D}


def build(nc, ins, out):
    with ExitStack() as ctx:
        def sb(name, shape, dt=F32):
            return ctx.enter_context(nc.sbuf_tensor(name, shape, dt))

        def sem(name):
            return ctx.enter_context(nc.semaphore(name))

        bank = [ctx.enter_context(nc.psum_tensor(f"bank{i}", [P, 512], F32)) for i in range(8)]
        full = [sem(f"full{i}") for i in range(8)]

        hi = {n: sb(f"{n}_hi", [P, k, c], F16) for n, k, c, _, _ in WEIGHTS}
        lo = {n: sb(f"{n}_lo", [P, k, c], F16) for n, k, c, _, _ in WEIGHTS}
        STAGE = max(k * c for _, k, c, _, _ in WEIGHTS)
        NSTAGE = 1
        decay = sb("decay", [P, 3 * NH * P])
        stage = decay[:, 0:STAGE].unsqueeze(1)
        col = {n: sb(f"c_{n}", [P, c]) for n, c in COLS.items()}
        row = {n: sb(f"r_{n}", [P, c]) for n, c in ROWS.items()}
        ident = sb("ident", [P, P])
        allone = sb("allone", [P, P])
        upto = sb("upto", [P, P])
        after = sb("after", [P, P])
        negid = sb("negid", [P, P], F16)
        past = sb("past", [P, GH, P], F16)
        spare = sb("spare", [P, 1])
        half = sb("half", [P, NT])
        eps, ws2_di, ws2_eps = sb("eps", [P, NT]), sb("ws2_di", [P, NT]), sb("ws2_eps", [P, NT])
        aneg = sb("aneg", [P, NH])

        xt = sb("xt", [P, KD, S])
        xn = sb("xn", [P, NT, D])
        xh, xl = sb("xh", [P, KD, S], F16), sb("xl", [P, KD, S], F16)
        ksb = sb("ksb", [P, KD, S])
        kv = sb("kv", [P, S])
        vh32 = ksb
        vhh, vhl = sb("vhh", [P, KD, S], F16), sb("vhl", [P, KD, S], F16)
        x2 = sb("x2", [P, NT, D])
        hsh, hsl = sb("hsh", [P, KD, S], F16), sb("hsl", [P, KD, S], F16)
        bT = sb("bT", [P, S])
        cT = sb("cT", [P, GH, S])
        hs32 = cT[:, 0:KD, :]
        xbn = sb("xbn", [P, NT, 2 * DXB])
        zs = sb("zs", [P, NT, DI])
        dtz = sb("dtz", [P, NT * NH])
        dta, dte, dtu, dtl, dtd, dtq = (sb(n, [P, NT * NH]) for n in ("dta", "dte", "dtu", "dtl", "dtd", "dtq"))
        dt = sb("dt", [P, NT, NH])
        aexp = sb("aexp", [P, NT, NH])
        decs = sb("decs", [P, 3, NT, NH])
        E = decay[:, 0:2 * NH * P].rearrange("p (u h t) -> p u h t", u=2, h=NH)
        R = decay[:, 2 * NH * P:3 * NH * P].rearrange("p (h t) -> p h t", h=NH)
        xdt = sb("xdt", [P, NH, HD])
        xw = sb("xw", [P, NH, HD])
        st = sb("st", [P, NG, GH, HD])
        yy = sb("yy", [P, 2, DI])
        sq = sb("sq", [P, DI], F16)
        ss = sb("ss", [P, NT])
        rmsv, rms = sb("rmsv", [P, NT]), sb("rms", [P, NT])
        ygh, ygl = sb("ygh", [P, KI, S], F16), sb("ygl", [P, KI, S], F16)
        wide_h, wide_l = sb("wide_h", [P, KF, S], F16), sb("wide_l", [P, KF, S], F16)
        glh, gll = wide_h, wide_l
        F = {}
        for ch in "XY":
            F[ch] = dict(
                r=sb(f"r{ch}", [P, NT, D]), xa=sb("xaX", [P, NT, D]) if ch == "X" else x2,
                stats=sb(f"stats{ch}", [P, NT, 6]), mv=sb(f"mv{ch}", [P, NT, 2]),
                ve=sb(f"ve{ch}", [P, NT]), rs=sb(f"rs{ch}", [P, NT]),
                th=xh if ch == "X" else hsh, tl=xl if ch == "X" else hsl,
                sg=sb(f"sg{ch}", [P, S]), h32=sb(f"h32{ch}", [P, 2, S]), hh=wide_h, hl=wide_l)
        gl32 = F["Y"]["h32"]
        vx, rx2, vy, hsc, twice = (sb(n, [P, NT]) for n in ("vx", "rx2", "vy", "hsc", "twice"))
        hat = F["Y"]["r"]
        yout = sb("yout", [P, NT, D])

        w_in = sem("w_in")
        rows_in = sem("rows_in")
        w_scaled, w_hi, w_lo = sem("w_scaled"), sem("w_hi"), sem("w_lo")
        consts, masks, aneg_done = sem("consts"), sem("masks"), sem("aneg_done")
        xt_in, xn_in, stored = sem("xt_in"), sem("xn_in"), sem("stored")
        xh_done, xl_done, k_done, kv_done, cum_done, vh_done, vhh_done, vhl_done = (
            sem(n) for n in ("xh_done", "xl_done", "k_done", "kv_done", "cum_done", "vh_done", "vhh_done", "vhl_done"))
        C = {ch: {n: sem(f"{n}_{ch}") for n in (
            "part", "r", "stats", "mv", "ve", "rs", "xa", "th", "tl", "sg", "h", "hh", "hl")} for ch in "XY"}
        (rx2_done, vx_done, vxe_done, vy_done, hsc_done, twice_done, hat_done, x2_done, x2b_done, hs_done, hsh_done,
         hsl_done, bT_done, cT_done, xbn_done, dtz_done, z_done, absz_done, e_done, u_done, l_done, dt_step, dt_done,
         dta_done, a_done, decs_done, R_done, E_done, W_done, xdt_done, xw_done, st_step, st_done, dx_done, yi_done,
         yb_done, y_done, yg_done, ss_done, rms_step, rms_done, ygh_done, ygl_done, gl_done, glh_done, gll_done,
         m_done, yhalf_done, yout_done) = (sem(n) for n in (
             "rx2_done vx_done vxe_done vy_done hsc_done twice_done hat_done x2_done x2b_done hs_done hsh_done "
             "hsl_done bT_done cT_done xbn_done dtz_done z_done absz_done e_done u_done l_done dt_step dt_done "
             "dta_done a_done decs_done R_done E_done W_done xdt_done xw_done st_step st_done dx_done yi_done "
             "yb_done y_done yg_done ss_done rms_step rms_done ygh_done ygl_done gl_done glh_done gll_done "
             "m_done yhalf_done yout_done").split())

        RN = {"X": NT, "Y": NT}

        release = {"X": {}, "Y": {}}
        for m in range(KD):
            release["X"].update({f"k{m}": (k_done, KD, m + 1), f"v{m}": (kv_done, KD, m + 1),
                                 f"q{m}": (vh_done, KD, m + 1), f"tr{m}": (C["X"]["tl"], KD, m + 1)})
            release["Y"].update({f"tr{m}": (hs_done, KD, m + 1), f"tq{m}": (C["Y"]["tl"], KD, m + 1)})
        for ch in "XY":
            for t in range(2 * NPAIR):
                release[ch][f"up{t}"] = (C[ch]["h" if t % 2 else "sg"], NPAIR + 1, t // 2 + 1)
            release[ch][f"up{2 * NPAIR}"] = (C[ch]["h"], NPAIR + 1, NPAIR + 1)
            for i in range(NT // 2):
                release[ch][f"dn{i}"] = (C[ch]["part"], NT // 2, i + 1)
                release[ch][f"o{i}"] = (C[ch]["r"], RN[ch], i + 1)
        release["Y"].update(bt=(bT_done, 1, 1), cum=(decs_done, 1, 1))
        for j in range(GH):
            release["Y"][f"ct{j}"] = (cT_done, GH, j + 1)
        for i in range(NT // 2):
            release["Y"][f"m{i}"] = (m_done, NT // 2, i + 1)
        for t in range(KF):
            release["Y"][f"f{t}"] = (gl_done, KF, t + 1)
        for c in range(NT):
            release["Y"].update({f"sm{c}": (dtz_done, NT, c + 1), f"z{c}": (z_done, NT, c + 1),
                                 f"ds{c}": (st_done, NT - 1, c + 1), f"yi{c}": (yi_done, NT, c + 1),
                                 f"yx{c}": (y_done, NT - 1, c), f"ty{c}": (ygl_done, NT, c + 1)})
            for g in range(NG):
                release["Y"][f"seg{c}_{g}"] = (E_done, NT * NG, c * NG + g + 1)
                release["Y"][f"g{c}_{g}"] = (W_done, NT * NG, c * NG + g + 1)

        def wait_before(eng, signal, b, per, k):
            if not isinstance(b, int) or b:
                eng.wait_ge(signal, at(b, per, k - per))

        def filled(eng, ch, name, b):
            k, n = USES[ch][0][name]
            eng.wait_ge(full[k], at(b, USES[ch][1][k], n + 1))
            return bank[k]

        def use(ch, name):
            return USES[ch][0][name][0]

        def per_engine(eng, phases):
            def turn(bx, by):
                for ch, kind, *arg in SCHED:
                    b = bx if ch == "X" else by
                    if b is not None and (ch, kind) in phases:
                        phases[ch, kind](b, *arg)
            turn(0, None)
            turn(1, 0)
            with eng.Fori(2, NB) as i:
                turn(i, i - 1)
            turn(None, NB - 1)

        block = ctx.enter_context(nc.Block())

        @block.sync
        def _(sp):
            for n in COLS:
                sp.dma_start(col[n][:], ins[n]).then_inc(rows_in, 16)
            for n in ROWS:
                sp.dma_start(row[n][:], ins[n].partition_broadcast(P)).then_inc(rows_in, 16)

            def load_x(b):
                wait_before(sp, xl_done, b, 1, 1)
                sp.dma_start(xt[:], ins["xt"][bass.ds(b, 1)].rearrange("o (k p) s -> (o p) k s", p=P)).then_inc(xt_in, 16)
                wait_before(sp, C["X"]["r"], b, RN["X"], NT // 2)
                sp.dma_start(xn[:], ins["x"][bass.ds(b, 1)].rearrange("o (i p) d -> (o p) i d", p=P)).then_inc(xn_in, 16)

            def store(b):
                sp.wait_ge(yout_done, b + 1)
                sp.dma_start(out[bass.ds(b, 1)].rearrange("o (i p) d -> (o p) i d", p=P), yout[:]).then_inc(stored, 16)

            load_x(0)
            for i, (n, k, c, integer, _) in enumerate(WEIGHTS):
                if i:
                    sp.wait_ge(w_lo, i)
                dst = stage[:, 0, 0:k * c]
                sp.dma_start(dst.bitcast(I32) if integer else dst, ins[n]).then_inc(w_in, 16)
            load_x(1)
            with sp.Fori(2, NB) as b:
                load_x(b)
                store(b - 2)
            store(NB - 2)
            store(NB - 1)
            sp.wait_ge(stored, 16 * NB)

        @block.tensor
        def _(pe):
            def fill(ch, name, b):
                k, n = USES[ch][0][name]
                before = [u for u in USES[ch][0] if USES[ch][0][u] == (k, (n - 1) % USES[ch][1][k])][0]
                signal, per, which = release[ch][before]
                if n:
                    pe.wait_ge(signal, at(b, per, which))
                else:
                    wait_before(pe, signal, b, per, which)
                return bank[k]

            def three(dst, lh, ll, rh, rl, first=True, last=True):
                nc.tensor.matmul(dst, lh, rh, start=first, stop=False)
                nc.tensor.matmul(dst, lh, rl, start=False, stop=False)
                return nc.tensor.matmul(dst, ll, rh, start=False, stop=last)

            def product(dst, lh, ll, rh, rl, tiles):
                for n, k in enumerate(tiles):
                    last = three(dst, lh(k), ll(k), rh(k), rl(k), n == 0, n == len(tiles) - 1)
                return last

            def chan_tile(dst, w, c0, act_h, act_l, m=P):
                return product(dst, lambda k: hi[w][:, k, c0:c0 + m], lambda k: lo[w][:, k, c0:c0 + m],
                               lambda k: act_h[:, k, :], lambda k: act_l[:, k, :], range(KD))

            def tok_tile(dst, i, act_h, act_l, w, c0, n, tiles):
                return product(dst, lambda k: act_h[:, k, i * P:(i + 1) * P], lambda k: act_l[:, k, i * P:(i + 1) * P],
                               lambda k: hi[w][:, k, c0:c0 + n], lambda k: lo[w][:, k, c0:c0 + n], tiles)

            def transposes(ch, b, names, src):
                for m in range(KD):
                    dst = fill(ch, names[m], b)
                    for i in range(NT):
                        last = nc.tensor.transpose(dst[:, i * P:(i + 1) * P], src[:, i, m * P:(m + 1) * P], ident[:])
                    last.then_inc(full[use(ch, names[m])], 1)

            def qkv(b):
                pe.wait_ge(xl_done, at(b, 1, 1))
                for m in range(KD):
                    for w, c0 in (("k", D), ("v", 2 * D), ("q", 0)):
                        dst = fill("X", f"{w}{m}", b)
                        chan_tile(dst[:], "wqkv", c0 + m * P, xh, xl).then_inc(full[use("X", f"{w}{m}")], 1)

            def attn_out(b):
                pe.wait_ge(vhl_done, at(b, KD, KD))
                for i in range(NT):
                    name = f"o{i // 2}"
                    dst = fill("X", name, b) if i % 2 == 0 else dst
                    last = tok_tile(dst[:, i % 2 * D:(i % 2 + 1) * D], i, vhh, vhl, "wo", 0, D, range(KD))
                    if i % 2:
                        last.then_inc(full[use("X", name)], 1)

            def x_tr(b):
                pe.wait_ge(C["X"]["xa"], at(b, 1, 1))
                transposes("X", b, ["tr0", "tr1"], F["X"]["xa"])

            def up(ch, w):
                def go(b, a, e):
                    pe.wait_ge(C[ch]["tl"], at(b, KD, KD))
                    for t in range(a, e):
                        dst = fill(ch, f"up{t}", b)
                        chan_tile(dst[:], w, t * P, F[ch]["th"], F[ch]["tl"]).then_inc(full[use(ch, f"up{t}")], 1)
                return go

            def down(ch, w):
                def go(b):
                    hh, hl = F[ch]["hh"], F[ch]["hl"]
                    pe.wait_ge(C[ch]["hl"], at(b, NPAIR + 1, NPAIR + 1))
                    for i in range(NT):
                        name = f"dn{i // 2}"
                        dst = fill(ch, name, b) if i % 2 == 0 else dst
                        o = dst[:, i % 2 * D:(i % 2 + 1) * D]
                        tok_part = slice(i * P, (i + 1) * P)
                        for k in range(NPAIR + 1):
                            p0 = 0 if k < NPAIR else HALF
                            last = three(o, hh[p0:P, k, tok_part], hl[p0:P, k, tok_part], hi[w][p0:P, k, :],
                                         lo[w][p0:P, k, :], k == 0, k == NPAIR)
                        if i % 2:
                            last.then_inc(full[use(ch, name)], 1)
                return go

            def y_tr(b):
                pe.wait_ge(hat_done, at(b, 1, 1))
                transposes("Y", b, ["tr0", "tr1"], hat)

            def proj(b):
                pe.wait_ge(hsl_done, at(b, KD, KD))
                dst = fill("Y", "bt", b)
                chan_tile(dst[:], "win", CX + DXB, hsh, hsl).then_inc(full[use("Y", "bt")], 1)
                for j in range(GH):
                    dst = fill("Y", f"ct{j}", b)
                    chan_tile(dst[:], "win", CC + j * P, hsh, hsl).then_inc(full[use("Y", f"ct{j}")], 1)
                for i in range(NT):
                    dst = fill("Y", f"sm{i}", b)
                    tok_tile(dst[:, 0:NSMALL], i, hsh, hsl, "win", CX, NSMALL, range(KD)).then_inc(
                        full[use("Y", f"sm{i}")], 1)
                dst = fill("Y", "cum", b)
                pe.wait_ge(a_done, at(b, 1, 1))
                av = aexp[:].rearrange("p c h -> p (c h)")
                nc.tensor.matmul(dst[:, 0:NT * NH], upto[:], av, start=True, stop=True)
                nc.tensor.matmul(dst[:, NT * NH:2 * NT * NH], allone[:], av, start=True, stop=True)
                nc.tensor.matmul(dst[:, 2 * NT * NH:3 * NT * NH], after[:], av, start=True, stop=True).then_inc(
                    full[use("Y", "cum")], 1)
                for i in range(NT):
                    dst = fill("Y", f"z{i}", b)
                    tok_tile(dst[:], i, hsh, hsl, "win", CZ, DI, range(KD)).then_inc(full[use("Y", f"z{i}")], 1)

            def pe_ssm_a(b, c):
                tok_part = slice(c * P, (c + 1) * P)
                for g in range(NG):
                    dst = fill("Y", f"seg{c}_{g}", b)
                    if g == 0:
                        pe.wait_ge(R_done, at(b, NT, c + 1))
                    nc.tensor.matmul(dst[:], after[:], R[:, g * GH:(g + 1) * GH, :], start=True, stop=False)
                    nc.tensor.matmul(dst[:], negid[:], past[:], start=False, stop=True).then_inc(
                        full[use("Y", f"seg{c}_{g}")], 1)
                for g in range(NG):
                    dst = fill("Y", f"g{c}_{g}", b)
                    if g == 0:
                        pe.wait_ge(cT_done, at(b, GH, GH))
                        pe.wait_ge(bT_done, at(b, 1, 1))
                    part = slice(g * HD, (g + 1) * HD)
                    nc.tensor.matmul(dst[:], bT[part, tok_part], cT[part, :, tok_part], start=True, stop=True).then_inc(
                        full[use("Y", f"g{c}_{g}")], 1)

            def pe_ssm_b(b, c):
                tok_part = slice(c * P, (c + 1) * P)
                dst = fill("Y", f"yi{c}", b)
                pe.wait_ge(xdt_done, at(b, NT, c + 1))
                pe.wait_ge(W_done, at(b, NT * NG, (c + 1) * NG))
                for h in range(NH):
                    last = nc.tensor.matmul(dst[:, h * HD:(h + 1) * HD], E[:, c % 2, h, :], xdt[:, h, :],
                                            start=True, stop=True)
                last.then_inc(full[use("Y", f"yi{c}")], 1)
                if c < NT - 1:
                    dst = fill("Y", f"ds{c}", b)
                    pe.wait_ge(xw_done, at(b, NT - 1, c + 1))
                    pe.wait_ge(xbn_done, at(b, NT, c + 1))
                    nc.tensor.matmul(dst[:], xbn[:, c, DXB:2 * DXB], xw[:].rearrange("p h d -> p (h d)"),
                                     start=True, stop=True).then_inc(full[use("Y", f"ds{c}")], 1)
                if c:
                    dst = fill("Y", f"yx{c}", b)
                    pe.wait_ge(st_done, at(b, NT - 1, c))
                    d4 = dst[:].rearrange("p (g j d) -> p g j d", g=NG, j=GH)
                    for j in range(GH):
                        last = nc.tensor.matmul(d4[:, :, j, :], cT[:, j, tok_part], st[:, :, j, :],
                                                start=True, stop=True)
                    last.then_inc(full[use("Y", f"yx{c}")], 1)

            def pe_ssm_c(b, c):
                dst = fill("Y", f"ty{c}", b)
                pe.wait_ge(yg_done, at(b, NT, c + 1))
                for k in range(KI):
                    last = nc.tensor.transpose(dst[:, k * P:(k + 1) * P], yy[:, c % 2, k * P:(k + 1) * P], ident[:])
                last.then_inc(full[use("Y", f"ty{c}")], 1)

            def fc1(b, a, e):
                for t in range(a, e):
                    dst = fill("Y", f"f{t}", b)
                    chan_tile(dst[:], "fc1", t * P, hsh, hsl).then_inc(full[use("Y", f"f{t}")], 1)

            def tok_pairs(b, names, a_h, a_l, w, tiles):
                for i in range(NT):
                    dst = fill("Y", names[i // 2], b) if i % 2 == 0 else dst
                    last = tok_tile(dst[:, i % 2 * D:(i % 2 + 1) * D], i, a_h, a_l, w, 0, D, tiles)
                    if i % 2:
                        last.then_inc(full[use("Y", names[i // 2])], 1)

            def fc2(b):
                pe.wait_ge(gll_done, at(b, KF, KF))
                tok_pairs(b, ["m0", "m1"], glh, gll, "fc2", range(KF))

            def y_out(b):
                pe.wait_ge(ygl_done, at(b, NT, NT))
                tok_pairs(b, ["o0", "o1"], ygh, ygl, "wout", range(KI))

            def y_tr3(b):
                pe.wait_ge(C["Y"]["xa"], at(b, 1, 1))
                transposes("Y", b, ["tq0", "tq1"], F["Y"]["xa"])

            pe.wait_ge(masks, 5)
            pe.wait_ge(w_lo, len(WEIGHTS))
            per_engine(pe, {
                ("X", "qkv"): qkv, ("X", "out"): attn_out, ("X", "tr"): x_tr, ("X", "up"): up("X", "up0"),
                ("X", "down"): down("X", "dn0"), ("Y", "tr"): y_tr, ("Y", "proj"): proj, ("Y", "ssm_a"): pe_ssm_a,
                ("Y", "ssm_b"): pe_ssm_b, ("Y", "ssm_c"): pe_ssm_c, ("Y", "fc1"): fc1, ("Y", "fc2"): fc2,
                ("Y", "out"): y_out, ("Y", "tr3"): y_tr3, ("Y", "up"): up("Y", "up1"), ("Y", "down"): down("Y", "dn1")})

        @block.scalar
        def _(act):
            act.wait_ge(rows_in, 16 * (len(COLS) + len(ROWS)))
            nc.scalar.activation(aneg[:], row["alog"][:], ACT.Exp).then_inc(aneg_done, 1)
            for i, (n, k, c, _, _) in enumerate(WEIGHTS):
                act.wait_ge(w_scaled, i + 1)
                nc.scalar.copy(hi[n][:].rearrange("p k c -> p (k c)"), stage[:, 0, 0:k * c]).then_inc(w_hi, 1)

            def qkv(b):
                act.wait_ge(xt_in, at(b, 16, 16))
                nc.scalar.copy(xh[:], xt[:]).then_inc(xh_done, 1)
                for m in range(KD):
                    src = filled(act, "X", f"k{m}", b)
                    nc.scalar.activation(ksb[:, m, :], src[:], ACT.Copy, scale=WS ** -2).then_inc(k_done, 1)
                for m in range(KD):
                    act.wait_ge(vh_done, at(b, KD, m + 1))
                    nc.scalar.copy(vhh[:, m, :], vh32[:, m, :]).then_inc(vhh_done, 1)

            def split_tr(ch, names):
                def go(b):
                    for m in range(KD):
                        src = filled(act, ch, names[m], b)
                        nc.scalar.copy(F[ch]["th"][:, m, :], src[:]).then_inc(C[ch]["th"], 1)
                return go

            def up(ch, scales):
                def go(b, a, e):
                    f = F[ch]
                    for t in range(a, e):
                        p0, p1 = (0, P) if t < 2 * NPAIR else (HALF, P)
                        pair = t // 2 if t < 2 * NPAIR else NPAIR
                        if t % 2 == 0:
                            src = filled(act, ch, f"up{t}", b)
                            if pair:
                                act.wait_ge(C[ch]["h"], at(b, NPAIR + 1, pair))
                            if t < 2 * NPAIR:
                                nc.scalar.activation(f["sg"][:], src[:], ACT.Silu,
                                                     scale=col[scales][:, t:t + 1]).then_inc(C[ch]["sg"], 1)
                            else:
                                nc.scalar.activation(f["sg"][HALF:P, :], src[0:HALF, :], ACT.Silu,
                                                     scale=col[scales][0:HALF, t:t + 1]).then_inc(C[ch]["sg"], 1)
                        if t % 2 or t == 2 * NPAIR:
                            act.wait_ge(C[ch]["h"], at(b, NPAIR + 1, pair + 1))
                            nc.scalar.copy(f["hh"][p0:P, pair, :], f["h32"][p0:P, pair % 2, :]).then_inc(C[ch]["hh"], 1)
                return go

            def y_tr(b):
                for m in range(KD):
                    src = filled(act, "Y", f"tr{m}", b)
                    nc.scalar.activation(hs32[:, m, :], src[:], ACT.Identity, bias=col["lnb"][:, m:m + 1],
                                         scale=col["lnw"][:, m:m + 1]).then_inc(hs_done, 1)

            def proj(b):
                src = filled(act, "Y", "bt", b)
                nc.scalar.activation(bT[:], src[:], ACT.Copy, scale=1 / WS).then_inc(bT_done, 1)
                for j in range(GH):
                    src = filled(act, "Y", f"ct{j}", b)
                    nc.scalar.activation(cT[:, j, :], src[:], ACT.Copy, scale=1 / WS).then_inc(cT_done, 1)
                for i in range(NT):
                    src = filled(act, "Y", f"sm{i}", b)
                    nc.scalar.activation(xbn[:, i, :], src[:, 0:2 * DXB], ACT.Copy, scale=1 / WS).then_inc(xbn_done, 1)
                act.preload_act_table_set("natural_log_exp_and_others")
                act.wait_ge(absz_done, at(b, 1, 1))
                nc.scalar.activation(dte[:], dta[:], ACT.Exp, scale=-1.0).then_inc(e_done, 1)
                act.wait_ge(u_done, at(b, 1, 1))
                nc.scalar.activation(dtl[:], dtu[:], ACT.Ln).then_inc(l_done, 1)
                src = filled(act, "Y", "cum", b)
                nc.scalar.activation(decs[:].rearrange("p w c h -> p (w c h)"), src[:, 0:3 * NT * NH], ACT.Exp).then_inc(
                    decs_done, 1)
                for i in range(NT):
                    src = filled(act, "Y", f"z{i}", b)
                    nc.scalar.activation(zs[:, i, :], src[:], ACT.Silu, scale=1 / WS).then_inc(z_done, 1)

            def ssm_a(b, c):
                if c >= 2:
                    filled(act, "Y", f"yi{c - 2}", b)
                for g in range(NG):
                    src = filled(act, "Y", f"seg{c}_{g}", b)
                    nc.scalar.activation(E[:, c % 2, g * GH:(g + 1) * GH, :].rearrange("p h t -> p (h t)"), src[:],
                                         ACT.Exp).then_inc(E_done, 1)

            def ssm_c(b, c):
                act.wait_ge(yg_done, at(b, NT, c + 1))
                if c:
                    act.wait_ge(ss_done, at(b, NT, c))
                nc.scalar.activation(sq[:], yy[:, c % 2, :], ACT.Square, accum_out=ss[:, c:c + 1]).then_inc(ss_done, 1)
                src = filled(act, "Y", f"ty{c}", b)
                nc.scalar.copy(ygh[:, :, c * P:(c + 1) * P], src[:].rearrange("p (k t) -> p k t", k=KI)).then_inc(
                    ygh_done, 1)

            def fc1(b, a, e):
                for t in range(a, e):
                    src = filled(act, "Y", f"f{t}", b)
                    if t >= 2:
                        act.wait_ge(gll_done, at(b, KF, t - 1))
                    nc.scalar.activation(gl32[:, t % 2, :], src[:], ACT.Gelu_apprx_tanh, bias=col["fc1b"][:, t:t + 1],
                                         scale=1 / WS).then_inc(gl_done, 1)

            per_engine(act, {
                ("X", "qkv"): qkv, ("X", "tr"): split_tr("X", ["tr0", "tr1"]), ("X", "up"): up("X", "sup0"),
                ("Y", "tr"): y_tr, ("Y", "proj"): proj, ("Y", "ssm_a"): ssm_a, ("Y", "ssm_c"): ssm_c,
                ("Y", "fc1"): fc1, ("Y", "tr3"): split_tr("Y", ["tq0", "tq1"]), ("Y", "up"): up("Y", "sup1")})

        @block.vector
        def _(dve):
            v = nc.vector
            v.memset(allone[:], 1.0).then_inc(consts, 1)
            v.memset(st[:], 0.0).then_inc(consts, 1)
            for tile, value in ((half, -0.5), (eps, EPS), (ws2_di, WS ** 2 / DI), (ws2_eps, WS ** 2 * EPS)):
                v.memset(tile[:], value).then_inc(consts, 1)
            dve.wait_ge(rows_in, 16 * (len(COLS) + len(ROWS)))
            dve.wait_ge(aneg_done, 1)
            v.tensor_scalar(aneg[:], aneg[:], -1.0, None, ALU.mult).then_inc(aneg_done, 1)
            for i, (n, k, c, integer, scale) in enumerate(WEIGHTS):
                s32 = stage[:, 0, 0:k * c]
                dve.wait_ge(w_in, 16 * (i + 1))
                if n == "wout":
                    for kk in range(KI):
                        part = s32[:, kk * c:(kk + 1) * c]
                        last = v.tensor_scalar(part, part, col["normw"][:, kk:kk + 1], scale, ALU.mult, ALU.mult)
                    last.then_inc(w_scaled, 1)
                elif integer:
                    v.tensor_scalar(s32, s32.bitcast(I32), -ZERO_POINT, scale, ALU.add, ALU.mult).then_inc(w_scaled, 1)
                else:
                    v.tensor_scalar(s32, s32, scale, None, ALU.mult).then_inc(w_scaled, 1)
                dve.wait_ge(w_scaled, i + 1)
                dve.wait_ge(w_hi, i + 1)
                v.tensor_tensor(lo[n][:].rearrange("p k c -> p (k c)"), s32, hi[n][:].rearrange("p k c -> p (k c)"),
                                ALU.subtract).then_inc(w_lo, 1)

            def low(out, src, high):
                return v.tensor_tensor(out, src, high, ALU.subtract)

            def norm_stats(ch, b, turn):
                f, c = F[ch], C[ch]
                dve.wait_ge(c["r"], at(b, RN[ch], NT // 2 * (turn + 1)))
                for i in range(NT):
                    v.bn_stats(f["stats"][:, i, :], f["r"][:, i, :]).then_inc(c["stats"], 1)
                dve.wait_ge(c["stats"], at(b, 2 * NT, (turn + 1) * NT))
                v.memset(spare[:], 0.0)
                for i in range(NT):
                    last = v.bn_aggr(f["mv"][:, i, :], f["stats"][:, i, :])
                last.then_inc(c["mv"], 1)

            def normed(ch, out, scale, done):
                f = F[ch]
                for i in range(NT):
                    last = v.tensor_scalar(out[:, i, :], f["r"][:, i, :], f["mv"][:, i, 0:1], scale[:, i:i + 1],
                                           ALU.subtract, ALU.mult)
                last.then_inc(done, 1)

            def qkv(b):
                dve.wait_ge(xh_done, at(b, 1, 1))
                low(xl[:], xt[:], xh[:]).then_inc(xl_done, 1)
                for m in range(KD):
                    src = filled(dve, "X", f"v{m}", b)
                    dve.wait_ge(k_done, at(b, KD, m + 1))
                    if m:
                        dve.wait_ge(vh_done, at(b, KD, m))
                    v.tensor_tensor(kv[:], ksb[:, m, :], src[:], ALU.mult).then_inc(kv_done, 1)
                    dve.wait_ge(kv_done, at(b, KD, m + 1))
                    v.tensor_tensor_scan(kv[:], allone[:, 0:1].to_broadcast([P, S]), kv[:], 0.0, ALU.mult,
                                         ALU.add).then_inc(cum_done, 1)
                    src = filled(dve, "X", f"q{m}", b)
                    dve.wait_ge(cum_done, at(b, KD, m + 1))
                    v.scalar_tensor_tensor(out=vh32[:, m, :], in0=src[:], scalar=SSM_DENOM / WS, in1=kv[:],
                                           op0=ALU.mult, op1=ALU.mult).then_inc(vh_done, 1)

            def attn_out(b):
                f = F["X"]
                dve.wait_ge(xn_in, at(b, 16, 16))
                for i in range(NT // 2):
                    src = filled(dve, "X", f"o{i}", b)
                    pair = slice(2 * i, 2 * i + 2)
                    v.scalar_tensor_tensor(out=f["r"][:, pair, :].rearrange("p i d -> p (i d)"), in0=src[:],
                                           scalar=1 / WS, in1=xn[:, pair, :].rearrange("p i d -> p (i d)"),
                                           op0=ALU.mult, op1=ALU.add).then_inc(C["X"]["r"], 1)
                norm_stats("X", b, 0)
                dve.wait_ge(C["X"]["rs"], at(b, 2, 1))
                normed("X", f["xa"], f["rs"], C["X"]["xa"])

            def split_tr(ch, names):
                def go(b):
                    for m in range(KD):
                        dve.wait_ge(C[ch]["th"], at(b, KD, m + 1))
                        low(F[ch]["tl"][:, m, :], bank[use(ch, names[m])][:], F[ch]["th"][:, m, :]).then_inc(
                            C[ch]["tl"], 1)
                return go

            def up(ch, scales):
                def go(b, a, e):
                    f = F[ch]
                    for t in range(a, e):
                        if t % 2 == 0 and t < 2 * NPAIR:
                            continue
                        pair = t // 2
                        p0 = 0 if t < 2 * NPAIR else HALF
                        src = filled(dve, ch, f"up{t}", b)
                        dve.wait_ge(C[ch]["sg"], at(b, NPAIR + 1, pair + 1))
                        if pair >= 2:
                            dve.wait_ge(C[ch]["hl"], at(b, NPAIR + 1, pair - 1))
                        v.scalar_tensor_tensor(out=f["h32"][p0:P, pair % 2, :], in0=src[p0:P, :],
                                               scalar=col[scales][p0:P, t:t + 1], in1=f["sg"][p0:P, :],
                                               op0=ALU.mult, op1=ALU.mult).then_inc(C[ch]["h"], 1)
                return go

            def down(ch, scale_row):
                def go(b):
                    f = F[ch]
                    s2 = row[scale_row][:].unsqueeze(1).to_broadcast([P, 2, D])
                    for i in range(NT // 2):
                        src = filled(dve, ch, f"dn{i}", b)
                        r = f["r"][:, 2 * i:2 * i + 2, :]
                        v.tensor_tensor(r, src[:].rearrange("p (i d) -> p i d", i=2), s2, ALU.mult).then_inc(
                            C[ch]["part"], 1)
                        dve.wait_ge(C[ch]["part"], at(b, NT // 2, i + 1))
                        v.tensor_tensor(r, r, f["xa"][:, 2 * i:2 * i + 2, :], ALU.add).then_inc(C[ch]["r"], 1)
                    norm_stats(ch, b, 1)
                    if ch == "Y":
                        dve.wait_ge(C["Y"]["rs"], at(b, 2, 2))
                        wait_before(dve, stored, b, 16, 16)
                        normed("Y", yout, f["rs"], yout_done)
                return go

            def y_tr(b):
                wait_before(dve, yout_done, b, 1, 1)
                dve.wait_ge(hsc_done, at(b, 1, 1))
                normed("X", hat, hsc, hat_done)
                dve.wait_ge(twice_done, at(b, 1, 1))
                normed("X", x2, twice, x2_done)
                for m in range(KD):
                    dve.wait_ge(hs_done, at(b, KD, m + 1))
                    v.tensor_copy(hsh[:, m, :], hs32[:, m, :]).then_inc(hsh_done, 1)
                    dve.wait_ge(hsh_done, at(b, KD, m + 1))
                    low(hsl[:, m, :], hs32[:, m, :], hsh[:, m, :]).then_inc(hsl_done, 1)

            def proj(b):
                for i in range(NT):
                    src = filled(dve, "Y", f"sm{i}", b)
                    dve.wait_ge(xbn_done, at(b, NT, i + 1))
                    v.scalar_tensor_tensor(out=dtz[:, i * NH:(i + 1) * NH], in0=src[:, 2 * DXB:NSMALL], scalar=1 / WS,
                                           in1=row["dtb"][:], op0=ALU.mult, op1=ALU.add).then_inc(dtz_done, 1)
                dve.wait_ge(dtz_done, at(b, NT, NT))
                v.scalar_tensor_tensor(out=dta[:], in0=dtz[:], scalar=-1.0, in1=dtz[:], op0=ALU.mult,
                                       op1=ALU.max).then_inc(absz_done, 1)
                dve.wait_ge(e_done, at(b, 1, 1))
                v.tensor_scalar(dtu[:], dte[:], 1.0, None, ALU.add).then_inc(u_done, 1)
                dve.wait_ge(u_done, at(b, 1, 1))
                v.tensor_scalar(dtd[:], dtu[:], -1.0, None, ALU.add).then_inc(dt_step, 1)
                dve.wait_ge(dt_step, at(b, 9, 1))
                v.tensor_scalar(dtq[:], dtd[:], -0.5, 1.0, ALU.mult, ALU.add).then_inc(dt_step, 1)
                dve.wait_ge(dt_step, at(b, 9, 2))
                v.tensor_tensor(dtq[:], dtq[:], dtd[:], ALU.mult).then_inc(dt_step, 1)
                dve.wait_ge(dt_step, at(b, 9, 3))
                dve.wait_ge(l_done, at(b, 1, 1))
                v.tensor_tensor(dtq[:], dtq[:], dtl[:], ALU.max).then_inc(dt_step, 1)
                dve.wait_ge(dt_step, at(b, 9, 4))
                v.tensor_tensor(dtq[:], dtq[:], dtd[:], ALU.min).then_inc(dt_step, 1)
                dve.wait_ge(dt_step, at(b, 9, 5))
                v.tensor_scalar(dtd[:], dtd[:], 1e-30, None, ALU.add).then_inc(dt_step, 1)
                dve.wait_ge(dt_step, at(b, 9, 6))
                v.reciprocal(dtd[:], dtd[:]).then_inc(dt_step, 1)
                dve.wait_ge(dt_step, at(b, 9, 7))
                v.scalar_tensor_tensor(out=dtq[:], in0=dtq[:], scalar=1e-30, in1=dtd[:], op0=ALU.add,
                                       op1=ALU.mult).then_inc(dt_step, 1)
                dve.wait_ge(dt_step, at(b, 9, 8))
                v.tensor_tensor(dtq[:], dtq[:], dte[:], ALU.mult).then_inc(dt_step, 1)
                dve.wait_ge(dt_step, at(b, 9, 9))
                v.scalar_tensor_tensor(out=dt[:].rearrange("p c h -> p (c h)"), in0=dtz[:], scalar=0.0, in1=dtq[:],
                                       op0=ALU.max, op1=ALU.add).then_inc(dt_done, 1)
                dve.wait_ge(dt_done, at(b, 1, 1))
                v.tensor_tensor(dta[:].rearrange("p (c h) -> p c h", c=NT), dt[:],
                                aneg[:].unsqueeze(1).to_broadcast([P, NT, NH]), ALU.mult).then_inc(dta_done, 1)
                dve.wait_ge(dta_done, at(b, 1, 1))
                v.tensor_scalar(aexp[:].rearrange("p c h -> p (c h)"), dta[:], DECAY_FLOOR, None, ALU.max).then_inc(
                    a_done, 1)

            def ssm_a(b, c):
                for g in range(NG):
                    src = filled(dve, "Y", f"g{c}_{g}", b)
                    dve.wait_ge(E_done, at(b, NT * NG, c * NG + g + 1))
                    w = E[:, c % 2, g * GH:(g + 1) * GH, :].rearrange("p h t -> p (h t)")
                    v.tensor_tensor(w, src[:], w, ALU.mult).then_inc(W_done, 1)

            def ssm_b(b, c):
                if c < NT - 1:
                    dve.wait_ge(decs_done, at(b, 1, 1))
                    src = filled(dve, "Y", f"ds{c}", b)
                    for g in range(NG):
                        part = slice(g * HD, (g + 1) * HD)
                        own = src[part, g * GH * HD:(g + 1) * GH * HD].rearrange("p (j d) -> p j d", j=GH)
                        if c == 0:
                            last = v.tensor_copy(st[part, g, :, :], own)
                        else:
                            filled(dve, "Y", f"yx{c}", b)
                            dve.wait_ge(st_done, at(b, NT - 1, c))
                            v.tensor_tensor(st[part, g, :, :], st[part, g, :, :],
                                            decs[part, 1, c, g * GH:(g + 1) * GH].unsqueeze(2).to_broadcast([HD, GH, HD]),
                                            ALU.mult).then_inc(st_step, 1)
                            dve.wait_ge(st_step, at(b, (NT - 2) * NG, (c - 1) * NG + g + 1))
                            last = v.tensor_tensor(st[part, g, :, :], st[part, g, :, :], own, ALU.add)
                    last.then_inc(st_done, 1)
                y = yy[:, c % 2, :]
                src = filled(dve, "Y", f"yi{c}", b)
                dve.wait_ge(dx_done, at(b, NT, c + 1))
                v.tensor_tensor(y, src[:], y, ALU.add).then_inc(yi_done, 1)
                if c:
                    src = filled(dve, "Y", f"yx{c}", b)
                    s3 = src[:].rearrange("p (h d) -> p h d", h=NH)
                    v.tensor_tensor(s3, s3, decs[:, 0, c, :].unsqueeze(2).to_broadcast([P, NH, HD]),
                                    ALU.mult).then_inc(yb_done, 1)
                    dve.wait_ge(yb_done, at(b, NT - 1, c))
                    dve.wait_ge(yi_done, at(b, NT, c + 1))
                    v.tensor_tensor(y, src[:], y, ALU.add).then_inc(y_done, 1)
                    dve.wait_ge(y_done, at(b, NT - 1, c))
                dve.wait_ge(yi_done, at(b, NT, c + 1))
                dve.wait_ge(z_done, at(b, NT, c + 1))
                v.tensor_tensor(y, y, zs[:, c, :], ALU.mult).then_inc(yg_done, 1)

            def ssm_c(b, c):
                dve.wait_ge(ygh_done, at(b, NT, c + 1))
                tok_part = slice(c * P, (c + 1) * P)
                low(ygl[:, :, tok_part], bank[use("Y", f"ty{c}")][:].rearrange("p (k t) -> p k t", k=KI),
                    ygh[:, :, tok_part]).then_inc(ygl_done, 1)

            def fc1(b, a, e):
                for t in range(a, e):
                    dve.wait_ge(gl_done, at(b, KF, t + 1))
                    v.tensor_copy(glh[:, t, :], gl32[:, t % 2, :]).then_inc(glh_done, 1)

            def fc2(b):
                dve.wait_ge(x2b_done, at(b, 1, 1))
                for i in range(NT // 2):
                    src = filled(dve, "Y", f"m{i}", b)
                    x2p = x2[:, 2 * i:2 * i + 2, :].rearrange("p i d -> p (i d)")
                    v.scalar_tensor_tensor(out=x2p, in0=src[:], scalar=1 / WS, in1=x2p, op0=ALU.mult,
                                           op1=ALU.add).then_inc(m_done, 1)

            def y_out(b):
                f = F["Y"]
                dve.wait_ge(rms_done, at(b, 1, 1))
                dve.wait_ge(m_done, at(b, NT // 2, NT // 2))
                for i in range(NT):
                    src = filled(dve, "Y", f"o{i // 2}", b)
                    last = v.scalar_tensor_tensor(out=f["r"][:, i, :], in0=src[:, i % 2 * D:(i % 2 + 1) * D],
                                                  scalar=rms[:, i:i + 1], in1=x2[:, i, :], op0=ALU.mult, op1=ALU.add)
                    if i % 2:
                        last.then_inc(C["Y"]["r"], 1)
                norm_stats("Y", b, 0)
                dve.wait_ge(C["Y"]["rs"], at(b, 2, 1))
                normed("Y", f["xa"], f["rs"], C["Y"]["xa"])

            per_engine(dve, {
                ("X", "qkv"): qkv, ("X", "out"): attn_out, ("X", "tr"): split_tr("X", ["tr0", "tr1"]),
                ("X", "up"): up("X", "sup0"), ("X", "down"): down("X", "sdn0"), ("Y", "tr"): y_tr, ("Y", "proj"): proj,
                ("Y", "ssm_a"): ssm_a, ("Y", "ssm_b"): ssm_b, ("Y", "ssm_c"): ssm_c, ("Y", "fc1"): fc1,
                ("Y", "fc2"): fc2,                ("Y", "out"): y_out, ("Y", "tr3"): split_tr("Y", ["tq0", "tq1"]), ("Y", "up"): up("Y", "sup1"),
                ("Y", "down"): down("Y", "sdn1")})

        @block.gpsimd
        def _(pool):
            g = nc.gpsimd
            for tile, value in ((ident, 0.0), (upto, 1.0), (after, 1.0), (negid, 0.0), (past, 1.0)):
                g.memset(tile[:], value).then_inc(consts, 1)
            pool.wait_ge(consts, 11)
            g.affine_select(out=ident[:], in_=ident[:], pattern=[[-1, P]], compare_op=ALU.not_equal, fill=1.0, base=0,
                            channel_multiplier=1).then_inc(masks, 1)
            g.affine_select(out=upto[:], in_=upto[:], pattern=[[1, P]], compare_op=ALU.is_ge, fill=0.0, base=0,
                            channel_multiplier=-1).then_inc(masks, 1)
            g.affine_select(out=after[:], in_=after[:], pattern=[[-1, P]], compare_op=ALU.is_gt, fill=0.0, base=0,
                            channel_multiplier=1).then_inc(masks, 1)
            g.affine_select(out=negid[:], in_=negid[:], pattern=[[-1, P]], compare_op=ALU.not_equal, fill=MASKED,
                            base=0, channel_multiplier=1).then_inc(masks, 1)
            g.affine_select(out=past[:], in_=past[:], pattern=[[0, GH], [-1, P]], compare_op=ALU.is_gt, fill=0.0,
                            base=0, channel_multiplier=1).then_inc(masks, 1)
            pool.wait_ge(masks, 5)
            pool.wait_ge(rows_in, 16 * (len(COLS) + len(ROWS)))

            def inv_root(ch, b, turn):
                f, c = F[ch], C[ch]
                pool.wait_ge(c["mv"], at(b, 2, turn + 1))
                g.tensor_tensor(f["ve"][:], f["mv"][:, :, 1], eps[:], ALU.add).then_inc(c["ve"], 1)
                pool.wait_ge(c["ve"], at(b, 2, turn + 1))
                g.tensor_tensor(f["rs"][:], f["ve"][:], half[:], ALU.pow).then_inc(c["rs"], 1)

            def qkv(b):
                for m in range(KD):
                    pool.wait_ge(vhh_done, at(b, KD, m + 1))
                    g.tensor_tensor(vhl[:, m, :], vh32[:, m, :], vhh[:, m, :], ALU.subtract).then_inc(vhl_done, 1)

            def up(ch):
                def go(b, a, e):
                    f = F[ch]
                    for t in range(a, e):
                        if t % 2 == 0 and t < 2 * NPAIR:
                            continue
                        pair = t // 2
                        p0 = 0 if t < 2 * NPAIR else HALF
                        pool.wait_ge(C[ch]["hh"], at(b, NPAIR + 1, pair + 1))
                        if p0:
                            pool.wait_ge(C[ch]["hl"], at(b, NPAIR + 1, pair))
                        g.tensor_tensor(f["hl"][p0:P, pair, :], f["h32"][p0:P, pair % 2, :], f["hh"][p0:P, pair, :],
                                        ALU.subtract).then_inc(C[ch]["hl"], 1)
                        if p0:
                            pool.wait_ge(C[ch]["hl"], at(b, NPAIR + 1, pair + 1))
                return go

            def x_down(b):
                inv_root("X", b, 1)
                f = F["X"]
                pool.wait_ge(C["X"]["rs"], at(b, 2, 2))
                g.tensor_tensor(twice[:], f["rs"][:], f["rs"][:], ALU.add).then_inc(twice_done, 1)
                g.tensor_tensor(rx2[:], f["rs"][:], f["rs"][:], ALU.mult).then_inc(rx2_done, 1)
                pool.wait_ge(rx2_done, at(b, 1, 1))
                g.tensor_tensor(vx[:], f["mv"][:, :, 1], rx2[:], ALU.mult).then_inc(vx_done, 1)
                pool.wait_ge(vx_done, at(b, 1, 1))
                g.tensor_tensor(vx[:], vx[:], eps[:], ALU.add).then_inc(vxe_done, 1)
                pool.wait_ge(vxe_done, at(b, 1, 1))
                g.tensor_tensor(vy[:], vx[:], half[:], ALU.pow).then_inc(vy_done, 1)
                pool.wait_ge(vy_done, at(b, 1, 1))
                g.tensor_tensor(hsc[:], f["rs"][:], vy[:], ALU.mult).then_inc(hsc_done, 1)

            def y_tr(b):
                pool.wait_ge(x2_done, at(b, 1, 1))
                g.tensor_tensor(x2[:], x2[:], row["fc2b"][:].unsqueeze(1).to_broadcast([P, NT, D]), ALU.add).then_inc(
                    x2b_done, 1)

            def ssm_a(b, c):
                pool.wait_ge(a_done, at(b, 1, 1))
                if c:
                    filled(pool, "Y", f"seg{c - 1}_{NG - 1}", b)
                g.tensor_tensor(R, aexp[:, c, :].unsqueeze(2).to_broadcast([P, NH, P]),
                                upto[:].unsqueeze(1).to_broadcast([P, NH, P]), ALU.mult).then_inc(R_done, 1)

            def ssm_b(b, c):
                x3 = xbn[:, c, 0:DXB].rearrange("p (g o d) -> p g o d", g=NG, o=1).to_broadcast([P, NG, GH, HD])
                if c:
                    filled(pool, "Y", f"yi{c - 1}", b)
                    pool.wait_ge(xw_done, at(b, NT - 1, c))
                else:
                    pool.wait_ge(xbn_done, at(b, NT, NT))
                    pool.wait_ge(dt_done, at(b, 1, 1))
                g.tensor_tensor(xdt[:].rearrange("p (g j) d -> p g j d", g=NG), x3,
                                dt[:, c, :].rearrange("p (g j o) -> p g j o", g=NG, o=1).to_broadcast([P, NG, GH, HD]),
                                ALU.mult).then_inc(xdt_done, 1)
                if c >= 2:
                    filled(pool, "Y", f"ty{c - 2}", b)
                    pool.wait_ge(ss_done, at(b, NT, c - 1))
                g.tensor_tensor(yy[:, c % 2, :].rearrange("p (g j d) -> p g j d", g=NG, j=GH), x3,
                                row["dskip"][:].rearrange("p (g j o) -> p g j o", g=NG, o=1).to_broadcast(
                                    [P, NG, GH, HD]), ALU.mult).then_inc(dx_done, 1)
                if c < NT - 1:
                    if c:
                        filled(pool, "Y", f"ds{c - 1}", b)
                    pool.wait_ge(xdt_done, at(b, NT, c + 1))
                    pool.wait_ge(decs_done, at(b, 1, 1))
                    g.tensor_tensor(xw[:], xdt[:], decs[:, 2, c, :].unsqueeze(2).to_broadcast([P, NH, HD]),
                                    ALU.mult).then_inc(xw_done, 1)

            def ssm_c(b, c):
                if c < NT - 1:
                    return
                pool.wait_ge(ss_done, at(b, NT, NT))
                g.tensor_tensor(rms[:], ss[:], ws2_di[:], ALU.mult).then_inc(rms_step, 1)
                pool.wait_ge(rms_step, at(b, 2, 1))
                g.tensor_tensor(rms[:], rms[:], ws2_eps[:], ALU.add).then_inc(rms_step, 1)
                pool.wait_ge(rms_step, at(b, 2, 2))
                g.tensor_tensor(rms[:], rms[:], half[:], ALU.pow).then_inc(rms_done, 1)

            def fc1(b, a, e):
                for t in range(a, e):
                    pool.wait_ge(glh_done, at(b, KF, t + 1))
                    g.tensor_tensor(gll[:, t, :], gl32[:, t % 2, :], glh[:, t, :], ALU.subtract).then_inc(gll_done, 1)

            per_engine(pool, {
                ("X", "qkv"): qkv, ("X", "out"): lambda b: inv_root("X", b, 0), ("X", "up"): up("X"),
                ("X", "down"): x_down, ("Y", "tr"): y_tr, ("Y", "ssm_a"): ssm_a, ("Y", "ssm_b"): ssm_b,
                ("Y", "ssm_c"): ssm_c, ("Y", "fc1"): fc1, ("Y", "out"): lambda b: inv_root("Y", b, 0),
                ("Y", "up"): up("Y"), ("Y", "down"): lambda b: inv_root("Y", b, 1)})


def ktiles(w):
    k, c = w.shape
    if k % P:
        w = np.concatenate([w[:k // P * P], np.zeros((P - k % P, c), w.dtype), w[k // P * P:]])
    return np.ascontiguousarray(w.reshape(-1, P, c).transpose(1, 0, 2)).reshape(P, -1)


def up_order(gate, up):
    parts = []
    for t in range(NPAIR):
        parts += [gate[t * P:(t + 1) * P], up[t * P:(t + 1) * P]]
    return np.concatenate(parts + [gate[NPAIR * P:], up[NPAIR * P:]])


def columns(v):
    return np.ascontiguousarray(v.reshape(-1, P).T)


def kernel(**inputs):
    import concourse.bacc as bacc
    from concourse.bass_utils import run_bass_kernel_spmd

    a = {n: np.asarray(x) for n, x in inputs.items()}
    win = a["L1_attn_W_in"]
    z, x, bp, cp, dt_ = np.split(win, [DI, DI + DXB, DI + 2 * DXB, 2 * DI + 2 * DXB], axis=1)
    cp = cp.reshape(D, NG, GH, HD).transpose(0, 2, 1, 3).reshape(D, DI)
    arrays = {
        "x": a["L0_attn_x"], "xt": np.ascontiguousarray(a["L0_attn_x"].transpose(0, 2, 1)),
        "wqkv": ktiles(np.concatenate([a["L0_attn_Wq"].T, a["L0_attn_Wk"].T, a["L0_attn_Wv"].T], axis=1)),
        "wo": ktiles(a["L0_attn_Wo"].T),
        "up0": ktiles(up_order(a["L0_ffn_wq_gate"], a["L0_ffn_wq_up"]).T), "dn0": ktiles(a["L0_ffn_wq_down"].T),
        "win": ktiles(np.concatenate([z, x, bp, dt_, cp], axis=1)), "fc1": ktiles(a["L1_attn_fc1_w"]),
        "wout": ktiles(a["L1_attn_W_out"]), "fc2": ktiles(a["L1_attn_fc2_w"]),
        "up1": ktiles(up_order(a["L1_ffn_gate_w"], a["L1_ffn_up_w"]).T), "dn1": ktiles(a["L1_ffn_down_w"].T),
        "lnw": columns(a["L1_attn_ln_w"]), "lnb": columns(a["L1_attn_ln_b"]), "fc1b": columns(a["L1_attn_fc1_b"]),
        "normw": columns(a["L1_attn_norm_w"]),
        "sup0": columns(up_order(a["L0_ffn_s_gate"], a["L0_ffn_s_up"])),
        "sup1": columns(up_order(a["L1_ffn_gate_s"], a["L1_ffn_up_s"])),
        "dtb": a["L1_attn_dt_bias"], "alog": a["L1_attn_A_log"], "dskip": a["L1_attn_D"],
        "sdn0": a["L0_ffn_s_down"], "sdn1": a["L1_ffn_down_s"], "fc2b": a["L1_attn_fc2_b"]}
    nc = bacc.Bacc("TRN2", target_bir_lowering=False, num_devices=1, dynamic_dma_scratch_size=1024)
    ins = {n: nc.dram_tensor(f"in_{n}", v.shape, mybir.dt.from_np(v.dtype), kind="ExternalInput").ap()
           for n, v in arrays.items()}
    out = nc.dram_tensor("out", (NB, S, D), F32, kind="ExternalOutput").ap()
    build(nc, ins, out)
    r = run_bass_kernel_spmd(nc, [{f"in_{n}": np.ascontiguousarray(v) for n, v in arrays.items()}], core_ids=[0])
    return r.results[0]["out"]
```

```python
from contextlib import ExitStack

import numpy as np

import concourse.bass as bass
from concourse import mybir

ALU = mybir.AluOpType
ACT = mybir.ActivationFunctionType
F32 = mybir.dt.float32
F16 = mybir.dt.float16
I32 = mybir.dt.int32

P = 128
NB, S, D = 8, 512, 256
KD = D // P
NT = S // P
HID = 704
NPAIR = HID // P
NMIX = NPAIR
NUP = 2 * NPAIR + 1
HALF = P // 2
DI, DXB, NH, HD = 512, 128, 8, 64
NG = 2
GH = NH // NG
INTER = 1024
KI = DI // P
KF = INTER // P
CZ, CX, CDT, CC = 0, DI, DI + 2 * DXB, DI + 2 * DXB + NH
NSMALL = 2 * DXB + NH
WIN = CC + DI
EPS = 1e-5
WS = 64.0
ZERO_POINT = 128.0
DECAY_FLOOR = -110.0
MASKED = -30000.0
SSM_DENOM = float(D) ** 0.5 / S


def at(b, per, k):
    return b * per + k


def plan(names, first):
    count, uses = [0] * 4, {}
    for i, name in enumerate(names):
        uses[name] = (first + i % 4, count[i % 4])
        count[i % 4] += 1
    return uses, {first + j: count[j] for j in range(4)}


X_USES = ([f"{w}{m}" for m in range(KD) for w in "kvq"] + [f"o{i}" for i in range(NT // 2)]
          + [f"tr{m}" for m in range(KD)] + [f"up{t}" for t in range(NUP)] + [f"dn{i}" for i in range(NT // 2)]
          + [f"hs{m}" for m in range(KD)])
SCHED = [("X", "split"), ("Z", "down"), ("Y", "gate"), ("Y", "proj"), ("X", "qkv"), ("Y", "decays"), ("Y", "seg", 0),
         ("Y", "seg", 1), ("X", "out"), ("Y", "seg", 2), ("Y", "seg", 3), ("Y", "fc1"), ("X", "tr"), ("Y", "fc2"),
         ("Y", "pairs", 0), ("Y", "pairs", 1), ("X", "up", 0, 3), ("Y", "chunk", 0), ("X", "up", 3, 4),
         ("Y", "pairs", 2), ("X", "up", 4, 5), ("Y", "turned", 0), ("Y", "chunk", 1), ("X", "up", 5, 6),
         ("Y", "pairs", 3), ("X", "up", 6, 7), ("Y", "turned", 1), ("Y", "chunk", 2), ("X", "up", 7, 9),
         ("Y", "turned", 2), ("Y", "chunk", 3), ("X", "up", 9, 11), ("Y", "turned", 3), ("Y", "out"), ("X", "down"),
         ("Y", "tr"), ("Y", "up", 0, 2), ("X", "sum", 0), ("Y", "up", 2, 4), ("X", "sum", 1), ("Y", "up", 4, 6),
         ("X", "hat"), ("Y", "up", 6, 11), ("X", "tr2"), ("X", "x2")]
WEIGHT_TURN = {("Y", "proj"): ["up0"], ("Y", "seg", 0): ["dn0"], ("Y", "fc1"): ["win"], ("Y", "pairs", 1): ["fc1"],
               ("Y", "pairs", 2): ["wout"], ("Y", "pairs", 3): ["fc2"], ("Y", "out"): ["up1"], ("Y", "up", 0, 2): ["dn1"]}
Y_PARTS = {"down": lambda: [f"dn{i}" for i in range(NT // 2)],
           "proj": lambda: [f"sm{i}" for i in range(NT)] + ["bt"] + [f"ct{j}" for j in range(GH)],
           "gate": lambda: [f"z{i}" for i in range(NT)], "decays": lambda: ["cum"],
           "seg": lambda c: [f"seg{c}_{g}" for g in range(NG)], "pairs": lambda c: [f"g{c}_{g}" for g in range(NG)],
           "chunk": lambda c: [f"yi{c}"] + ([f"yx{c}"] if c else []) + ([f"ds{c}"] if c < NT - 1 else []),
           "turned": lambda c: [f"ty{c}"], "fc1": lambda: [f"f{t}" for t in range(KF)],
           "fc2": lambda: [f"m{i}" for i in range(NT // 2)], "out": lambda: [f"o{i}" for i in range(NT // 2)],
           "tr": lambda: [f"tq{m}" for m in range(KD)], "up": lambda a, e: [f"up{t}" for t in range(a, e)]}
Y_USES = []
for ch, kind, *arg in [s for s in SCHED if s[0] == "Y"] + [s for s in SCHED if s[0] == "Z"]:
    Y_USES += Y_PARTS[kind](*arg)
XU, XN = plan(X_USES, 0)
YU, YN = plan(Y_USES, 4)
USES = {"X": (XU, XN), "Y": (YU, YN)}

WEIGHTS = [
    ("wqkv", KD, 3 * D, False, WS), ("wo", KD, D, False, WS), ("up0", KD, NUP * P, True, 1.0),
    ("dn0", NPAIR + 1, D, True, 1.0), ("win", KD, WIN, False, WS), ("fc1", KD, INTER, False, WS),
    ("wout", KI, D, False, WS), ("fc2", KF, D, False, WS), ("up1", KD, NUP * P, False, 1.0),
    ("dn1", NPAIR + 1, D, False, 1.0)]
WIDX = {w[0]: i for i, w in enumerate(WEIGHTS)}
WIDE = ("up0", "win", "up1")
STAGE = max(k * c for n, k, c, _, _ in WEIGHTS if n in WIDE)


def same_stage_before(i):
    users = [j for j in range(i) if (WEIGHTS[j][0] in WIDE) == (WEIGHTS[i][0] in WIDE)]
    return users[-1] + 1 if users else 0


COLS = {"lnw": KD, "lnb": KD, "fc1b": KF, "normw": KI, "sup0": NUP, "sup1": NUP}
ROWS = {"dtb": NH, "alog": NH, "dskip": NH, "sdn0": D, "sdn1": D, "fc2b": D}


def build(nc, ins, out):
    with ExitStack() as ctx:
        def sb(name, shape, dt=F32):
            return ctx.enter_context(nc.sbuf_tensor(name, shape, dt))

        def sem(name):
            return ctx.enter_context(nc.semaphore(name))

        bank = [ctx.enter_context(nc.psum_tensor(f"bank{i}", [P, 512], F32)) for i in range(8)]
        full = [sem(f"full{i}") for i in range(8)]

        hi = {n: sb(f"{n}_hi", [P, k, c], F16) for n, k, c, _, _ in WEIGHTS}
        lo = {n: sb(f"{n}_lo", [P, k, c], F16) for n, k, c, _, _ in WEIGHTS}
        decay = sb("decay", [P, (NT + 1) * NH * P])

        def stage(n, k, c):
            return decay[:, 0:k * c] if n in WIDE else decay[:, STAGE:STAGE + k * c]

        col = {n: sb(f"c_{n}", [P, c]) for n, c in COLS.items()}
        row = {n: sb(f"r_{n}", [P, c]) for n, c in ROWS.items()}
        ident = sb("ident", [P, P])
        allone = sb("allone", [P, P])
        upto = sb("upto", [P, P])
        after = sb("after", [P, P])
        upto16, after16 = sb("upto16", [P, P], F16), sb("after16", [P, P], F16)
        negid = sb("negid", [P, P], F16)
        past = sb("past", [P, GH, P], F16)
        spare = sb("spare", [P, 1])
        half = sb("half", [P, NT])
        eps, ws2_di, ws2_eps = sb("eps", [P, NT]), sb("ws2_di", [P, NT]), sb("ws2_eps", [P, NT])
        zero_point = sb("zero_point", [P, 1])
        normws = sb("normws", [P, KI])
        aneg = sb("aneg", [P, NH])

        xt = sb("xt", [P, KD, S])
        xn = sb("xn", [P, NT, D])
        xh, xl = sb("xh", [P, KD, S], F16), sb("xl", [P, KD, S], F16)
        ksb = sb("ksb", [P, KD, S])
        kv = sb("kv", [P, S])
        vh32 = ksb
        vhh, vhl = sb("vhh", [P, KD, S], F16), sb("vhl", [P, KD, S], F16)
        x2 = sb("x2", [P, NT, D])
        hsh, hsl = sb("hsh", [P, KD, S], F16), sb("hsl", [P, KD, S], F16)
        bT = sb("bT", [P, S])
        cT = sb("cT", [P, GH, S])
        hs32 = cT[:, 0:KD, :]
        xbn = sb("xbn", [P, NT, 2 * DXB])
        zs = sb("zs", [P, NT, DI])
        dtz = sb("dtz", [P, NT * NH])
        dta, dte, dtu, dtl, dtd, dtq = (sb(n, [P, NT * NH]) for n in ("dta", "dte", "dtu", "dtl", "dtd", "dtq"))
        dt = sb("dt", [P, NT, NH])
        aexp = sb("aexp", [P, NT, NH])
        decs = sb("decs", [P, 3, NT, NH])
        E = decay[:, 0:NT * NH * P].rearrange("p (c h t) -> p c h t", c=NT, h=NH)
        Rh, Rl = ([decay[:, (2 * k + i) * NH * P // 2:(2 * k + i + 1) * NH * P // 2].bitcast(F16).rearrange(
            "p (h t) -> p h t", h=NH) for k in (NT - 1, NT)] for i in range(2))
        ah, al = sb("ah", [P, NT, NH], F16), sb("al", [P, NT, NH], F16)
        xdt = sb("xdt", [P, 2, NH, HD])
        xw = sb("xw", [P, NH, HD])
        st = sb("st", [P, NG, GH, HD])
        yy = sb("yy", [P, 2, DI])
        sq = sb("sq", [P, DI], F16)
        ss = sb("ss", [P, NT])
        rmsv, rms = sb("rmsv", [P, NT]), sb("rms", [P, NT])
        ygh, ygl = sb("ygh", [P, KI, S], F16), sb("ygl", [P, KI, S], F16)
        wide_h, wide_l = sb("wide_h", [P, KF, S], F16), sb("wide_l", [P, KF, S], F16)
        glh, gll = wide_h, wide_l
        F = {}
        for ch in "XY":
            F[ch] = dict(
                r=sb(f"r{ch}", [P, NT, D]), xa=sb(f"xa{ch}", [P, NT, D]),
                stats=sb(f"stats{ch}", [P, NT, 6]), mv=sb(f"mv{ch}", [P, NT, 2]),
                ve=sb(f"ve{ch}", [P, NT]), rs=sb(f"rs{ch}", [P, NT]),
                th=xh if ch == "X" else hsh, tl=xl if ch == "X" else hsl,
                sg=sb(f"sg{ch}", [P, S]), h32=sb(f"h32{ch}", [P, 2, S]), hh=wide_h, hl=wide_l)
        gl32 = F["Y"]["h32"]
        vx, rx2, vy, hsc, twice = (sb(n, [P, NT]) for n in ("vx", "rx2", "vy", "hsc", "twice"))
        hat = F["X"]["xa"]
        yout = sb("yout", [P, NT, D])

        w_in = [sem("w_in_wide"), sem("w_in_narrow")]
        rows_in = sem("rows_in")
        w_hi, w_lo = sem("w_hi"), sem("w_lo")
        consts, masks, aneg_done, normws_done, zp_done = (
            sem(n) for n in ("consts", "masks", "aneg_done", "normws_done", "zp_done"))
        xt_in, xn_in, stored = sem("xt_in"), sem("xn_in"), sem("stored")
        xh_done, xl_done, k_done, kv_done, cum_done, vh_done, vhh_done, vhl_done = (
            sem(n) for n in ("xh_done", "xl_done", "k_done", "kv_done", "cum_done", "vh_done", "vhh_done", "vhl_done"))
        C = {ch: {n: sem(f"{n}_{ch}") for n in (
            "part", "r", "stats", "mv", "ve", "rs", "xa", "th", "tl", "sg", "h", "hh", "hl")} for ch in "XY"}
        (rx2_done, vx_done, vxe_done, vy_done, hsc_done, twice_done, hat_done, x2_done, x2b_done, hs_done, hsh_done,
         hsl_done, bT_done, cT_done, xbn_done, dtz_done, z_done, absz_done, e_done, u_done, l_done, dt_step, dt_done,
         dta_done, a_done, ah_done, al_done, decs_done, Rh_done, Rl_done, E_done, W_done, xdt_done, xw_done, st_step, st_done, dx_done, yi_done,
         yb_done, y_done, yg_done, ss_done, rms_step, rms_done, ygh_done, ygl_done, gl_done, glh_done, gll_done,
         m_done, yhalf_done, yout_done) = (sem(n) for n in (
             "rx2_done vx_done vxe_done vy_done hsc_done twice_done hat_done x2_done x2b_done hs_done hsh_done "
             "hsl_done bT_done cT_done xbn_done dtz_done z_done absz_done e_done u_done l_done dt_step dt_done "
             "dta_done a_done ah_done al_done decs_done Rh_done Rl_done E_done W_done xdt_done xw_done st_step st_done dx_done yi_done "
             "yb_done y_done yg_done ss_done rms_step rms_done ygh_done ygl_done gl_done glh_done gll_done "
             "m_done yhalf_done yout_done").split())

        RN = {"X": NT, "Y": NT}

        release = {"X": {}, "Y": {}}
        for m in range(KD):
            release["X"].update({f"k{m}": (k_done, KD, m + 1), f"v{m}": (kv_done, KD, m + 1),
                                 f"q{m}": (vh_done, KD, m + 1), f"tr{m}": (C["X"]["tl"], KD, m + 1),
                                 f"hs{m}": (hs_done, KD, m + 1)})
            release["Y"][f"tq{m}"] = (C["Y"]["tl"], KD, m + 1)
        for ch in "XY":
            for t in range(2 * NPAIR):
                release[ch][f"up{t}"] = (C[ch]["h" if t % 2 else "sg"], NPAIR + 1, t // 2 + 1)
            release[ch][f"up{2 * NPAIR}"] = (C[ch]["h"], NPAIR + 1, NPAIR + 1)
            for i in range(NT // 2):
                release[ch][f"dn{i}"] = (C[ch]["part"], NT // 2, i + 1)
                release[ch][f"o{i}"] = (C[ch]["r"], RN[ch], i + 1)
        release["Y"].update(bt=(bT_done, 1, 1), cum=(decs_done, 1, 1))
        for j in range(GH):
            release["Y"][f"ct{j}"] = (cT_done, GH, j + 1)
        for i in range(NT // 2):
            release["Y"][f"m{i}"] = (m_done, NT // 2, i + 1)
        for t in range(KF):
            release["Y"][f"f{t}"] = (gl_done, KF, t + 1)
        for c in range(NT):
            release["Y"].update({f"sm{c}": (dtz_done, NT, c + 1), f"z{c}": (z_done, NT, c + 1),
                                 f"ds{c}": (st_done, NT - 1, c + 1), f"yi{c}": (yi_done, NT, c + 1),
                                 f"yx{c}": (y_done, NT - 1, c), f"ty{c}": (ygl_done, NT, c + 1)})
            for g in range(NG):
                release["Y"][f"seg{c}_{g}"] = (E_done, NT * NG, c * NG + g + 1)
                release["Y"][f"g{c}_{g}"] = (W_done, NT * NG, c * NG + g + 1)

        def wait_before(eng, signal, b, per, k):
            if not isinstance(b, int) or b:
                eng.wait_ge(signal, at(b, per, k - per))

        def filled(eng, ch, name, b):
            k, n = USES[ch][0][name]
            eng.wait_ge(full[k], at(b, USES[ch][1][k], n + 1))
            return bank[k]

        def use(ch, name):
            return USES[ch][0][name][0]

        def per_engine(eng, phases):
            def turn(bx, by, bz):
                for step in SCHED:
                    ch, kind, *arg = step
                    b = {"X": bx, "Y": by, "Z": bz}[ch]
                    if b is not None and (ch, kind) in phases:
                        phases[ch, kind](b, *arg)
                    if isinstance(bx, int) and bx == 0 and "weight" in phases:
                        for name in WEIGHT_TURN.get(step, []):
                            phases["weight"](name)
            turn(0, None, None)
            turn(1, 0, None)
            with eng.Fori(2, NB) as i:
                turn(i, i - 1, i - 2)
            turn(None, NB - 1, NB - 2)
            turn(None, None, NB - 1)

        block = ctx.enter_context(nc.Block())

        @block.sync
        def _(sp):
            def load_x(b):
                wait_before(sp, xl_done, b, 1, 1)
                sp.dma_start(xt[:], ins["xt"][bass.ds(b, 1)].rearrange("o (k p) s -> (o p) k s", p=P)).then_inc(xt_in, 16)
                wait_before(sp, C["X"]["r"], b, RN["X"], NT // 2)
                sp.dma_start(xn[:], ins["x"][bass.ds(b, 1)].rearrange("o (i p) d -> (o p) i d", p=P)).then_inc(xn_in, 16)

            def store(b):
                sp.wait_ge(yout_done, b + 1)
                sp.dma_start(out[bass.ds(b, 1)].rearrange("o (i p) d -> (o p) i d", p=P), yout[:]).then_inc(stored, 16)

            load_x(0)
            for i, (n, k, c, integer, _) in enumerate(WEIGHTS):
                if same_stage_before(i):
                    sp.wait_ge(w_lo, same_stage_before(i))
                dst = stage(n, k, c)
                sp.dma_start(dst.bitcast(I32) if integer else dst, ins[n]).then_inc(w_in[n not in WIDE], 16)
                if n == "up0":
                    for m in COLS:
                        sp.dma_start(col[m][:], ins[m]).then_inc(rows_in, 16)
                    for m in ROWS:
                        sp.dma_start(row[m][:], ins[m].partition_broadcast(P)).then_inc(rows_in, 16)
                if n == "win":
                    load_x(1)
            load_x(2)
            with sp.Fori(3, NB) as b:
                load_x(b)
                store(b - 3)
            for b in range(NB - 3, NB):
                store(b)
            sp.wait_ge(stored, 16 * NB + 1)

        @block.tensor
        def _(pe):
            def fill(ch, name, b):
                k, n = USES[ch][0][name]
                before = [u for u in USES[ch][0] if USES[ch][0][u] == (k, (n - 1) % USES[ch][1][k])][0]
                signal, per, which = release[ch][before]
                if n:
                    pe.wait_ge(signal, at(b, per, which))
                else:
                    wait_before(pe, signal, b, per, which)
                return bank[k]

            def three(dst, lh, ll, rh, rl, first=True, last=True, shared=False):
                nc.tensor.matmul(dst, lh, rh, start=first, stop=False, skip_group_check=shared)
                nc.tensor.matmul(dst, lh, rl, start=False, stop=False, skip_group_check=shared)
                return nc.tensor.matmul(dst, ll, rh, start=False, stop=last, skip_group_check=shared)

            def product(dst, lh, ll, rh, rl, tiles, ready=None):
                for n, k in enumerate(tiles):
                    if ready:
                        ready(k)
                    last = three(dst, lh(k), ll(k), rh(k), rl(k), n == 0, n == len(tiles) - 1)
                return last

            def chan_tile(dst, w, c0, act_h, act_l, m=P, ready=None):
                return product(dst, lambda k: hi[w][:, k, c0:c0 + m], lambda k: lo[w][:, k, c0:c0 + m],
                               lambda k: act_h[:, k, :], lambda k: act_l[:, k, :], range(KD), ready)

            def tok_tile(dst, i, act_h, act_l, w, c0, n, tiles):
                return product(dst, lambda k: act_h[:, k, i * P:(i + 1) * P], lambda k: act_l[:, k, i * P:(i + 1) * P],
                               lambda k: hi[w][:, k, c0:c0 + n], lambda k: lo[w][:, k, c0:c0 + n], tiles)

            def transposes(ch, b, names, src):
                for m in range(KD):
                    dst = fill(ch, names[m], b)
                    for i in range(NT):
                        last = nc.tensor.transpose(dst[:, i * P:(i + 1) * P], src[:, i, m * P:(m + 1) * P], ident[:])
                    last.then_inc(full[use(ch, names[m])], 1)

            def qkv(b):
                pe.wait_ge(xl_done, at(b, 1, 1))
                for m in range(KD):
                    for w, c0 in (("k", D), ("v", 2 * D), ("q", 0)):
                        dst = fill("X", f"{w}{m}", b)
                        chan_tile(dst[:], "wqkv", c0 + m * P, xh, xl).then_inc(full[use("X", f"{w}{m}")], 1)

            def rows_of_two(dst, pair, a_h, a_l, w, tiles, ready):
                for k in range(tiles):
                    ready(k)
                    p0 = HALF if w in ("dn0", "dn1") and k == NPAIR else 0
                    for j in range(2):
                        tok_part = slice((2 * pair + j) * P, (2 * pair + j + 1) * P)
                        last = three(dst[:, j * D:(j + 1) * D], a_h[p0:P, k, tok_part], a_l[p0:P, k, tok_part],
                                     hi[w][p0:P, k, :], lo[w][p0:P, k, :], k == 0 and j == 0, k == tiles - 1, True)
                return last

            def attn_out(b):
                if isinstance(b, int) and b == 0:
                    pe.wait_ge(w_lo, WIDX["wo"] + 1)
                for i in range(NT // 2):
                    dst = fill("X", f"o{i}", b)
                    rows_of_two(dst, i, vhh, vhl, "wo", KD, lambda k: pe.wait_ge(vhl_done, at(b, KD, k + 1))
                                ).then_inc(full[use("X", f"o{i}")], 1)

            def x_tr(b):
                pe.wait_ge(C["X"]["xa"], at(b, 1, 1))
                transposes("X", b, ["tr0", "tr1"], F["X"]["xa"])

            def up(ch, w):
                def go(b, a, e):
                    if isinstance(b, int) and b == 0:
                        pe.wait_ge(w_lo, WIDX[w] + 1)
                    for t in range(a, e):
                        dst = fill(ch, f"up{t}", b)
                        chan_tile(dst[:], w, t * P, F[ch]["th"], F[ch]["tl"],
                                  ready=(lambda k: pe.wait_ge(C[ch]["tl"], at(b, KD, k + 1))) if t == 0 else None
                                  ).then_inc(full[use(ch, f"up{t}")], 1)
                return go

            def down(ch, w, b, i):
                if isinstance(b, int) and b == 0:
                    pe.wait_ge(w_lo, WIDX[w] + 1)
                dst = fill(ch, f"dn{i}", b)
                rows_of_two(dst, i, F[ch]["hh"], F[ch]["hl"], w, NPAIR + 1,
                            lambda k: pe.wait_ge(C[ch]["hl"], at(b, NPAIR + 1, k + 1))).then_inc(
                    full[use(ch, f"dn{i}")], 1)

            def x_down(b):
                for i in range(NT // 2):
                    down("X", "dn0", b, i)

            def z_down(b):
                for i in range(NT // 2):
                    down("Y", "dn1", b, i)

            def x_tr2(b):
                pe.wait_ge(hat_done, at(b, 1, 1))
                transposes("X", b, ["hs0", "hs1"], hat)

            def proj(b):
                for i in range(NT):
                    dst = fill("Y", f"sm{i}", b)
                    tok_tile(dst[:, 0:NSMALL], i, hsh, hsl, "win", CX, NSMALL, range(KD)).then_inc(
                        full[use("Y", f"sm{i}")], 1)
                dst = fill("Y", "bt", b)
                chan_tile(dst[:], "win", CX + DXB, hsh, hsl).then_inc(full[use("Y", "bt")], 1)
                for j in range(GH):
                    dst = fill("Y", f"ct{j}", b)
                    chan_tile(dst[:], "win", CC + j * P, hsh, hsl).then_inc(full[use("Y", f"ct{j}")], 1)

            def decays(b):
                dst = fill("Y", "cum", b)
                pe.wait_ge(a_done, at(b, 1, 1))
                av = aexp[:].rearrange("p c h -> p (c h)")
                nc.tensor.matmul(dst[:, 0:NT * NH], upto[:], av, start=True, stop=True)
                nc.tensor.matmul(dst[:, NT * NH:2 * NT * NH], allone[:], av, start=True, stop=True)
                nc.tensor.matmul(dst[:, 2 * NT * NH:3 * NT * NH], after[:], av, start=True, stop=True).then_inc(
                    full[use("Y", "cum")], 1)

            def gate(b):
                if isinstance(b, int) and b == 0:
                    pe.wait_ge(w_lo, len(WEIGHTS))
                pe.wait_ge(hsl_done, at(b, KD, KD))
                for i in range(NT):
                    dst = fill("Y", f"z{i}", b)
                    tok_tile(dst[:], i, hsh, hsl, "win", CZ, DI, range(KD)).then_inc(full[use("Y", f"z{i}")], 1)

            def seg(b, c):
                for g in range(NG):
                    dst = fill("Y", f"seg{c}_{g}", b)
                    group = slice(g * GH, (g + 1) * GH)
                    pe.wait_ge(Rh_done, at(b, NT * NG, c * NG + g + 1))
                    nc.tensor.matmul(dst[:], after16[:], Rh[c % 2][:, group, :], start=True, stop=False)
                    pe.wait_ge(Rl_done, at(b, NT * NG, c * NG + g + 1))
                    nc.tensor.matmul(dst[:], after16[:], Rl[c % 2][:, group, :], start=False, stop=False)
                    nc.tensor.matmul(dst[:], negid[:], past[:], start=False, stop=True).then_inc(
                        full[use("Y", f"seg{c}_{g}")], 1)

            def pairs(b, c):
                tok_part = slice(c * P, (c + 1) * P)
                for g in range(NG):
                    dst = fill("Y", f"g{c}_{g}", b)
                    if g == 0:
                        pe.wait_ge(cT_done, at(b, GH, GH))
                        pe.wait_ge(bT_done, at(b, 1, 1))
                    part = slice(g * HD, (g + 1) * HD)
                    nc.tensor.matmul(dst[:], bT[part, tok_part], cT[part, :, tok_part], start=True, stop=True).then_inc(
                        full[use("Y", f"g{c}_{g}")], 1)

            def chunk(b, c):
                tok_part = slice(c * P, (c + 1) * P)
                dst = fill("Y", f"yi{c}", b)
                pe.wait_ge(xdt_done, at(b, NT, c + 1))
                pe.wait_ge(W_done, at(b, NT * NG, (c + 1) * NG))
                for h in range(NH):
                    last = nc.tensor.matmul(dst[:, h * HD:(h + 1) * HD], E[:, c, h, :], xdt[:, c % 2, h, :],
                                            start=True, stop=True)
                last.then_inc(full[use("Y", f"yi{c}")], 1)
                if c:
                    dst = fill("Y", f"yx{c}", b)
                    pe.wait_ge(st_done, at(b, NT - 1, c))
                    d4 = dst[:].rearrange("p (g j d) -> p g j d", g=NG, j=GH)
                    for j in range(GH):
                        last = nc.tensor.matmul(d4[:, :, j, :], cT[:, j, tok_part], st[:, :, j, :],
                                                start=True, stop=True)
                    last.then_inc(full[use("Y", f"yx{c}")], 1)
                if c < NT - 1:
                    dst = fill("Y", f"ds{c}", b)
                    pe.wait_ge(xw_done, at(b, NT - 1, c + 1))
                    pe.wait_ge(xbn_done, at(b, NT, c + 1))
                    nc.tensor.matmul(dst[:], xbn[:, c, DXB:2 * DXB], xw[:].rearrange("p h d -> p (h d)"),
                                     start=True, stop=True).then_inc(full[use("Y", f"ds{c}")], 1)

            def turned(b, c):
                dst = fill("Y", f"ty{c}", b)
                pe.wait_ge(yg_done, at(b, NT, c + 1))
                for k in range(KI):
                    last = nc.tensor.transpose(dst[:, k * P:(k + 1) * P], yy[:, c % 2, k * P:(k + 1) * P], ident[:])
                last.then_inc(full[use("Y", f"ty{c}")], 1)

            def fc1(b):
                for t in range(KF):
                    dst = fill("Y", f"f{t}", b)
                    chan_tile(dst[:], "fc1", t * P, hsh, hsl).then_inc(full[use("Y", f"f{t}")], 1)

            def fc2(b):
                for i in range(NT // 2):
                    dst = fill("Y", f"m{i}", b)
                    rows_of_two(dst, i, glh, gll, "fc2", KF, lambda k: pe.wait_ge(gll_done, at(b, KF, k + 1))
                                ).then_inc(full[use("Y", f"m{i}")], 1)

            def y_out(b):
                for i in range(NT):
                    dst = fill("Y", f"o{i // 2}", b) if i % 2 == 0 else dst
                    pe.wait_ge(ygl_done, at(b, NT, i + 1))
                    last = tok_tile(dst[:, i % 2 * D:(i % 2 + 1) * D], i, ygh, ygl, "wout", 0, D, range(KI))
                    if i % 2:
                        last.then_inc(full[use("Y", f"o{i // 2}")], 1)

            def y_tr(b):
                pe.wait_ge(C["Y"]["xa"], at(b, 1, 1))
                transposes("Y", b, ["tq0", "tq1"], F["Y"]["xa"])

            pe.wait_ge(masks, 7)
            pe.wait_ge(w_lo, WIDX["wqkv"] + 1)
            per_engine(pe, {
                ("X", "qkv"): qkv, ("X", "out"): attn_out, ("X", "tr"): x_tr, ("X", "up"): up("X", "up0"),
                ("X", "down"): x_down, ("X", "tr2"): x_tr2, ("Y", "proj"): proj, ("Y", "gate"): gate,
                ("Y", "decays"): decays, ("Y", "seg"): seg, ("Y", "pairs"): pairs, ("Y", "chunk"): chunk,
                ("Y", "turned"): turned, ("Y", "fc1"): fc1, ("Y", "fc2"): fc2, ("Y", "out"): y_out,
                ("Y", "tr"): y_tr, ("Y", "up"): up("Y", "up1"), ("Z", "down"): z_down})

        @block.scalar
        def _(act):
            def weight(name):
                i = WIDX[name]
                n, k, c, integer, scale = WEIGHTS[i]
                act.wait_ge(w_in[n not in WIDE], 16 * sum((w[0] in WIDE) == (n in WIDE) for w in WEIGHTS[:i + 1]))
                src, dst = stage(n, k, c), hi[n][:].rearrange("p k c -> p (k c)")
                if n == "wout":
                    act.wait_ge(normws_done, 1)
                    for kk in range(KI):
                        last = nc.scalar.activation(hi[n][:, kk, :], src[:, kk * c:(kk + 1) * c], ACT.Copy,
                                                    scale=normws[:, kk:kk + 1])
                elif integer:
                    act.wait_ge(zp_done, 1)
                    last = nc.scalar.activation(dst, src.bitcast(I32), ACT.Identity, bias=zero_point[:], scale=scale)
                else:
                    last = nc.scalar.activation(dst, src, ACT.Copy, scale=scale)
                last.then_inc(w_hi, 1)

            def split(b):
                act.wait_ge(xt_in, at(b, 16, 16))
                nc.scalar.copy(xh[:], xt[:]).then_inc(xh_done, 1)

            def qkv(b):
                for m in range(KD):
                    src = filled(act, "X", f"k{m}", b)
                    nc.scalar.activation(ksb[:, m, :], src[:], ACT.Copy, scale=WS ** -2).then_inc(k_done, 1)
                for m in range(KD):
                    act.wait_ge(vh_done, at(b, KD, m + 1))
                    nc.scalar.copy(vhh[:, m, :], vh32[:, m, :]).then_inc(vhh_done, 1)

            def split_tr(ch, names):
                def go(b):
                    for m in range(KD):
                        src = filled(act, ch, names[m], b)
                        nc.scalar.copy(F[ch]["th"][:, m, :], src[:]).then_inc(C[ch]["th"], 1)
                return go

            def up(ch, scales):
                def go(b, a, e):
                    f = F[ch]
                    for t in range(a, e):
                        p0, p1 = (0, P) if t < 2 * NPAIR else (HALF, P)
                        pair = t // 2 if t < 2 * NPAIR else NPAIR
                        if t % 2 == 0:
                            src = filled(act, ch, f"up{t}", b)
                            if pair:
                                act.wait_ge(C[ch]["h"], at(b, NPAIR + 1, pair))
                            if t < 2 * NPAIR:
                                nc.scalar.activation(f["sg"][:], src[:], ACT.Silu,
                                                     scale=col[scales][:, t:t + 1]).then_inc(C[ch]["sg"], 1)
                            else:
                                nc.scalar.activation(f["sg"][HALF:P, :], src[0:HALF, :], ACT.Silu,
                                                     scale=col[scales][0:HALF, t:t + 1]).then_inc(C[ch]["sg"], 1)
                        if t % 2 or t == 2 * NPAIR:
                            act.wait_ge(C[ch]["h"], at(b, NPAIR + 1, pair + 1))
                            nc.scalar.copy(f["hh"][p0:P, pair, :], f["h32"][p0:P, pair % 2, :]).then_inc(C[ch]["hh"], 1)
                return go

            def x_tr2(b):
                for m in range(KD):
                    src = filled(act, "X", f"hs{m}", b)
                    nc.scalar.activation(hs32[:, m, :], src[:], ACT.Identity, bias=col["lnb"][:, m:m + 1],
                                         scale=col["lnw"][:, m:m + 1]).then_inc(hs_done, 1)

            def proj(b):
                for i in range(NT):
                    src = filled(act, "Y", f"sm{i}", b)
                    nc.scalar.activation(xbn[:, i, :], src[:, 0:2 * DXB], ACT.Copy, scale=1 / WS).then_inc(xbn_done, 1)
                act.preload_act_table_set("natural_log_exp_and_others")
                src = filled(act, "Y", "bt", b)
                nc.scalar.activation(bT[:], src[:], ACT.Copy, scale=1 / WS).then_inc(bT_done, 1)
                for j in range(GH):
                    if j == 0:
                        act.wait_ge(absz_done, at(b, 1, 1))
                        nc.scalar.activation(dte[:], dta[:], ACT.Exp, scale=-1.0).then_inc(e_done, 1)
                    if j == 1:
                        act.wait_ge(u_done, at(b, 1, 1))
                        nc.scalar.activation(dtl[:], dtu[:], ACT.Ln).then_inc(l_done, 1)
                    src = filled(act, "Y", f"ct{j}", b)
                    nc.scalar.activation(cT[:, j, :], src[:], ACT.Copy, scale=1 / WS).then_inc(cT_done, 1)

            def decays(b):
                src = filled(act, "Y", "cum", b)
                nc.scalar.activation(decs[:].rearrange("p w c h -> p (w c h)"), src[:, 0:3 * NT * NH], ACT.Exp).then_inc(
                    decs_done, 1)

            def gate(b):
                for i in range(NT):
                    src = filled(act, "Y", f"z{i}", b)
                    nc.scalar.activation(zs[:, i, :], src[:], ACT.Silu, scale=1 / WS).then_inc(z_done, 1)

            def seg(b, c):
                for g in range(NG):
                    src = filled(act, "Y", f"seg{c}_{g}", b)
                    nc.scalar.activation(E[:, c, g * GH:(g + 1) * GH, :].rearrange("p h t -> p (h t)"), src[:],
                                         ACT.Exp).then_inc(E_done, 1)

            def turned(b, c):
                act.wait_ge(yg_done, at(b, NT, c + 1))
                if c:
                    act.wait_ge(ss_done, at(b, NT, c))
                nc.scalar.activation(sq[:], yy[:, c % 2, :], ACT.Square, accum_out=ss[:, c:c + 1]).then_inc(ss_done, 1)
                src = filled(act, "Y", f"ty{c}", b)
                nc.scalar.copy(ygh[:, :, c * P:(c + 1) * P], src[:].rearrange("p (k t) -> p k t", k=KI)).then_inc(
                    ygh_done, 1)

            def fc1(b):
                for t in range(KF):
                    src = filled(act, "Y", f"f{t}", b)
                    if t >= 2:
                        act.wait_ge(gll_done, at(b, KF, t - 1))
                    nc.scalar.activation(gl32[:, t % 2, :], src[:], ACT.Gelu_apprx_tanh, bias=col["fc1b"][:, t:t + 1],
                                         scale=1 / WS).then_inc(gl_done, 1)

            weight("wqkv")
            split(0)
            weight("wo")
            act.wait_ge(rows_in, 16 * (len(COLS) + len(ROWS)))
            nc.scalar.activation(aneg[:], row["alog"][:], ACT.Exp).then_inc(aneg_done, 1)
            per_engine(act, {
                "weight": weight, ("X", "split"): lambda b: None if isinstance(b, int) and b == 0 else split(b),
                ("X", "qkv"): qkv, ("X", "tr"): split_tr("X", ["tr0", "tr1"]), ("X", "up"): up("X", "sup0"),
                ("X", "tr2"): x_tr2, ("Y", "proj"): proj, ("Y", "gate"): gate, ("Y", "decays"): decays,
                ("Y", "seg"): seg, ("Y", "turned"): turned, ("Y", "fc1"): fc1,
                ("Y", "tr"): split_tr("Y", ["tq0", "tq1"]), ("Y", "up"): up("Y", "sup1")})

        @block.vector
        def _(dve):
            v = nc.vector
            v.memset(zero_point[:], -ZERO_POINT).then_inc(zp_done, 1)
            v.memset(allone[:], 1.0).then_inc(consts, 1)
            v.memset(yout[:], 0.0).then_inc(stored, 1)
            v.memset(st[:], 0.0).then_inc(consts, 1)
            for tile, value in ((half, -0.5), (eps, EPS), (ws2_di, WS ** 2 / DI), (ws2_eps, WS ** 2 * EPS)):
                v.memset(tile[:], value).then_inc(consts, 1)

            def weight(name):
                i = WIDX[name]
                n, k, c, integer, scale = WEIGHTS[i]
                src, high, low_ = stage(n, k, c), hi[n], lo[n]
                dve.wait_ge(w_hi, i + 1)
                if n == "wout":
                    for kk in range(KI):
                        last = v.scalar_tensor_tensor(out=low_[:, kk, :], in0=src[:, kk * c:(kk + 1) * c],
                                                      scalar=normws[:, kk:kk + 1], in1=high[:, kk, :],
                                                      op0=ALU.mult, op1=ALU.subtract)
                else:
                    last = v.scalar_tensor_tensor(out=low_[:].rearrange("p k c -> p (k c)"),
                                                  in0=src.bitcast(I32) if integer else src,
                                                  scalar=-ZERO_POINT if integer else scale,
                                                  in1=high[:].rearrange("p k c -> p (k c)"),
                                                  op0=ALU.add if integer else ALU.mult, op1=ALU.subtract)
                last.then_inc(w_lo, 1)

            def low(out, src, high):
                return v.tensor_tensor(out, src, high, ALU.subtract)

            def norm_stats(ch, b, turn):
                f, c = F[ch], C[ch]
                dve.wait_ge(c["r"], at(b, RN[ch], NT // 2 * (turn + 1)))
                for i in range(NT):
                    v.bn_stats(f["stats"][:, i, :], f["r"][:, i, :]).then_inc(c["stats"], 1)
                dve.wait_ge(c["stats"], at(b, 2 * NT, (turn + 1) * NT))
                v.memset(spare[:], 0.0)
                for i in range(NT):
                    last = v.bn_aggr(f["mv"][:, i, :], f["stats"][:, i, :])
                last.then_inc(c["mv"], 1)

            def normed(ch, out, scale, done):
                f = F[ch]
                for i in range(NT):
                    last = v.tensor_scalar(out[:, i, :], f["r"][:, i, :], f["mv"][:, i, 0:1], scale[:, i:i + 1],
                                           ALU.subtract, ALU.mult)
                last.then_inc(done, 1)

            def split(b):
                dve.wait_ge(xh_done, at(b, 1, 1))
                low(xl[:], xt[:], xh[:]).then_inc(xl_done, 1)

            def qkv(b):
                for m in range(KD):
                    src = filled(dve, "X", f"v{m}", b)
                    dve.wait_ge(k_done, at(b, KD, m + 1))
                    if m:
                        dve.wait_ge(vh_done, at(b, KD, m))
                    v.tensor_tensor(kv[:], ksb[:, m, :], src[:], ALU.mult).then_inc(kv_done, 1)
                    dve.wait_ge(kv_done, at(b, KD, m + 1))
                    v.tensor_tensor_scan(kv[:], allone[:, 0:1].to_broadcast([P, S]), kv[:], 0.0, ALU.mult,
                                         ALU.add).then_inc(cum_done, 1)
                    src = filled(dve, "X", f"q{m}", b)
                    dve.wait_ge(cum_done, at(b, KD, m + 1))
                    v.scalar_tensor_tensor(out=vh32[:, m, :], in0=src[:], scalar=SSM_DENOM / WS, in1=kv[:],
                                           op0=ALU.mult, op1=ALU.mult).then_inc(vh_done, 1)

            def attn_out(b):
                f = F["X"]
                dve.wait_ge(xn_in, at(b, 16, 16))
                for i in range(NT // 2):
                    src = filled(dve, "X", f"o{i}", b)
                    pair = slice(2 * i, 2 * i + 2)
                    v.scalar_tensor_tensor(out=f["r"][:, pair, :].rearrange("p i d -> p (i d)"), in0=src[:],
                                           scalar=1 / WS, in1=xn[:, pair, :].rearrange("p i d -> p (i d)"),
                                           op0=ALU.mult, op1=ALU.add).then_inc(C["X"]["r"], 1)
                norm_stats("X", b, 0)
                dve.wait_ge(C["X"]["rs"], at(b, 2, 1))
                normed("X", f["xa"], f["rs"], C["X"]["xa"])

            def split_tr(ch, names):
                def go(b):
                    for m in range(KD):
                        dve.wait_ge(C[ch]["th"], at(b, KD, m + 1))
                        low(F[ch]["tl"][:, m, :], bank[use(ch, names[m])][:], F[ch]["th"][:, m, :]).then_inc(
                            C[ch]["tl"], 1)
                return go

            def up(ch, scales):
                def go(b, a, e):
                    f = F[ch]
                    for t in range(a, e):
                        if t % 2 == 0 and t < 2 * NPAIR:
                            continue
                        pair = t // 2
                        p0 = 0 if t < 2 * NPAIR else HALF
                        src = filled(dve, ch, f"up{t}", b)
                        dve.wait_ge(C[ch]["sg"], at(b, NPAIR + 1, pair + 1))
                        if pair >= 2:
                            dve.wait_ge(C[ch]["hl"], at(b, NPAIR + 1, pair - 1))
                        v.scalar_tensor_tensor(out=f["h32"][p0:P, pair % 2, :], in0=src[p0:P, :],
                                               scalar=col[scales][p0:P, t:t + 1], in1=f["sg"][p0:P, :],
                                               op0=ALU.mult, op1=ALU.mult).then_inc(C[ch]["h"], 1)
                return go

            def down(ch, scale_row, b, i):
                f = F[ch]
                src = filled(dve, ch, f"dn{i}", b)
                r = f["r"][:, 2 * i:2 * i + 2, :]
                v.tensor_tensor(r, src[:].rearrange("p (i d) -> p i d", i=2),
                                row[scale_row][:].unsqueeze(1).to_broadcast([P, 2, D]), ALU.mult).then_inc(
                    C[ch]["part"], 1)
                dve.wait_ge(C[ch]["part"], at(b, NT // 2, i + 1))
                v.tensor_tensor(r, r, f["xa"][:, 2 * i:2 * i + 2, :], ALU.add).then_inc(C[ch]["r"], 1)


            def z_down(b):
                for i in range(NT // 2):
                    down("Y", "sdn1", b, i)
                norm_stats("Y", b, 1)
                dve.wait_ge(C["Y"]["rs"], at(b, 2, 2))
                dve.wait_ge(stored, at(b, 16, 1))
                normed("Y", yout, F["Y"]["rs"], yout_done)

            def x_sum(b, i):
                down("X", "sdn0", b, i)
                if i:
                    norm_stats("X", b, 1)

            def x_hat(b):
                dve.wait_ge(hsc_done, at(b, 1, 1))
                normed("X", hat, hsc, hat_done)

            def x_x2(b):
                dve.wait_ge(twice_done, at(b, 1, 1))
                normed("X", x2, twice, x2_done)

            def x_tr2(b):
                for m in range(KD):
                    dve.wait_ge(hs_done, at(b, KD, m + 1))
                    v.tensor_copy(hsh[:, m, :], hs32[:, m, :]).then_inc(hsh_done, 1)
                    dve.wait_ge(hsh_done, at(b, KD, m + 1))
                    low(hsl[:, m, :], hs32[:, m, :], hsh[:, m, :]).then_inc(hsl_done, 1)

            def proj(b):
                for i in range(NT):
                    src = filled(dve, "Y", f"sm{i}", b)
                    dve.wait_ge(xbn_done, at(b, NT, i + 1))
                    v.scalar_tensor_tensor(out=dtz[:, i * NH:(i + 1) * NH], in0=src[:, 2 * DXB:NSMALL], scalar=1 / WS,
                                           in1=row["dtb"][:], op0=ALU.mult, op1=ALU.add).then_inc(dtz_done, 1)
                dve.wait_ge(dtz_done, at(b, NT, NT))
                v.scalar_tensor_tensor(out=dta[:], in0=dtz[:], scalar=-1.0, in1=dtz[:], op0=ALU.mult,
                                       op1=ALU.max).then_inc(absz_done, 1)
                dve.wait_ge(e_done, at(b, 1, 1))
                v.tensor_scalar(dtu[:], dte[:], 1.0, None, ALU.add).then_inc(u_done, 1)
                dve.wait_ge(u_done, at(b, 1, 1))
                v.tensor_scalar(dtd[:], dtu[:], -1.0, None, ALU.add).then_inc(dt_step, 1)
                dve.wait_ge(dt_step, at(b, 9, 1))
                v.tensor_scalar(dtq[:], dtd[:], -0.5, 1.0, ALU.mult, ALU.add).then_inc(dt_step, 1)
                dve.wait_ge(dt_step, at(b, 9, 2))
                v.tensor_tensor(dtq[:], dtq[:], dtd[:], ALU.mult).then_inc(dt_step, 1)
                dve.wait_ge(dt_step, at(b, 9, 3))
                dve.wait_ge(l_done, at(b, 1, 1))
                v.tensor_tensor(dtq[:], dtq[:], dtl[:], ALU.max).then_inc(dt_step, 1)
                dve.wait_ge(dt_step, at(b, 9, 4))
                v.tensor_tensor(dtq[:], dtq[:], dtd[:], ALU.min).then_inc(dt_step, 1)
                dve.wait_ge(dt_step, at(b, 9, 5))
                v.tensor_scalar(dtd[:], dtd[:], 1e-30, None, ALU.add).then_inc(dt_step, 1)
                dve.wait_ge(dt_step, at(b, 9, 6))
                v.reciprocal(dtd[:], dtd[:]).then_inc(dt_step, 1)
                dve.wait_ge(dt_step, at(b, 9, 7))
                v.scalar_tensor_tensor(out=dtq[:], in0=dtq[:], scalar=1e-30, in1=dtd[:], op0=ALU.add,
                                       op1=ALU.mult).then_inc(dt_step, 1)
                dve.wait_ge(dt_step, at(b, 9, 8))
                v.tensor_tensor(dtq[:], dtq[:], dte[:], ALU.mult).then_inc(dt_step, 1)
                dve.wait_ge(dt_step, at(b, 9, 9))
                v.scalar_tensor_tensor(out=dt[:].rearrange("p c h -> p (c h)"), in0=dtz[:], scalar=0.0, in1=dtq[:],
                                       op0=ALU.max, op1=ALU.add).then_inc(dt_done, 1)
                dve.wait_ge(dt_done, at(b, 1, 1))
                v.tensor_tensor(dta[:].rearrange("p (c h) -> p c h", c=NT), dt[:],
                                aneg[:].unsqueeze(1).to_broadcast([P, NT, NH]), ALU.mult).then_inc(dta_done, 1)
                dve.wait_ge(dta_done, at(b, 1, 1))
                v.tensor_scalar(aexp[:].rearrange("p c h -> p (c h)"), dta[:], DECAY_FLOOR, None, ALU.max).then_inc(
                    a_done, 1)
                dve.wait_ge(a_done, at(b, 1, 1))
                v.tensor_copy(ah[:], aexp[:]).then_inc(ah_done, 1)
                dve.wait_ge(ah_done, at(b, 1, 1))
                low(al[:], aexp[:], ah[:]).then_inc(al_done, 1)
                for c in range(2):
                    exponents(b, c)

            def seg(b, c):
                if c < NT - 2:
                    exponents(b, c + 2)

            def exponents(b, c):
                for n in range(NG):
                    group = slice(n * GH, (n + 1) * GH)
                    if c >= 2:
                        filled(dve, "Y", f"seg{c - 2}_{n}", b)
                    dve.wait_ge(al_done, at(b, 1, 1))
                    v.tensor_tensor(Rl[c % 2][:, group, :], al[:, c, group].unsqueeze(2).to_broadcast([P, GH, P]),
                                    upto16[:].unsqueeze(1).to_broadcast([P, GH, P]), ALU.mult).then_inc(Rl_done, 1)

            def pairs(b, c):
                for g in range(NG):
                    src = filled(dve, "Y", f"g{c}_{g}", b)
                    dve.wait_ge(E_done, at(b, NT * NG, c * NG + g + 1))
                    w = E[:, c, g * GH:(g + 1) * GH, :].rearrange("p h t -> p (h t)")
                    v.tensor_tensor(w, src[:], w, ALU.mult).then_inc(W_done, 1)

            def chunk(b, c):
                y = yy[:, c % 2, :]
                src = filled(dve, "Y", f"yi{c}", b)
                dve.wait_ge(dx_done, at(b, NT, c + 1))
                v.tensor_tensor(y, src[:], y, ALU.add).then_inc(yi_done, 1)
                if c:
                    src = filled(dve, "Y", f"yx{c}", b)
                    s3 = src[:].rearrange("p (h d) -> p h d", h=NH)
                    v.tensor_tensor(s3, s3, decs[:, 0, c, :].unsqueeze(2).to_broadcast([P, NH, HD]),
                                    ALU.mult).then_inc(yb_done, 1)
                    dve.wait_ge(yb_done, at(b, NT - 1, c))
                    dve.wait_ge(yi_done, at(b, NT, c + 1))
                    v.tensor_tensor(y, src[:], y, ALU.add).then_inc(y_done, 1)
                if c < NT - 1:
                    dve.wait_ge(decs_done, at(b, 1, 1))
                    src = filled(dve, "Y", f"ds{c}", b)
                    for g in range(NG):
                        part = slice(g * HD, (g + 1) * HD)
                        own = src[part, g * GH * HD:(g + 1) * GH * HD].rearrange("p (j d) -> p j d", j=GH)
                        if c == 0:
                            last = v.tensor_copy(st[part, g, :, :], own)
                        else:
                            filled(dve, "Y", f"yx{c}", b)
                            dve.wait_ge(st_done, at(b, NT - 1, c))
                            v.tensor_tensor(st[part, g, :, :], st[part, g, :, :],
                                            decs[part, 1, c, g * GH:(g + 1) * GH].unsqueeze(2).to_broadcast([HD, GH, HD]),
                                            ALU.mult).then_inc(st_step, 1)
                            dve.wait_ge(st_step, at(b, (NT - 2) * NG, (c - 1) * NG + g + 1))
                            last = v.tensor_tensor(st[part, g, :, :], st[part, g, :, :], own, ALU.add)
                    last.then_inc(st_done, 1)

            def turned(b, c):
                dve.wait_ge(ygh_done, at(b, NT, c + 1))
                tok_part = slice(c * P, (c + 1) * P)
                low(ygl[:, :, tok_part], bank[use("Y", f"ty{c}")][:].rearrange("p (k t) -> p k t", k=KI),
                    ygh[:, :, tok_part]).then_inc(ygl_done, 1)

            def fc1(b):
                for t in range(KF):
                    dve.wait_ge(gl_done, at(b, KF, t + 1))
                    v.tensor_copy(glh[:, t, :], gl32[:, t % 2, :]).then_inc(glh_done, 1)

            def fc2(b):
                dve.wait_ge(x2b_done, at(b, 1, 1))
                for i in range(NT // 2):
                    src = filled(dve, "Y", f"m{i}", b)
                    x2p = x2[:, 2 * i:2 * i + 2, :].rearrange("p i d -> p (i d)")
                    v.scalar_tensor_tensor(out=x2p, in0=src[:], scalar=1 / WS, in1=x2p, op0=ALU.mult,
                                           op1=ALU.add).then_inc(m_done, 1)

            def y_out(b):
                f = F["Y"]
                dve.wait_ge(rms_done, at(b, 1, 1))
                dve.wait_ge(m_done, at(b, NT // 2, NT // 2))
                for i in range(NT):
                    src = filled(dve, "Y", f"o{i // 2}", b)
                    last = v.scalar_tensor_tensor(out=f["r"][:, i, :], in0=src[:, i % 2 * D:(i % 2 + 1) * D],
                                                  scalar=rms[:, i:i + 1], in1=x2[:, i, :], op0=ALU.mult, op1=ALU.add)
                    if i % 2:
                        last.then_inc(C["Y"]["r"], 1)
                norm_stats("Y", b, 0)
                dve.wait_ge(C["Y"]["rs"], at(b, 2, 1))
                normed("Y", f["xa"], f["rs"], C["Y"]["xa"])

            weight("wqkv")
            split(0)
            weight("wo")
            dve.wait_ge(masks, 7)
            dve.wait_ge(rows_in, 16 * (len(COLS) + len(ROWS)))
            v.tensor_scalar(normws[:], col["normw"][:], WS, None, ALU.mult).then_inc(normws_done, 1)
            dve.wait_ge(aneg_done, 1)
            v.tensor_scalar(aneg[:], aneg[:], -1.0, None, ALU.mult).then_inc(aneg_done, 1)
            per_engine(dve, {
                "weight": weight, ("X", "split"): lambda b: None if isinstance(b, int) and b == 0 else split(b),
                ("X", "qkv"): qkv, ("X", "out"): attn_out, ("X", "tr"): split_tr("X", ["tr0", "tr1"]),
                ("X", "up"): up("X", "sup0"), ("X", "sum"): x_sum, ("X", "hat"): x_hat, ("X", "x2"): x_x2,
                ("X", "tr2"): x_tr2, ("Y", "proj"): proj, ("Y", "seg"): seg, ("Y", "pairs"): pairs, ("Y", "chunk"): chunk, ("Y", "turned"): turned,
                ("Y", "fc1"): fc1, ("Y", "fc2"): fc2, ("Y", "out"): y_out, ("Y", "tr"): split_tr("Y", ["tq0", "tq1"]),
                ("Y", "up"): up("Y", "sup1"), ("Z", "down"): z_down})

        @block.gpsimd
        def _(pool):
            g = nc.gpsimd
            for tile, value in ((ident, 0.0), (upto, 1.0), (after, 1.0), (upto16, 1.0), (after16, 1.0), (negid, 0.0),
                                (past, 1.0)):
                g.memset(tile[:], value).then_inc(consts, 1)
            pool.wait_ge(consts, 13)
            g.affine_select(out=ident[:], in_=ident[:], pattern=[[-1, P]], compare_op=ALU.not_equal, fill=1.0, base=0,
                            channel_multiplier=1).then_inc(masks, 1)
            for tile in (upto, upto16):
                g.affine_select(out=tile[:], in_=tile[:], pattern=[[1, P]], compare_op=ALU.is_ge, fill=0.0, base=0,
                                channel_multiplier=-1).then_inc(masks, 1)
            for tile in (after, after16):
                g.affine_select(out=tile[:], in_=tile[:], pattern=[[-1, P]], compare_op=ALU.is_gt, fill=0.0, base=0,
                                channel_multiplier=1).then_inc(masks, 1)
            g.affine_select(out=negid[:], in_=negid[:], pattern=[[-1, P]], compare_op=ALU.not_equal, fill=MASKED,
                            base=0, channel_multiplier=1).then_inc(masks, 1)
            g.affine_select(out=past[:], in_=past[:], pattern=[[0, GH], [-1, P]], compare_op=ALU.is_gt, fill=0.0,
                            base=0, channel_multiplier=1).then_inc(masks, 1)
            pool.wait_ge(masks, 7)
            pool.wait_ge(rows_in, 16 * (len(COLS) + len(ROWS)))

            def inv_root(ch, b, turn):
                f, c = F[ch], C[ch]
                pool.wait_ge(c["mv"], at(b, 2, turn + 1))
                g.tensor_tensor(f["ve"][:], f["mv"][:, :, 1], eps[:], ALU.add).then_inc(c["ve"], 1)
                pool.wait_ge(c["ve"], at(b, 2, turn + 1))
                g.tensor_tensor(f["rs"][:], f["ve"][:], half[:], ALU.pow).then_inc(c["rs"], 1)

            def qkv(b):
                for m in range(KD):
                    pool.wait_ge(vhh_done, at(b, KD, m + 1))
                    g.tensor_tensor(vhl[:, m, :], vh32[:, m, :], vhh[:, m, :], ALU.subtract).then_inc(vhl_done, 1)

            def up(ch):
                def go(b, a, e):
                    f = F[ch]
                    for t in range(a, e):
                        if t % 2 == 0 and t < 2 * NPAIR:
                            continue
                        pair = t // 2
                        p0 = 0 if t < 2 * NPAIR else HALF
                        pool.wait_ge(C[ch]["hh"], at(b, NPAIR + 1, pair + 1))
                        if p0:
                            pool.wait_ge(C[ch]["hl"], at(b, NPAIR + 1, pair))
                        g.tensor_tensor(f["hl"][p0:P, pair, :], f["h32"][p0:P, pair % 2, :], f["hh"][p0:P, pair, :],
                                        ALU.subtract).then_inc(C[ch]["hl"], 1)
                        if p0:
                            pool.wait_ge(C[ch]["hl"], at(b, NPAIR + 1, pair + 1))
                return go

            def x_sum(b, i):
                if i == 0:
                    return
                inv_root("X", b, 1)
                f = F["X"]
                pool.wait_ge(C["X"]["rs"], at(b, 2, 2))
                g.tensor_tensor(twice[:], f["rs"][:], f["rs"][:], ALU.add).then_inc(twice_done, 1)
                g.tensor_tensor(rx2[:], f["rs"][:], f["rs"][:], ALU.mult).then_inc(rx2_done, 1)
                pool.wait_ge(rx2_done, at(b, 1, 1))
                g.tensor_tensor(vx[:], f["mv"][:, :, 1], rx2[:], ALU.mult).then_inc(vx_done, 1)
                pool.wait_ge(vx_done, at(b, 1, 1))
                g.tensor_tensor(vx[:], vx[:], eps[:], ALU.add).then_inc(vxe_done, 1)
                pool.wait_ge(vxe_done, at(b, 1, 1))
                g.tensor_tensor(vy[:], vx[:], half[:], ALU.pow).then_inc(vy_done, 1)
                pool.wait_ge(vy_done, at(b, 1, 1))
                g.tensor_tensor(hsc[:], f["rs"][:], vy[:], ALU.mult).then_inc(hsc_done, 1)

            def x_x2(b):
                pool.wait_ge(x2_done, at(b, 1, 1))
                g.tensor_tensor(x2[:], x2[:], row["fc2b"][:].unsqueeze(1).to_broadcast([P, NT, D]), ALU.add).then_inc(
                    x2b_done, 1)

            def proj(b):
                for c in range(2):
                    exponents(b, c)

            def seg(b, c):
                if c < NT - 2:
                    exponents(b, c + 2)

            def exponents(b, c):
                for n in range(NG):
                    group = slice(n * GH, (n + 1) * GH)
                    if c >= 2:
                        filled(pool, "Y", f"seg{c - 2}_{n}", b)
                    pool.wait_ge(ah_done, at(b, 1, 1))
                    g.tensor_tensor(Rh[c % 2][:, group, :], ah[:, c, group].unsqueeze(2).to_broadcast([P, GH, P]),
                                    upto16[:].unsqueeze(1).to_broadcast([P, GH, P]), ALU.mult).then_inc(Rh_done, 1)

            def pairs(b, c):
                x3 = xbn[:, c, 0:DXB].rearrange("p (g o d) -> p g o d", g=NG, o=1).to_broadcast([P, NG, GH, HD])
                if c == 0:
                    pool.wait_ge(xbn_done, at(b, NT, NT))
                    pool.wait_ge(dt_done, at(b, 1, 1))
                if c >= 2:
                    filled(pool, "Y", f"yi{c - 2}", b)
                    pool.wait_ge(xw_done, at(b, NT - 1, c - 1))
                g.tensor_tensor(xdt[:, c % 2].rearrange("p (g j) d -> p g j d", g=NG), x3,
                                dt[:, c, :].rearrange("p (g j o) -> p g j o", g=NG, o=1).to_broadcast([P, NG, GH, HD]),
                                ALU.mult).then_inc(xdt_done, 1)
                if c >= 2:
                    filled(pool, "Y", f"ty{c - 2}", b)
                    pool.wait_ge(ss_done, at(b, NT, c - 1))
                g.tensor_tensor(yy[:, c % 2, :].rearrange("p (g j d) -> p g j d", g=NG, j=GH), x3,
                                row["dskip"][:].rearrange("p (g j o) -> p g j o", g=NG, o=1).to_broadcast(
                                    [P, NG, GH, HD]), ALU.mult).then_inc(dx_done, 1)
                if c < NT - 1:
                    if c:
                        filled(pool, "Y", f"ds{c - 1}", b)
                    pool.wait_ge(xdt_done, at(b, NT, c + 1))
                    pool.wait_ge(decs_done, at(b, 1, 1))
                    g.tensor_tensor(xw[:], xdt[:, c % 2], decs[:, 2, c, :].unsqueeze(2).to_broadcast([P, NH, HD]),
                                    ALU.mult).then_inc(xw_done, 1)

            def chunk(b, c):
                pool.wait_ge(z_done, at(b, NT, c + 1))
                if c:
                    pool.wait_ge(y_done, at(b, NT - 1, c))
                else:
                    pool.wait_ge(yi_done, at(b, NT, 1))
                g.tensor_tensor(yy[:, c % 2, :], yy[:, c % 2, :], zs[:, c, :], ALU.mult).then_inc(yg_done, 1)

            def turned(b, c):
                if c < NT - 1:
                    return
                pool.wait_ge(ss_done, at(b, NT, NT))
                g.tensor_tensor(rms[:], ss[:], ws2_di[:], ALU.mult).then_inc(rms_step, 1)
                pool.wait_ge(rms_step, at(b, 2, 1))
                g.tensor_tensor(rms[:], rms[:], ws2_eps[:], ALU.add).then_inc(rms_step, 1)
                pool.wait_ge(rms_step, at(b, 2, 2))
                g.tensor_tensor(rms[:], rms[:], half[:], ALU.pow).then_inc(rms_done, 1)

            def fc1(b):
                for t in range(KF):
                    pool.wait_ge(glh_done, at(b, KF, t + 1))
                    g.tensor_tensor(gll[:, t, :], gl32[:, t % 2, :], glh[:, t, :], ALU.subtract).then_inc(gll_done, 1)

            per_engine(pool, {
                ("X", "qkv"): qkv, ("X", "out"): lambda b: inv_root("X", b, 0), ("X", "up"): up("X"),
                ("X", "sum"): x_sum, ("X", "x2"): x_x2, ("Y", "proj"): proj, ("Y", "seg"): seg, ("Y", "pairs"): pairs,
                ("Y", "chunk"): chunk, ("Y", "turned"): turned, ("Y", "fc1"): fc1, ("Y", "out"): lambda b: inv_root("Y", b, 0),
                ("Y", "up"): up("Y"), ("Z", "down"): lambda b: inv_root("Y", b, 1)})


def ktiles(w):
    k, c = w.shape
    if k % P:
        w = np.concatenate([w[:k // P * P], np.zeros((P - k % P, c), w.dtype), w[k // P * P:]])
    return np.ascontiguousarray(w.reshape(-1, P, c).transpose(1, 0, 2)).reshape(P, -1)


def up_order(gate, up):
    parts = []
    for t in range(NPAIR):
        parts += [gate[t * P:(t + 1) * P], up[t * P:(t + 1) * P]]
    return np.concatenate(parts + [gate[NPAIR * P:], up[NPAIR * P:]])


def columns(v):
    return np.ascontiguousarray(v.reshape(-1, P).T)


def kernel(**inputs):
    import concourse.bacc as bacc
    from concourse.bass_utils import run_bass_kernel_spmd

    a = {n: np.asarray(x) for n, x in inputs.items()}
    win = a["L1_attn_W_in"]
    z, x, bp, cp, dt_ = np.split(win, [DI, DI + DXB, DI + 2 * DXB, 2 * DI + 2 * DXB], axis=1)
    cp = cp.reshape(D, NG, GH, HD).transpose(0, 2, 1, 3).reshape(D, DI)
    arrays = {
        "x": a["L0_attn_x"], "xt": np.ascontiguousarray(a["L0_attn_x"].transpose(0, 2, 1)),
        "wqkv": ktiles(np.concatenate([a["L0_attn_Wq"].T, a["L0_attn_Wk"].T, a["L0_attn_Wv"].T], axis=1)),
        "wo": ktiles(a["L0_attn_Wo"].T),
        "up0": ktiles(up_order(a["L0_ffn_wq_gate"], a["L0_ffn_wq_up"]).T), "dn0": ktiles(a["L0_ffn_wq_down"].T),
        "win": ktiles(np.concatenate([z, x, bp, dt_, cp], axis=1)), "fc1": ktiles(a["L1_attn_fc1_w"]),
        "wout": ktiles(a["L1_attn_W_out"]), "fc2": ktiles(a["L1_attn_fc2_w"]),
        "up1": ktiles(up_order(a["L1_ffn_gate_w"], a["L1_ffn_up_w"]).T), "dn1": ktiles(a["L1_ffn_down_w"].T),
        "lnw": columns(a["L1_attn_ln_w"]), "lnb": columns(a["L1_attn_ln_b"]), "fc1b": columns(a["L1_attn_fc1_b"]),
        "normw": columns(a["L1_attn_norm_w"]),
        "sup0": columns(up_order(a["L0_ffn_s_gate"], a["L0_ffn_s_up"])),
        "sup1": columns(up_order(a["L1_ffn_gate_s"], a["L1_ffn_up_s"])),
        "dtb": a["L1_attn_dt_bias"], "alog": a["L1_attn_A_log"], "dskip": a["L1_attn_D"],
        "sdn0": a["L0_ffn_s_down"], "sdn1": a["L1_ffn_down_s"], "fc2b": a["L1_attn_fc2_b"]}
    nc = bacc.Bacc("TRN2", target_bir_lowering=False, num_devices=1, dynamic_dma_scratch_size=1024)
    ins = {n: nc.dram_tensor(f"in_{n}", v.shape, mybir.dt.from_np(v.dtype), kind="ExternalInput").ap()
           for n, v in arrays.items()}
    out = nc.dram_tensor("out", (NB, S, D), F32, kind="ExternalOutput").ap()
    build(nc, ins, out)
    r = run_bass_kernel_spmd(nc, [{f"in_{n}": np.ascontiguousarray(v) for n, v in arrays.items()}], core_ids=[0])
    return r.results[0]["out"]
```

```python
from contextlib import ExitStack

import numpy as np

import concourse.bass as bass
from concourse import mybir

ALU = mybir.AluOpType
ACT = mybir.ActivationFunctionType
F32 = mybir.dt.float32
F16 = mybir.dt.float16
I32 = mybir.dt.int32

P = 128
NB, S, D = 8, 512, 256
KD = D // P
NT = S // P
HID = 704
NPAIR = HID // P
NUP = 2 * NPAIR + 1
HALF = P // 2
DI, DXB, NH, HD = 512, 128, 8, 64
NG = 2
GH = NH // NG
INTER = 1024
KI = DI // P
KF = INTER // P
CZ, CX, CC = 0, DI, DI + 2 * DXB + NH
NSMALL = 2 * DXB + NH
WIN = CC + DI
EPS = 1e-5
WS = 64.0
ZERO_POINT = 128.0
DECAY_FLOOR = -110.0
SSM_DENOM = float(D) ** 0.5 / S


def at(b, per, k):
    return b * per + k


def plan(names, first):
    count, uses = [0] * 4, {}
    for i, name in enumerate(names):
        uses[name] = (first + i % 4, count[i % 4])
        count[i % 4] += 1
    return uses, {first + j: count[j] for j in range(4)}


QKV_USES = [f"{w}{m}" for m in range(KD) for w in "kvq"]
X_USES = ([f"o{i}" for i in range(NT // 2)] + [f"tr{m}" for m in range(KD)] + [f"up{t}" for t in range(NUP)]
          + [f"dn{i}" for i in range(NT // 2)] + QKV_USES + [f"hs{m}" for m in range(KD)])
SCHED = [("Z", "down"), ("Y", "gate"), ("Y", "proj"), ("X", "out", 0), ("Y", "decays"), ("Y", "seg", 0),
         ("Y", "seg", 1), ("X", "out", 1), ("X", "res"), ("Y", "seg", 2), ("Y", "seg", 3), ("Y", "fc1"), ("X", "tr"),
         ("Y", "mask", 0), ("Y", "mask", 1), ("Y", "fc2", 0), ("Y", "mask", 2), ("Y", "mask", 3), ("Y", "fc2", 1),
         ("Y", "pairs", 0), ("Y", "pairs", 1), ("X", "up", 0, 3), ("Y", "chunk", 0), ("X", "up", 3, 4),
         ("Y", "pairs", 2), ("X", "up", 4, 5), ("Y", "turned", 0), ("Y", "chunk", 1), ("X", "up", 5, 6),
         ("Y", "pairs", 3), ("X", "up", 6, 8), ("Y", "turned", 1), ("Y", "chunk", 2), ("X", "up", 8, 11),
         ("Y", "turned", 2), ("Y", "chunk", 3), ("X", "down"), ("W", "split"), ("X", "sum", 0), ("Y", "turned", 3),
         ("X", "sum", 1), ("X", "root"), ("Y", "out"), ("W", "qkv", 0), ("W", "vh", 0), ("Y", "norm"), ("X", "hat"),
         ("W", "qkv", 1), ("Y", "tr"), ("X", "tr2"), ("W", "vh", 1), ("Y", "up", 0, 11), ("X", "hs"), ("X", "x2")]
EXACT = ("up0", "dn0", "dn1", "up1")
EXACT_TURN = {("X", "up", 4, 5): "up0", ("X", "up", 6, 8): "dn0", ("W", "split"): "dn1", ("X", "sum", 1): "up1",
              ("X", "tr2"): None}
HIGH_TURN = {("Y", "proj"): "dn0", ("X", "out", 1): "win", ("X", "res"): "dn1", ("X", "up", 0, 3): "fc1",
             ("X", "up", 6, 8): "up1", ("X", "up", 8, 11): "wout", ("X", "hs"): "fc2"}
LOW_TURN = {("X", "res"): "dn0", ("X", "up", 0, 3): "win", ("X", "up", 3, 4): "fc1", ("X", "down"): "wout",
            ("X", "x2"): "fc2"}
POOL_LOW_TURN = {("X", "res"): "dn1", ("X", "up", 8, 11): "up1"}
FIRST = [step for step in SCHED if step != ("W", "vh", 1)]
FIRST.insert(FIRST.index(("X", "hs")) + 1, ("W", "vh", 1))
LAST_X = SCHED[:SCHED.index(("X", "up", 8, 11))] + [
    ("X", "up", 8, 9), ("Y", "turned", 2), ("Y", "chunk", 3), ("X", "up", 9, 11), ("Y", "turned", 3), ("Y", "out"),
    ("X", "down"), ("X", "sum", 0), ("Y", "norm"), ("Y", "tr"), ("X", "sum", 1), ("X", "root"), ("Y", "up", 0, 5),
    ("X", "hat"), ("Y", "up", 5, 11), ("X", "tr2"), ("X", "hs"), ("X", "x2")]
Y_PARTS = {"down": lambda: [f"dn{i}" for i in range(NT // 2)],
           "proj": lambda: [f"sm{i}" for i in range(NT)] + ["bt"] + [f"ct{j}" for j in range(GH)],
           "gate": lambda: [f"z{i}" for i in range(NT)], "decays": lambda: ["cum"],
           "seg": lambda c: [f"seg{c}_{g}" for g in range(NG)], "pairs": lambda c: [f"g{c}_{g}" for g in range(NG)],
           "chunk": lambda c: [f"yi{c}"] + ([f"yx{c}"] if c else []) + ([f"ds{c}"] if c < NT - 1 else []),
           "turned": lambda c: [f"ty{c}"], "fc1": lambda: [f"f{t}" for t in range(KF)],
           "fc2": lambda i: [f"m{i}"], "out": lambda: [f"o{i}" for i in range(NT // 2)],
           "norm": lambda: [], "mask": lambda c: [],
           "tr": lambda: [f"tq{m}" for m in range(KD)], "up": lambda a, e: [f"up{t}" for t in range(a, e)]}
LAST_Y = [s for s in SCHED if s[:2] not in (("Y", "fc2"), ("Y", "mask"))]
for before, step in ((("Y", "turned", 2), ("Y", "fc2", 0)), (("Y", "turned", 3), ("Y", "fc2", 1)),
                     (("Y", "fc1"), ("Y", "mask", 0)), (("Y", "fc1"), ("Y", "mask", 1)),
                     (("Y", "pairs", 2), ("Y", "mask", 2)), (("Y", "pairs", 3), ("Y", "mask", 3))):
    LAST_Y.insert(LAST_Y.index(before), step)


def y_uses(sched):
    return [use for chain in "YZ" for ch, kind, *arg in sched if ch == chain for use in Y_PARTS[kind](*arg)]


XU, XN = plan(X_USES, 0)
QKV_COUNT = {k: sum(XU[u][0] == k for u in QKV_USES) for k in range(4)}
YU, YN = plan(y_uses(SCHED), 4)
YU_LAST, _ = plan(y_uses(LAST_Y), 4)
COUNTS = {"X": XN, "Y": YN}


def uses(ch, b):
    return XU if ch == "X" else YU_LAST if isinstance(b, int) and b == NB - 1 else YU


WEIGHTS = [
    ("wqkv", KD, 3 * D, False, WS), ("wo", KD, D, False, WS), ("up0", KD, NUP * P, True, 1.0),
    ("dn0", NPAIR + 1, D, True, 1.0), ("win", KD, WIN, False, WS), ("dn1", NPAIR + 1, D, False, 1.0),
    ("fc1", KD, INTER, False, WS), ("up1", KD, NUP * P, False, 1.0), ("wout", KI, D, False, WS),
    ("fc2", KF, D, False, WS)]
WIDX = {w[0]: i for i, w in enumerate(WEIGHTS)}
POOL_LOWS = ["dn1", "up1"]
DVE_LOWS = [w[0] for w in WEIGHTS if w[0] not in POOL_LOWS]
STAGES = [("up0", "win", "up1"), ("wqkv", "wo", "dn0", "fc1", "wout", "fc2"), ("dn1",)]
STAGE_OF = {n: i for i, names in enumerate(STAGES) for n in names}
WIDE = max(k * c for n, k, c, _, _ in WEIGHTS if STAGE_OF[n] == 0)
LOADS = ["wqkv", "wo", "up0", "dn0", "dn1", "win", "fc1", "up1", "wout", "fc2"]


COLS = {"lnw": KD, "lnb": KD, "fc1b": KF, "normw": KI, "sup0": NUP, "sup1": NUP}
ROWS = {"dtb": NH, "alog": NH, "dskip": NH, "sdn0": D, "sdn1": D, "fc2b": D}


def starts(sizes):
    ends = np.cumsum([0] + list(sizes.values())).tolist()
    return dict(zip(sizes, ends))


def build(nc, ins, out):
    with ExitStack() as ctx:
        def sb(name, shape, dt=F32):
            return ctx.enter_context(nc.sbuf_tensor(name, shape, dt))

        def sem(name):
            return ctx.enter_context(nc.semaphore(name))

        bank = [ctx.enter_context(nc.psum_tensor(f"bank{i}", [P, 512], F32)) for i in range(8)]
        full = [sem(f"full{i}") for i in range(8)]

        hi = {n: sb(f"{n}_hi", [P, k, c], F16) for n, k, c, _, _ in WEIGHTS}
        lo = {n: sb(f"{n}_lo", [P, k, c], F16) for n, k, c, _, _ in WEIGHTS}
        decay = sb("decay", [P, (NT + 1) * NH * P])

        def stage(n, k, c):
            start, tile = [(0, decay[:]), (WIDE, decay[:]), (0, cT[:].rearrange("p j s -> p (j s)"))][STAGE_OF[n]]
            return tile[:, start:start + k * c]

        cols, rows = sb("cols", [P, sum(COLS.values())]), sb("rows", [P, sum(ROWS.values())])
        col = {n: cols[:, c:c + COLS[n]] for n, c in starts(COLS).items()}
        row = {n: rows[:, c:c + ROWS[n]] for n, c in starts(ROWS).items()}
        ident = sb("ident", [P, P])
        allone = sb("allone", [P, P])
        upto = sb("upto", [P, P])
        after = sb("after", [P, P])
        upto16, after16 = sb("upto16", [P, P], F16), sb("after16", [P, P], F16)
        spare = sb("spare", [P, 1])
        rest = sb("rest", [P, len(EXACT)])
        all_exact = sb("all_exact", [1, 1], I32)
        half = sb("half", [P, NT])
        eps, ws2_di, ws2_eps = sb("eps", [P, NT]), sb("ws2_di", [P, NT]), sb("ws2_eps", [P, NT])
        zero_point = sb("zero_point", [P, 1])
        normws = sb("normws", [P, KI])
        aneg = sb("aneg", [P, NH])

        xt = sb("xt", [P, KD, S])
        xn = sb("xn", [P, NT, D])
        xh, xl = sb("xh", [P, KD, S], F16), sb("xl", [P, KD, S], F16)
        ksb = sb("ksb", [P, KD, S])
        kv = sb("kv", [P, S])
        vh32 = ksb
        vhh, vhl = sb("vhh", [P, KD, S], F16), sb("vhl", [P, KD, S], F16)
        x2 = sb("x2", [P, NT, D])
        hsh, hsl = sb("hsh", [P, KD, S], F16), sb("hsl", [P, KD, S], F16)
        bT = sb("bT", [P, S])
        cT = sb("cT", [P, GH, S])
        hs32 = cT[:, 0:KD, :]
        xbn = sb("xbn", [P, NT, 2 * DXB])
        zs = sb("zs", [P, NT, DI])
        dtz = sb("dtz", [P, NT * NH])
        dta, dte, dtu, dtl, dtd, dtq = (sb(n, [P, NT * NH]) for n in ("dta", "dte", "dtu", "dtl", "dtd", "dtq"))
        dt = sb("dt", [P, NT, NH])
        aexp = sb("aexp", [P, NT, NH])
        decs = sb("decs", [P, 3, NT, NH])
        E = decay[:, 0:NT * NH * P].rearrange("p (c h t) -> p c h t", c=NT, h=NH)
        Rh, Rl = ([decay[:, (2 * k + i) * NH * P // 2:(2 * k + i + 1) * NH * P // 2].bitcast(F16).rearrange(
            "p (h t) -> p h t", h=NH) for k in (NT - 1, NT)] for i in range(2))
        ah, al = sb("ah", [P, NT, NH], F16), sb("al", [P, NT, NH], F16)
        xdt = sb("xdt", [P, 2, NH, HD])
        xw = sb("xw", [P, NH, HD])
        st = sb("st", [P, NG, GH, HD])
        yy = sb("yy", [P, 2, DI])
        sq = sb("sq", [P, DI], F16)
        ss = sb("ss", [P, NT])
        rms = sb("rms", [P, NT])
        ygh, ygl = sb("ygh", [P, KI, S], F16), sb("ygl", [P, KI, S], F16)
        wide_h, wide_l = sb("wide_h", [P, KF, S], F16), sb("wide_l", [P, KF, S], F16)
        glh, gll = wide_h, wide_l
        sg = sb("sg", [P, 2, S])
        F = {}
        for ch in "XY":
            F[ch] = dict(
                r=sb(f"r{ch}", [P, NT, D]), xa=sb(f"xa{ch}", [P, NT, D]),
                stats=sb(f"stats{ch}", [P, NT, 6]), mv=sb(f"mv{ch}", [P, NT, 2]),
                ve=sb(f"ve{ch}", [P, NT]), rs=sb(f"rs{ch}", [P, NT]),
                th=xh if ch == "X" else hsh, tl=xl if ch == "X" else hsl,
                h32=sb(f"h32{ch}", [P, 2, S]), hh=wide_h, hl=wide_l)
        gl32 = F["Y"]["h32"]
        vx, rx2, vy, hsc, twice = (sb(n, [P, NT]) for n in ("vx", "rx2", "vy", "hsc", "twice"))
        hat = F["X"]["xa"]
        yout = sb("yout", [P, NT, D])

        w_in = [sem("w_in_wide"), sem("w_in_narrow"), sem("w_in_c")]
        rows_in = sem("rows_in")
        w_hi, w_lo, w_lo_pool = sem("w_hi"), sem("w_lo"), sem("w_lo_pool")
        consts, masks, aneg_done, normws_done, zp_done = (
            sem(n) for n in ("consts", "masks", "aneg_done", "normws_done", "zp_done"))
        rest_done, exact_summed, exact_done = sem("rest_done"), sem("exact_summed"), sem("exact_done")
        xt_in, xn_in, stored = sem("xt_in"), sem("xn_in"), sem("stored")
        xh_done, xl_done, k_done, kv_done, cum_done, vh_done, vhh_done, vhl_done = (
            sem(n) for n in ("xh_done", "xl_done", "k_done", "kv_done", "cum_done", "vh_done", "vhh_done", "vhl_done"))
        C = {ch: {n: sem(f"{n}_{ch}") for n in (
            "part", "r", "stats", "mv", "ve", "rs", "xa", "th", "tl", "sg", "h", "hh", "hl", "mixh", "mixl")}
            for ch in "XY"}
        (rx2_done, vx_done, vxe_done, vy_done, hsc_done, twice_done, hat_done, x2_done, x2b_done, hs_done, hsh_done,
         hsl_done, bT_done, cT_done, xbn_done, dtz_done, z_done, absz_done, e_done, u_done, l_done, dt_step, dt_done,
         dta_done, a_done, ah_done, al_done, decs_done, Rh_done, Rl_done, E_done, mask_done, W_done, xdt_done,
         xw_done, st_step, st_done, dx_done, yi_done, yb_done, y_done, yg_done, ss_done, rms_step, rms_done,
         ygh_done, ygl_done, gl_done, glh_done, gll_done, m_done, yout_done) = (sem(n) for n in (
             "rx2_done vx_done vxe_done vy_done hsc_done twice_done hat_done x2_done x2b_done hs_done hsh_done "
             "hsl_done bT_done cT_done xbn_done dtz_done z_done absz_done e_done u_done l_done dt_step dt_done "
             "dta_done a_done ah_done al_done decs_done Rh_done Rl_done E_done mask_done W_done xdt_done "
             "xw_done st_step st_done dx_done yi_done yb_done y_done yg_done ss_done rms_step rms_done "
             "ygh_done ygl_done gl_done glh_done gll_done m_done yout_done").split())

        RN = {"X": NT, "Y": NT}

        release = {"X": {}, "Y": {}}
        for m in range(KD):
            release["X"].update({f"k{m}": (k_done, KD, m + 1), f"v{m}": (kv_done, KD, m + 1),
                                 f"q{m}": (vh_done, KD, m + 1), f"tr{m}": (C["X"]["tl"], KD, m + 1),
                                 f"hs{m}": (hs_done, KD, m + 1)})
            release["Y"][f"tq{m}"] = (C["Y"]["tl"], KD, m + 1)
        for ch in "XY":
            for t in range(2 * NPAIR):
                release[ch][f"up{t}"] = (C[ch]["h" if t % 2 else "sg"], NPAIR + 1, t // 2 + 1)
            release[ch][f"up{2 * NPAIR}"] = (C[ch]["h"], NPAIR + 1, NPAIR + 1)
            for i in range(NT // 2):
                release[ch][f"dn{i}"] = (C[ch]["part"], NT // 2, i + 1)
                release[ch][f"o{i}"] = (C[ch]["r"], RN[ch], i + 1)
        release["Y"].update(bt=(bT_done, 1, 1), cum=(decs_done, 1, 1))
        for j in range(GH):
            release["Y"][f"ct{j}"] = (cT_done, GH, j + 1)
        for i in range(NT // 2):
            release["Y"][f"m{i}"] = (m_done, NT // 2, i + 1)
        for t in range(KF):
            release["Y"][f"f{t}"] = (gl_done, KF, t + 1)
        for c in range(NT):
            release["Y"].update({f"sm{c}": (dtz_done, NT, c + 1), f"z{c}": (z_done, NT, c + 1),
                                 f"ds{c}": (st_done, NT - 1, c + 1), f"yi{c}": (yi_done, NT, c + 1),
                                 f"yx{c}": (y_done, NT - 1, c), f"ty{c}": (ygl_done, NT, c + 1)})
            for g in range(NG):
                release["Y"][f"seg{c}_{g}"] = (E_done, NT * NG, c * NG + g + 1)
                release["Y"][f"g{c}_{g}"] = (W_done, NT * NG, c * NG + g + 1)

        def low_ready(eng, name):
            if name in POOL_LOWS:
                eng.wait_ge(w_lo_pool, POOL_LOWS.index(name) + 1)
            else:
                eng.wait_ge(w_lo, DVE_LOWS.index(name) + 1)

        def wait_before(eng, signal, b, per, k):
            if not isinstance(b, int) or b:
                eng.wait_ge(signal, at(b, per, k - per))

        def filled(eng, ch, name, b):
            k, n = uses(ch, b)[name]
            value = at(b, COUNTS[ch][k], n + 1)
            if name in QKV_USES:
                value = at(b, XN[k], n + 1 - XN[k])
                if isinstance(b, int) and b == 0:
                    value = 1 + [u for u in QKV_USES if XU[u][0] == k].index(name)
            if ch == "X" and not (name in QKV_USES and isinstance(b, int) and b == 0):
                value = value + QKV_COUNT[k]
                if isinstance(b, int) and b == NB - 1 and name.startswith("hs"):
                    value -= QKV_COUNT[k]
            eng.wait_ge(full[k], value)
            return bank[k]

        def use(ch, name, b):
            return uses(ch, b)[name][0]

        def per_engine(eng, phases):
            def turn(bw, bx, by, bz, sched=SCHED):
                for step in sched:
                    ch, kind, *arg = step
                    b = {"W": bw, "X": bx, "Y": by, "Z": bz}[ch]
                    if b is not None and (ch, kind) in phases:
                        phases[ch, kind](b, *arg)
                    if isinstance(bx, int) and bx == 0:
                        if "weight" in phases and step in phases["weights at"]:
                            phases["weight"](phases["weights at"][step])
                        if "rest" in phases and step in EXACT_TURN:
                            phases["rest"](EXACT_TURN[step])

            def turns():
                turn(2, 1, 0, None)
                with eng.Fori(2, NB - 1) as i:
                    turn(i + 1, i, i - 1, i - 2)
                turn(None, NB - 1, NB - 2, NB - 3, LAST_X)
                turn(None, None, NB - 1, NB - 2, LAST_Y)
                turn(None, None, None, NB - 1)

            for step in SCHED:
                if step[0] == "W" and step[:2] in phases:
                    phases[step[:2]](0, *step[2:])
                if step == ("W", "vh", 1) and "weight" in phases and eng is not nc.gpsimd:
                    phases["weight"]("up0")
            turn(1, 0, None, None, FIRST)
            if "both ways" in phases:
                phases["both ways"](turns)
            else:
                turns()

        block = ctx.enter_context(nc.Block())

        @block.sync
        def _(sp):
            def load_xt(b):
                wait_before(sp, xl_done, b, 1, 1)
                sp.dma_start(xt[:], ins["xt"][bass.ds(b, 1)].rearrange("o (k p) s -> (o p) k s", p=P)).then_inc(
                    xt_in, 16)

            def load_xn(b):
                wait_before(sp, C["X"]["r"], b, RN["X"], NT // 2)
                sp.dma_start(xn[:], ins["x"][bass.ds(b, 1)].rearrange("o (i p) d -> (o p) i d", p=P)).then_inc(
                    xn_in, 16)

            def load_x(b):
                load_xt(b)
                load_xn(b)

            def store(b):
                sp.wait_ge(yout_done, b + 1)
                sp.dma_start(out[bass.ds(b, 1)].rearrange("o (i p) d -> (o p) i d", p=P), yout[:]).then_inc(stored, 16)

            for n in LOADS:
                _, k, c, integer, _ = WEIGHTS[WIDX[n]]
                before = STAGES[STAGE_OF[n]][:STAGES[STAGE_OF[n]].index(n)]
                if before:
                    low_ready(sp, before[-1])
                dst = stage(n, k, c)
                sp.dma_start(dst.bitcast(I32) if integer else dst, ins[n]).then_inc(w_in[STAGE_OF[n]], 16)
                if n == "wqkv":
                    load_xt(0)
                if n == "wo":
                    load_xn(0)
                if n == "up0":
                    sp.dma_start(cols[:], ins["cols"]).then_inc(rows_in, 16)
                    sp.dma_start(rows[:], ins["rows"].partition_broadcast(P)).then_inc(rows_in, 16)
                if n == "wout":
                    load_x(1)
            load_x(2)
            with sp.Fori(3, NB) as b:
                load_x(b)
                store(b - 3)
            for b in range(NB - 3, NB):
                store(b)
            sp.wait_ge(stored, 16 * NB + 1)

        @block.tensor
        def _(pe):
            def fill(ch, name, b):
                k, n = uses(ch, b)[name]
                of_bank = lambda all_: [u for u, (bank_, _) in all_.items() if bank_ == k]
                names, names_before = of_bank(uses(ch, b)), of_bank(uses(ch, None))
                ahead = lambda u: int(ch == "X" and u in QKV_USES)
                for back in range(1, len(names) + 1):
                    before = names[n - back] if back <= n else names_before[n - back]
                    batch = b - ahead(name) + ahead(before) - (back > n)
                    turn_ = b - ahead(name) - (back > n)
                    if not isinstance(b, int) or (0 <= batch < NB and (turn_ >= 0 or turn_ == -1 and ahead(before))):
                        signal, per, which = release[ch][before]
                        pe.wait_ge(signal, at(batch, per, which))
                        break
                return bank[k]

            skipped = set()

            def three(dst, lh, ll, rh, rl, first=True, last=True, shared=False):
                passes = [(lh, rh)] + ([(lh, rl)] if rl is not None else []) + ([(ll, rh)] if ll is not None else [])
                for n, (a, c) in enumerate(passes):
                    end = nc.tensor.matmul(dst, a, c, start=first and n == 0, stop=last and n == len(passes) - 1,
                                           skip_group_check=shared)
                return end

            def hidden_ready(ch, b, k):
                if k < NPAIR:
                    pe.wait_ge(C[ch]["hl"], at(b, NPAIR, k + 1))
                else:
                    pe.wait_ge(C[ch]["mixl"], at(b, 1, 1))

            def low_part(w, *where):
                return None if w in skipped else lo[w][where]

            def product(dst, lh, ll, rh, rl, tiles, ready=None):
                for n, k in enumerate(tiles):
                    if ready:
                        ready(k)
                    last = three(dst, lh(k), ll(k), rh(k), rl(k), n == 0, n == len(tiles) - 1)
                return last

            def chan_tile(dst, w, c0, act_h, act_l, m=P, ready=None):
                return product(dst, lambda k: hi[w][:, k, c0:c0 + m],
                               lambda k: low_part(w, slice(0, P), k, slice(c0, c0 + m)),
                               lambda k: act_h[:, k, :], lambda k: act_l[:, k, :], range(KD), ready)

            def tok_tile(dst, i, act_h, act_l, w, c0, n, tiles):
                return product(dst, lambda k: act_h[:, k, i * P:(i + 1) * P], lambda k: act_l[:, k, i * P:(i + 1) * P],
                               lambda k: hi[w][:, k, c0:c0 + n],
                               lambda k: low_part(w, slice(0, P), k, slice(c0, c0 + n)), tiles)

            def transposes(ch, b, names, src):
                for m in range(KD):
                    dst = fill(ch, names[m], b)
                    for i in range(NT):
                        last = nc.tensor.transpose(dst[:, i * P:(i + 1) * P], src[:, i, m * P:(m + 1) * P], ident[:])
                    last.then_inc(full[use(ch, names[m], b)], 1)

            def qkv(b, m):
                pe.wait_ge(xl_done, at(b, 1, 1))
                for w, c0 in (("k", D), ("v", 2 * D), ("q", 0)):
                    dst = fill("X", f"{w}{m}", b)
                    chan_tile(dst[:], "wqkv", c0 + m * P, xh, xl).then_inc(full[use("X", f"{w}{m}", b)], 1)

            def two_rows(dst, pair, a_h, a_l, w, k, end):
                for j in range(2):
                    tok_part = slice((2 * pair + j) * P, (2 * pair + j + 1) * P)
                    d, first = dst[:, j * D:(j + 1) * D], k == 0 and j == 0
                    if w in ("dn0", "dn1") and k == NPAIR:
                        rl = low_part(w, slice(HALF, P), k, slice(0, D))
                        last = nc.tensor.matmul(d, a_h[:, k, tok_part], hi[w][:, k, :], start=first,
                                                stop=end and rl is None, skip_group_check=True)
                        if rl is not None:
                            last = nc.tensor.matmul(d, a_h[HALF:P, k, tok_part], rl, start=False, stop=end,
                                                    skip_group_check=True)
                    else:
                        last = three(d, a_h[:, k, tok_part], a_l[:, k, tok_part], hi[w][:, k, :],
                                     low_part(w, slice(0, P), k, slice(0, D)), first, end, True)
                return last

            def rows_of_two(dst, pair, a_h, a_l, w, tiles, ready):
                for k in range(tiles):
                    ready(k)
                    last = two_rows(dst, pair, a_h, a_l, w, k, k == tiles - 1)
                return last

            def attn_out(b, i):
                if isinstance(b, int) and b == 0:
                    low_ready(pe, "wo")
                dst = fill("X", f"o{i}", b)
                rows_of_two(dst, i, vhh, vhl, "wo", KD, lambda k: pe.wait_ge(vhl_done, at(b, KD, k + 1))
                            ).then_inc(full[use("X", f"o{i}", b)], 1)

            def x_tr(b):
                pe.wait_ge(C["X"]["xa"], at(b, 1, 1))
                transposes("X", b, ["tr0", "tr1"], F["X"]["xa"])

            def up(ch, w):
                def go(b, a, e):
                    if isinstance(b, int) and b == 0:
                        low_ready(pe, w)
                    for t in range(a, e):
                        dst = fill(ch, f"up{t}", b)
                        chan_tile(dst[:], w, t * P, F[ch]["th"], F[ch]["tl"],
                                  ready=(lambda k: pe.wait_ge(C[ch]["tl"], at(b, KD, k + 1))) if t == 0 else None
                                  ).then_inc(full[use(ch, f"up{t}", b)], 1)
                return go

            def down(ch, w, b, i):
                if isinstance(b, int) and b == 0:
                    low_ready(pe, w)
                dst = fill(ch, f"dn{i}", b)
                rows_of_two(dst, i, F[ch]["hh"], F[ch]["hl"], w, NPAIR + 1,
                            lambda k: hidden_ready(ch, b, k)).then_inc(
                    full[use(ch, f"dn{i}", b)], 1)

            def x_down(b):
                for i in range(NT // 2):
                    down("X", "dn0", b, i)

            def z_down(b):
                if isinstance(b, int) and b == 0:
                    low_ready(pe, "dn1")
                f = F["Y"]
                dst = [fill("Y", f"dn{i}", b) for i in range(NT // 2)]
                for k in range(NPAIR + 1):
                    hidden_ready("Y", b, k)
                    for i in range(NT // 2):
                        last = two_rows(dst[i], i, f["hh"], f["hl"], "dn1", k, k == NPAIR)
                        if k == NPAIR:
                            last.then_inc(full[use("Y", f"dn{i}", b)], 1)

            def x_tr2(b):
                pe.wait_ge(hat_done, at(b, 1, 1))
                transposes("X", b, ["hs0", "hs1"], hat)

            def proj(b):
                for i in range(NT):
                    dst = fill("Y", f"sm{i}", b)
                    tok_tile(dst[:, 0:NSMALL], i, hsh, hsl, "win", CX, NSMALL, range(KD)).then_inc(
                        full[use("Y", f"sm{i}", b)], 1)
                dst = fill("Y", "bt", b)
                chan_tile(dst[:], "win", CX + DXB, hsh, hsl).then_inc(full[use("Y", "bt", b)], 1)
                for j in range(GH):
                    dst = fill("Y", f"ct{j}", b)
                    chan_tile(dst[:], "win", CC + j * P, hsh, hsl).then_inc(full[use("Y", f"ct{j}", b)], 1)

            def decays(b):
                dst = fill("Y", "cum", b)
                pe.wait_ge(a_done, at(b, 1, 1))
                av = aexp[:].rearrange("p c h -> p (c h)")
                nc.tensor.matmul(dst[:, 0:NT * NH], upto[:], av, start=True, stop=True)
                nc.tensor.matmul(dst[:, NT * NH:2 * NT * NH], allone[:], av, start=True, stop=True)
                nc.tensor.matmul(dst[:, 2 * NT * NH:3 * NT * NH], after[:], av, start=True, stop=True).then_inc(
                    full[use("Y", "cum", b)], 1)

            def gate(b):
                if isinstance(b, int) and b == 0:
                    low_ready(pe, "win")
                pe.wait_ge(hsl_done, at(b, KD, KD))
                for i in range(NT):
                    dst = fill("Y", f"z{i}", b)
                    tok_tile(dst[:], i, hsh, hsl, "win", CZ, DI, range(KD)).then_inc(full[use("Y", f"z{i}", b)], 1)

            def seg(b, c):
                for g in range(NG):
                    dst = fill("Y", f"seg{c}_{g}", b)
                    group = slice(g * GH, (g + 1) * GH)
                    pe.wait_ge(Rh_done, at(b, NT * NG, c * NG + g + 1))
                    nc.tensor.matmul(dst[:], after16[:], Rh[c % 2][:, group, :], start=True, stop=False)
                    pe.wait_ge(Rl_done, at(b, NT * NG, c * NG + g + 1))
                    nc.tensor.matmul(dst[:], after16[:], Rl[c % 2][:, group, :], start=False, stop=True).then_inc(
                        full[use("Y", f"seg{c}_{g}", b)], 1)

            def pairs(b, c):
                tok_part = slice(c * P, (c + 1) * P)
                for g in range(NG):
                    dst = fill("Y", f"g{c}_{g}", b)
                    if g == 0:
                        pe.wait_ge(cT_done, at(b, GH, GH))
                        pe.wait_ge(bT_done, at(b, 1, 1))
                    part = slice(g * HD, (g + 1) * HD)
                    nc.tensor.matmul(dst[:], bT[part, tok_part], cT[part, :, tok_part], start=True, stop=True).then_inc(
                        full[use("Y", f"g{c}_{g}", b)], 1)

            def chunk(b, c):
                tok_part = slice(c * P, (c + 1) * P)
                dst = fill("Y", f"yi{c}", b)
                pe.wait_ge(xdt_done, at(b, NT, c + 1))
                pe.wait_ge(W_done, at(b, NT * NG, (c + 1) * NG))
                for h in range(NH):
                    last = nc.tensor.matmul(dst[:, h * HD:(h + 1) * HD], E[:, c, h, :], xdt[:, c % 2, h, :],
                                            start=True, stop=True)
                last.then_inc(full[use("Y", f"yi{c}", b)], 1)
                if c:
                    dst = fill("Y", f"yx{c}", b)
                    pe.wait_ge(st_done, at(b, NT - 1, c))
                    d4 = dst[:].rearrange("p (g j d) -> p g j d", g=NG, j=GH)
                    for j in range(GH):
                        last = nc.tensor.matmul(d4[:, :, j, :], cT[:, j, tok_part], st[:, :, j, :],
                                                start=True, stop=True)
                    last.then_inc(full[use("Y", f"yx{c}", b)], 1)
                if c < NT - 1:
                    dst = fill("Y", f"ds{c}", b)
                    pe.wait_ge(xw_done, at(b, NT - 1, c + 1))
                    pe.wait_ge(xbn_done, at(b, NT, c + 1))
                    nc.tensor.matmul(dst[:], xbn[:, c, DXB:2 * DXB], xw[:].rearrange("p h d -> p (h d)"),
                                     start=True, stop=True).then_inc(full[use("Y", f"ds{c}", b)], 1)

            def turned(b, c):
                dst = fill("Y", f"ty{c}", b)
                pe.wait_ge(yg_done, at(b, NT, c + 1))
                for k in range(KI):
                    last = nc.tensor.transpose(dst[:, k * P:(k + 1) * P], yy[:, c % 2, k * P:(k + 1) * P], ident[:])
                last.then_inc(full[use("Y", f"ty{c}", b)], 1)

            def fc1(b):
                if isinstance(b, int) and b == 0:
                    low_ready(pe, "fc1")
                for t in range(KF):
                    dst = fill("Y", f"f{t}", b)
                    chan_tile(dst[:], "fc1", t * P, hsh, hsl).then_inc(full[use("Y", f"f{t}", b)], 1)

            def fc2(b, i):
                if isinstance(b, int) and b == 0:
                    low_ready(pe, "fc2")
                dst = fill("Y", f"m{i}", b)
                rows_of_two(dst, i, glh, gll, "fc2", KF, lambda k: pe.wait_ge(gll_done, at(b, KF, k + 1))
                            ).then_inc(full[use("Y", f"m{i}", b)], 1)

            def y_out(b):
                if isinstance(b, int) and b == 0:
                    low_ready(pe, "wout")
                for i in range(NT):
                    dst = fill("Y", f"o{i // 2}", b) if i % 2 == 0 else dst
                    pe.wait_ge(ygl_done, at(b, NT, i + 1))
                    last = tok_tile(dst[:, i % 2 * D:(i % 2 + 1) * D], i, ygh, ygl, "wout", 0, D, range(KI))
                    if i % 2:
                        last.then_inc(full[use("Y", f"o{i // 2}", b)], 1)

            def y_tr(b):
                pe.wait_ge(C["Y"]["xa"], at(b, 1, 1))
                transposes("Y", b, ["tq0", "tq1"], F["Y"]["xa"])

            def rest_sum(name):
                if name is not None:
                    return
                pe.wait_ge(rest_done, len(EXACT))
                for n in range(len(EXACT)):
                    last = nc.tensor.matmul(bank[4][:, 0:1], allone[:], rest[:, n:n + 1], start=n == 0,
                                            stop=n == len(EXACT) - 1)
                last.then_inc(exact_summed, 1)

            def both_ways(turns):
                pe.wait_ge(exact_done, 1)
                yes = pe.value_load(all_exact[:], min_val=0, max_val=1)
                with pe.If(yes):
                    skipped.update(EXACT)
                    turns()
                    skipped.clear()
                with pe.Else():
                    turns()

            pe.wait_ge(masks, 5)
            low_ready(pe, "wqkv")
            per_engine(pe, {
                "rest": rest_sum, "both ways": both_ways,
                ("W", "qkv"): qkv, ("X", "out"): attn_out, ("X", "tr"): x_tr, ("X", "up"): up("X", "up0"),
                ("X", "down"): x_down, ("X", "tr2"): x_tr2, ("Y", "proj"): proj, ("Y", "gate"): gate,
                ("Y", "decays"): decays, ("Y", "seg"): seg, ("Y", "pairs"): pairs, ("Y", "chunk"): chunk,
                ("Y", "turned"): turned, ("Y", "fc1"): fc1, ("Y", "fc2"): fc2, ("Y", "out"): y_out,
                ("Y", "tr"): y_tr, ("Y", "up"): up("Y", "up1"), ("Z", "down"): z_down})

        @block.scalar
        def _(act):
            def weight(name):
                i = WIDX[name]
                n, k, c, integer, scale = WEIGHTS[i]
                act.wait_ge(w_in[STAGE_OF[n]], 16 * (STAGES[STAGE_OF[n]].index(n) + 1))
                src, dst = stage(n, k, c), hi[n][:].rearrange("p k c -> p (k c)")
                if n == "wout":
                    act.wait_ge(normws_done, 1)
                    for kk in range(KI):
                        last = nc.scalar.activation(hi[n][:, kk, :], src[:, kk * c:(kk + 1) * c], ACT.Copy,
                                                    scale=normws[:, kk:kk + 1])
                elif integer:
                    act.wait_ge(zp_done, 1)
                    last = nc.scalar.activation(dst, src.bitcast(I32), ACT.Identity, bias=zero_point[:], scale=scale)
                else:
                    last = nc.scalar.activation(dst, src, ACT.Copy, scale=scale)
                last.then_inc(w_hi, 1)

            def rest_of(name):
                if name is None:
                    return
                n = EXACT.index(name)
                low_ready(act, name)
                if n:
                    act.wait_ge(rest_done, n)
                flat = lo[name][:].rearrange("p k c -> p (k c)")
                scratch = zs[:].rearrange("p c d -> p (c d)").bitcast(F16)[:, 0:flat.shape[-1]]
                nc.scalar.activation(scratch, flat, ACT.Square, accum_out=rest[:, n:n + 1]).then_inc(rest_done, 1)

            def split(b):
                act.wait_ge(xt_in, at(b, 16, 16))
                nc.scalar.copy(xh[:], xt[:]).then_inc(xh_done, 1)

            def later_split(b):
                if not (isinstance(b, int) and b == 0):
                    split(b)

            def qkv(b, m):
                src = filled(act, "X", f"k{m}", b)
                nc.scalar.activation(ksb[:, m, :], src[:], ACT.Copy, scale=WS ** -2).then_inc(k_done, 1)

            def vh(b, m):
                act.wait_ge(vh_done, at(b, KD, m + 1))
                nc.scalar.copy(vhh[:, m, :], vh32[:, m, :]).then_inc(vhh_done, 1)

            def split_tr(ch, names):
                def go(b):
                    for m in range(KD):
                        src = filled(act, ch, names[m], b)
                        nc.scalar.copy(F[ch]["th"][:, m, :], src[:]).then_inc(C[ch]["th"], 1)
                return go

            def up(ch, scales):
                def go(b, a, e):
                    f = F[ch]
                    for t in range(a, e):
                        pair = t // 2
                        if t % 2 == 0:
                            src = filled(act, ch, f"up{t}", b)
                            if pair >= 2:
                                act.wait_ge(C[ch]["h"], at(b, NPAIR + 1, pair - 1))
                            if t < 2 * NPAIR:
                                nc.scalar.activation(sg[:, pair % 2, :], src[:], ACT.Silu,
                                                     scale=col[scales][:, t:t + 1]).then_inc(C[ch]["sg"], 1)
                            else:
                                nc.scalar.activation(sg[HALF:P, pair % 2, :], src[0:HALF, :], ACT.Silu,
                                                     scale=col[scales][0:HALF, t:t + 1]).then_inc(C[ch]["sg"], 1)
                        if t % 2 == 0 and pair:
                            act.wait_ge(C[ch]["h"], at(b, NPAIR + 1, pair))
                            nc.scalar.copy(f["hh"][:, pair - 1, :], f["h32"][:, (pair - 1) % 2, :]).then_inc(
                                C[ch]["hh"], 1)
                return go

            def x_tr2(b):
                if isinstance(b, int) and b == 0:
                    low_ready(act, "dn1")
                for m in range(KD):
                    src = filled(act, "X", f"hs{m}", b)
                    nc.scalar.activation(hs32[:, m, :], src[:], ACT.Identity, bias=col["lnb"][:, m:m + 1],
                                         scale=col["lnw"][:, m:m + 1]).then_inc(hs_done, 1)

            def proj(b):
                for i in range(NT):
                    src = filled(act, "Y", f"sm{i}", b)
                    nc.scalar.activation(xbn[:, i, :], src[:, 0:2 * DXB], ACT.Copy, scale=1 / WS).then_inc(xbn_done, 1)
                act.preload_act_table_set("natural_log_exp_and_others")
                src = filled(act, "Y", "bt", b)
                nc.scalar.activation(bT[:], src[:], ACT.Copy, scale=1 / WS).then_inc(bT_done, 1)
                for j in range(GH):
                    if j == 0:
                        act.wait_ge(absz_done, at(b, 1, 1))
                        nc.scalar.activation(dte[:], dta[:], ACT.Exp, scale=-1.0).then_inc(e_done, 1)
                    if j == 1:
                        act.wait_ge(u_done, at(b, 1, 1))
                        nc.scalar.activation(dtl[:], dtu[:], ACT.Ln).then_inc(l_done, 1)
                    src = filled(act, "Y", f"ct{j}", b)
                    nc.scalar.activation(cT[:, j, :], src[:], ACT.Copy, scale=1 / WS).then_inc(cT_done, 1)

            def decays(b):
                src = filled(act, "Y", "cum", b)
                nc.scalar.activation(decs[:].rearrange("p w c h -> p (w c h)"), src[:, 0:3 * NT * NH],
                                     ACT.Exp).then_inc(decs_done, 1)

            def gate(b):
                for i in range(NT):
                    src = filled(act, "Y", f"z{i}", b)
                    nc.scalar.activation(zs[:, i, :], src[:], ACT.Silu, scale=1 / WS).then_inc(z_done, 1)

            def seg(b, c):
                for g in range(NG):
                    src = filled(act, "Y", f"seg{c}_{g}", b)
                    nc.scalar.activation(E[:, c, g * GH:(g + 1) * GH, :].rearrange("p h t -> p (h t)"), src[:],
                                         ACT.Exp).then_inc(E_done, 1)

            def turned(b, c):
                act.wait_ge(yg_done, at(b, NT, c + 1))
                if c:
                    act.wait_ge(ss_done, at(b, NT, c))
                nc.scalar.activation(sq[:], yy[:, c % 2, :], ACT.Square, accum_out=ss[:, c:c + 1]).then_inc(ss_done, 1)
                src = filled(act, "Y", f"ty{c}", b)
                nc.scalar.copy(ygh[:, :, c * P:(c + 1) * P], src[:].rearrange("p (k t) -> p k t", k=KI)).then_inc(
                    ygh_done, 1)

            def fc1(b):
                for t in range(KF):
                    src = filled(act, "Y", f"f{t}", b)
                    if t >= 2:
                        act.wait_ge(gll_done, at(b, KF, t - 1))
                    nc.scalar.activation(gl32[:, t % 2, :], src[:], ACT.Gelu_apprx_tanh, bias=col["fc1b"][:, t:t + 1],
                                         scale=1 / WS).then_inc(gl_done, 1)

            weight("wqkv")
            split(0)
            weight("wo")
            act.wait_ge(rows_in, 16 * 2)
            nc.scalar.activation(aneg[:], row["alog"][:], ACT.Exp).then_inc(aneg_done, 1)
            per_engine(act, {
                "weight": weight, "weights at": HIGH_TURN, "rest": rest_of, ("W", "split"): later_split,
                ("W", "qkv"): qkv, ("W", "vh"): vh, ("X", "tr"): split_tr("X", ["tr0", "tr1"]),
                ("X", "up"): up("X", "sup0"), ("X", "tr2"): x_tr2, ("Y", "proj"): proj, ("Y", "gate"): gate,
                ("Y", "decays"): decays,
                ("Y", "seg"): seg, ("Y", "turned"): turned, ("Y", "fc1"): fc1,
                ("Y", "tr"): split_tr("Y", ["tq0", "tq1"]), ("Y", "up"): up("Y", "sup1")})

        @block.vector
        def _(dve):
            v = nc.vector
            v.memset(zero_point[:], -ZERO_POINT).then_inc(zp_done, 1)
            v.memset(allone[:], 1.0).then_inc(consts, 1)
            v.memset(yout[:], 0.0).then_inc(stored, 1)
            v.memset(st[:], 0.0).then_inc(consts, 1)
            for tile, value in ((half, -0.5), (eps, EPS), (ws2_di, WS ** 2 / DI), (ws2_eps, WS ** 2 * EPS)):
                v.memset(tile[:], value).then_inc(consts, 1)

            def weight(name):
                i = WIDX[name]
                n, k, c, integer, scale = WEIGHTS[i]
                src, high, low_ = stage(n, k, c), hi[n], lo[n]
                dve.wait_ge(w_hi, i + 1)
                if n == "wout":
                    for kk in range(KI):
                        last = v.scalar_tensor_tensor(out=low_[:, kk, :], in0=src[:, kk * c:(kk + 1) * c],
                                                      scalar=normws[:, kk:kk + 1], in1=high[:, kk, :],
                                                      op0=ALU.mult, op1=ALU.subtract)
                else:
                    last = v.scalar_tensor_tensor(out=low_[:].rearrange("p k c -> p (k c)"),
                                                  in0=src.bitcast(I32) if integer else src,
                                                  scalar=-ZERO_POINT if integer else scale,
                                                  in1=high[:].rearrange("p k c -> p (k c)"),
                                                  op0=ALU.add if integer else ALU.mult, op1=ALU.subtract)
                last.then_inc(w_lo, 1)

            def low(out, src, high):
                return v.tensor_tensor(out, src, high, ALU.subtract)

            def norm_stats(ch, b, turn):
                f, c = F[ch], C[ch]
                dve.wait_ge(c["r"], at(b, RN[ch], NT // 2 * (turn + 1)))
                for i in range(NT):
                    v.bn_stats(f["stats"][:, i, :], f["r"][:, i, :]).then_inc(c["stats"], 1)
                dve.wait_ge(c["stats"], at(b, 2 * NT, (turn + 1) * NT))
                v.memset(spare[:], 0.0)
                for i in range(NT):
                    last = v.bn_aggr(f["mv"][:, i, :], f["stats"][:, i, :])
                last.then_inc(c["mv"], 1)

            def normed(ch, out, scale, done):
                f = F[ch]
                for i in range(NT):
                    last = v.tensor_scalar(out[:, i, :], f["r"][:, i, :], f["mv"][:, i, 0:1], scale[:, i:i + 1],
                                           ALU.subtract, ALU.mult)
                last.then_inc(done, 1)

            def split(b):
                dve.wait_ge(xh_done, at(b, 1, 1))
                low(xl[:], xt[:], xh[:]).then_inc(xl_done, 1)

            def later_split(b):
                if not (isinstance(b, int) and b == 0):
                    split(b)

            def vh(b, m):
                src = filled(dve, "X", f"v{m}", b)
                dve.wait_ge(k_done, at(b, KD, m + 1))
                if m:
                    dve.wait_ge(vh_done, at(b, KD, m))
                v.tensor_tensor(kv[:], ksb[:, m, :], src[:], ALU.mult).then_inc(kv_done, 1)
                dve.wait_ge(kv_done, at(b, KD, m + 1))
                v.tensor_tensor_scan(kv[:], allone[:, 0:1].to_broadcast([P, S]), kv[:], 0.0, ALU.mult,
                                     ALU.add).then_inc(cum_done, 1)
                src = filled(dve, "X", f"q{m}", b)
                dve.wait_ge(cum_done, at(b, KD, m + 1))
                v.scalar_tensor_tensor(out=vh32[:, m, :], in0=src[:], scalar=SSM_DENOM / WS, in1=kv[:],
                                       op0=ALU.mult, op1=ALU.mult).then_inc(vh_done, 1)

            def attn_out(b):
                f = F["X"]
                dve.wait_ge(xn_in, at(b, 16, 16))
                for i in range(NT // 2):
                    src = filled(dve, "X", f"o{i}", b)
                    pair = slice(2 * i, 2 * i + 2)
                    v.scalar_tensor_tensor(out=f["r"][:, pair, :].rearrange("p i d -> p (i d)"), in0=src[:],
                                           scalar=1 / WS, in1=xn[:, pair, :].rearrange("p i d -> p (i d)"),
                                           op0=ALU.mult, op1=ALU.add).then_inc(C["X"]["r"], 1)
                norm_stats("X", b, 0)
                dve.wait_ge(C["X"]["rs"], at(b, 2, 1))
                normed("X", f["xa"], f["rs"], C["X"]["xa"])

            def split_tr(ch, names):
                def go(b):
                    for m in range(KD):
                        dve.wait_ge(C[ch]["th"], at(b, KD, m + 1))
                        low(F[ch]["tl"][:, m, :], bank[use(ch, names[m], b)][:], F[ch]["th"][:, m, :]).then_inc(
                            C[ch]["tl"], 1)
                return go

            def up(ch, scales):
                def go(b, a, e):
                    f = F[ch]
                    for t in range(a, e):
                        if t % 2 == 0 and t < 2 * NPAIR:
                            continue
                        pair = t // 2
                        p0 = 0 if t < 2 * NPAIR else HALF
                        src = filled(dve, ch, f"up{t}", b)
                        dve.wait_ge(C[ch]["sg"], at(b, NPAIR + 1, pair + 1))
                        if pair >= 2:
                            dve.wait_ge(C[ch]["hl"], at(b, NPAIR, pair - 1))
                        v.scalar_tensor_tensor(out=f["h32"][p0:P, pair % 2, :], in0=src[p0:P, :],
                                               scalar=col[scales][p0:P, t:t + 1], in1=sg[p0:P, pair % 2, :],
                                               op0=ALU.mult, op1=ALU.mult).then_inc(C[ch]["h"], 1)
                        if p0:
                            h32 = f["h32"][HALF:P, pair % 2, :]
                            dve.wait_ge(C[ch]["h"], at(b, NPAIR + 1, NPAIR + 1))
                            v.tensor_copy(f["hh"][HALF:P, pair, :], h32).then_inc(C[ch]["mixh"], 1)
                            dve.wait_ge(C[ch]["mixh"], at(b, 1, 1))
                            low(f["hh"][0:HALF, pair, :], h32, f["hh"][HALF:P, pair, :]).then_inc(C[ch]["mixl"], 1)
                return go

            def down(ch, scale_row, b, i):
                f = F[ch]
                src = filled(dve, ch, f"dn{i}", b)
                r = f["r"][:, 2 * i:2 * i + 2, :]
                v.tensor_tensor(r, src[:].rearrange("p (i d) -> p i d", i=2),
                                row[scale_row][:].unsqueeze(1).to_broadcast([P, 2, D]), ALU.mult).then_inc(
                    C[ch]["part"], 1)
                dve.wait_ge(C[ch]["part"], at(b, NT // 2, i + 1))
                v.tensor_tensor(r, r, f["xa"][:, 2 * i:2 * i + 2, :], ALU.add).then_inc(C[ch]["r"], 1)


            def z_down(b):
                for i in range(NT // 2):
                    down("Y", "sdn1", b, i)
                norm_stats("Y", b, 1)
                dve.wait_ge(C["Y"]["rs"], at(b, 2, 2))
                dve.wait_ge(stored, at(b, 16, 1))
                normed("Y", yout, F["Y"]["rs"], yout_done)

            def x_sum(b, i):
                down("X", "sdn0", b, i)
                if i:
                    norm_stats("X", b, 1)

            def x_hat(b):
                dve.wait_ge(hsc_done, at(b, 1, 1))
                normed("X", hat, hsc, hat_done)

            def x_x2(b):
                dve.wait_ge(twice_done, at(b, 1, 1))
                normed("X", x2, twice, x2_done)

            def x_hs(b):
                for m in range(KD):
                    dve.wait_ge(hs_done, at(b, KD, m + 1))
                    v.tensor_copy(hsh[:, m, :], hs32[:, m, :]).then_inc(hsh_done, 1)
                    dve.wait_ge(hsh_done, at(b, KD, m + 1))
                    low(hsl[:, m, :], hs32[:, m, :], hsh[:, m, :]).then_inc(hsl_done, 1)

            def proj(b):
                for i in range(NT):
                    src = filled(dve, "Y", f"sm{i}", b)
                    dve.wait_ge(xbn_done, at(b, NT, i + 1))
                    v.scalar_tensor_tensor(out=dtz[:, i * NH:(i + 1) * NH], in0=src[:, 2 * DXB:NSMALL], scalar=1 / WS,
                                           in1=row["dtb"][:], op0=ALU.mult, op1=ALU.add).then_inc(dtz_done, 1)
                dve.wait_ge(dtz_done, at(b, NT, NT))
                v.scalar_tensor_tensor(out=dta[:], in0=dtz[:], scalar=-1.0, in1=dtz[:], op0=ALU.mult,
                                       op1=ALU.max).then_inc(absz_done, 1)
                dve.wait_ge(e_done, at(b, 1, 1))
                v.tensor_scalar(dtu[:], dte[:], 1.0, None, ALU.add).then_inc(u_done, 1)
                dve.wait_ge(u_done, at(b, 1, 1))
                v.tensor_scalar(dtd[:], dtu[:], -1.0, None, ALU.add).then_inc(dt_step, 1)
                dve.wait_ge(dt_step, at(b, 9, 1))
                v.tensor_scalar(dtq[:], dtd[:], -0.5, 1.0, ALU.mult, ALU.add).then_inc(dt_step, 1)
                dve.wait_ge(dt_step, at(b, 9, 2))
                v.tensor_tensor(dtq[:], dtq[:], dtd[:], ALU.mult).then_inc(dt_step, 1)
                dve.wait_ge(dt_step, at(b, 9, 3))
                dve.wait_ge(l_done, at(b, 1, 1))
                v.tensor_tensor(dtq[:], dtq[:], dtl[:], ALU.max).then_inc(dt_step, 1)
                dve.wait_ge(dt_step, at(b, 9, 4))
                v.tensor_tensor(dtq[:], dtq[:], dtd[:], ALU.min).then_inc(dt_step, 1)
                dve.wait_ge(dt_step, at(b, 9, 5))
                v.tensor_scalar(dtd[:], dtd[:], 1e-30, None, ALU.add).then_inc(dt_step, 1)
                dve.wait_ge(dt_step, at(b, 9, 6))
                v.reciprocal(dtd[:], dtd[:]).then_inc(dt_step, 1)
                dve.wait_ge(dt_step, at(b, 9, 7))
                v.scalar_tensor_tensor(out=dtq[:], in0=dtq[:], scalar=1e-30, in1=dtd[:], op0=ALU.add,
                                       op1=ALU.mult).then_inc(dt_step, 1)
                dve.wait_ge(dt_step, at(b, 9, 8))
                v.tensor_tensor(dtq[:], dtq[:], dte[:], ALU.mult).then_inc(dt_step, 1)
                dve.wait_ge(dt_step, at(b, 9, 9))
                v.scalar_tensor_tensor(out=dt[:].rearrange("p c h -> p (c h)"), in0=dtz[:], scalar=0.0, in1=dtq[:],
                                       op0=ALU.max, op1=ALU.add).then_inc(dt_done, 1)
                dve.wait_ge(dt_done, at(b, 1, 1))
                v.tensor_tensor(dta[:].rearrange("p (c h) -> p c h", c=NT), dt[:],
                                aneg[:].unsqueeze(1).to_broadcast([P, NT, NH]), ALU.mult).then_inc(dta_done, 1)
                dve.wait_ge(dta_done, at(b, 1, 1))
                v.tensor_scalar(aexp[:].rearrange("p c h -> p (c h)"), dta[:], DECAY_FLOOR, None, ALU.max).then_inc(
                    a_done, 1)
                dve.wait_ge(a_done, at(b, 1, 1))
                v.tensor_copy(ah[:], aexp[:]).then_inc(ah_done, 1)
                dve.wait_ge(ah_done, at(b, 1, 1))
                low(al[:], aexp[:], ah[:]).then_inc(al_done, 1)
                for c in range(2):
                    exponents(b, c)

            def seg(b, c):
                if c < NT - 2:
                    exponents(b, c + 2)

            def exponents(b, c):
                for n in range(NG):
                    group = slice(n * GH, (n + 1) * GH)
                    if c >= 2:
                        filled(dve, "Y", f"seg{c - 2}_{n}", b)
                    dve.wait_ge(al_done, at(b, 1, 1))
                    v.tensor_tensor(Rl[c % 2][:, group, :], al[:, c, group].unsqueeze(2).to_broadcast([P, GH, P]),
                                    upto16[:].unsqueeze(1).to_broadcast([P, GH, P]), ALU.mult).then_inc(Rl_done, 1)

            def mask(b, c):
                dve.wait_ge(E_done, at(b, NT * NG, (c + 1) * NG))
                v.tensor_tensor(E[:, c], E[:, c], upto[:].unsqueeze(1).to_broadcast([P, NH, P]), ALU.mult).then_inc(
                    mask_done, 1)

            def pairs(b, c):
                dve.wait_ge(mask_done, at(b, NT, c + 1))
                for g in range(NG):
                    src = filled(dve, "Y", f"g{c}_{g}", b)
                    w = E[:, c, g * GH:(g + 1) * GH, :].rearrange("p h t -> p (h t)")
                    v.tensor_tensor(w, src[:], w, ALU.mult).then_inc(W_done, 1)

            def chunk(b, c):
                y = yy[:, c % 2, :]
                src = filled(dve, "Y", f"yi{c}", b)
                dve.wait_ge(dx_done, at(b, NT, c + 1))
                v.tensor_tensor(y, src[:], y, ALU.add).then_inc(yi_done, 1)
                if c:
                    src = filled(dve, "Y", f"yx{c}", b)
                    s3 = src[:].rearrange("p (h d) -> p h d", h=NH)
                    v.tensor_tensor(s3, s3, decs[:, 0, c, :].unsqueeze(2).to_broadcast([P, NH, HD]),
                                    ALU.mult).then_inc(yb_done, 1)
                    dve.wait_ge(yb_done, at(b, NT - 1, c))
                    dve.wait_ge(yi_done, at(b, NT, c + 1))
                    v.tensor_tensor(y, src[:], y, ALU.add).then_inc(y_done, 1)
                if c < NT - 1:
                    dve.wait_ge(decs_done, at(b, 1, 1))
                    src = filled(dve, "Y", f"ds{c}", b)
                    for g in range(NG):
                        part = slice(g * HD, (g + 1) * HD)
                        own = src[part, g * GH * HD:(g + 1) * GH * HD].rearrange("p (j d) -> p j d", j=GH)
                        if c == 0:
                            last = v.tensor_copy(st[part, g, :, :], own)
                        else:
                            filled(dve, "Y", f"yx{c}", b)
                            dve.wait_ge(st_done, at(b, NT - 1, c))
                            over = decs[part, 1, c, g * GH:(g + 1) * GH].unsqueeze(2).to_broadcast([HD, GH, HD])
                            v.tensor_tensor(st[part, g, :, :], st[part, g, :, :], over, ALU.mult).then_inc(st_step, 1)
                            dve.wait_ge(st_step, at(b, (NT - 2) * NG, (c - 1) * NG + g + 1))
                            last = v.tensor_tensor(st[part, g, :, :], st[part, g, :, :], own, ALU.add)
                    last.then_inc(st_done, 1)

            def turned(b, c):
                dve.wait_ge(ygh_done, at(b, NT, c + 1))
                tok_part = slice(c * P, (c + 1) * P)
                low(ygl[:, :, tok_part], bank[use("Y", f"ty{c}", b)][:].rearrange("p (k t) -> p k t", k=KI),
                    ygh[:, :, tok_part]).then_inc(ygl_done, 1)

            def fc1(b):
                for t in range(KF):
                    dve.wait_ge(gl_done, at(b, KF, t + 1))
                    v.tensor_copy(glh[:, t, :], gl32[:, t % 2, :]).then_inc(glh_done, 1)

            def fc2(b, i):
                dve.wait_ge(x2b_done, at(b, 1, 1))
                src = filled(dve, "Y", f"m{i}", b)
                x2p = x2[:, 2 * i:2 * i + 2, :].rearrange("p i d -> p (i d)")
                v.scalar_tensor_tensor(out=x2p, in0=src[:], scalar=1 / WS, in1=x2p, op0=ALU.mult,
                                       op1=ALU.add).then_inc(m_done, 1)

            def y_out(b):
                f = F["Y"]
                dve.wait_ge(rms_done, at(b, 1, 1))
                dve.wait_ge(m_done, at(b, NT // 2, NT // 2))
                for i in range(NT):
                    src = filled(dve, "Y", f"o{i // 2}", b)
                    last = v.scalar_tensor_tensor(out=f["r"][:, i, :], in0=src[:, i % 2 * D:(i % 2 + 1) * D],
                                                  scalar=rms[:, i:i + 1], in1=x2[:, i, :], op0=ALU.mult, op1=ALU.add)
                    if i % 2:
                        last.then_inc(C["Y"]["r"], 1)
                norm_stats("Y", b, 0)

            def y_norm(b):
                f = F["Y"]
                dve.wait_ge(C["Y"]["rs"], at(b, 2, 1))
                normed("Y", f["xa"], f["rs"], C["Y"]["xa"])

            def exact(name):
                if name is None:
                    dve.wait_ge(exact_summed, 1)
                    v.tensor_scalar(all_exact[:], bank[4][0:1, 0:1], 0.0, None, ALU.is_equal).then_inc(exact_done, 1)

            weight("wqkv")
            split(0)
            weight("wo")
            dve.wait_ge(masks, 5)
            dve.wait_ge(rows_in, 16 * 2)
            v.tensor_scalar(normws[:], col["normw"][:], WS, None, ALU.mult).then_inc(normws_done, 1)
            dve.wait_ge(aneg_done, 1)
            v.tensor_scalar(aneg[:], aneg[:], -1.0, None, ALU.mult).then_inc(aneg_done, 1)
            per_engine(dve, {
                "rest": exact,
                "weight": weight, "weights at": LOW_TURN, ("W", "split"): later_split,
                ("W", "vh"): vh, ("X", "res"): attn_out, ("X", "tr"): split_tr("X", ["tr0", "tr1"]),
                ("X", "up"): up("X", "sup0"), ("X", "sum"): x_sum, ("X", "hat"): x_hat, ("X", "x2"): x_x2,
                ("X", "hs"): x_hs, ("Y", "proj"): proj, ("Y", "seg"): seg, ("Y", "mask"): mask,
                ("Y", "pairs"): pairs, ("Y", "chunk"): chunk, ("Y", "turned"): turned,
                ("Y", "fc1"): fc1, ("Y", "fc2"): fc2, ("Y", "out"): y_out, ("Y", "norm"): y_norm,
                ("Y", "tr"): split_tr("Y", ["tq0", "tq1"]),
                ("Y", "up"): up("Y", "sup1"), ("Z", "down"): z_down})

        @block.gpsimd
        def _(pool):
            g = nc.gpsimd
            for tile, value in ((ident, 0.0), (upto, 1.0), (after, 1.0), (upto16, 1.0), (after16, 1.0)):
                g.memset(tile[:], value).then_inc(consts, 1)
            pool.wait_ge(consts, 11)
            g.affine_select(out=ident[:], in_=ident[:], pattern=[[-1, P]], compare_op=ALU.not_equal, fill=1.0, base=0,
                            channel_multiplier=1).then_inc(masks, 1)
            for tile in (upto, upto16):
                g.affine_select(out=tile[:], in_=tile[:], pattern=[[1, P]], compare_op=ALU.is_ge, fill=0.0, base=0,
                                channel_multiplier=-1).then_inc(masks, 1)
            for tile in (after, after16):
                g.affine_select(out=tile[:], in_=tile[:], pattern=[[-1, P]], compare_op=ALU.is_gt, fill=0.0, base=0,
                                channel_multiplier=1).then_inc(masks, 1)
            pool.wait_ge(masks, 5)
            pool.wait_ge(rows_in, 16 * 2)

            def weight(name):
                n, k, c, _, _ = WEIGHTS[WIDX[name]]
                pool.wait_ge(w_hi, WIDX[name] + 1)
                g.tensor_tensor(lo[n][:].rearrange("p k c -> p (k c)"), stage(n, k, c),
                                hi[n][:].rearrange("p k c -> p (k c)"), ALU.subtract).then_inc(w_lo_pool, 1)

            def inv_root(ch, b, turn):
                f, c = F[ch], C[ch]
                pool.wait_ge(c["mv"], at(b, 2, turn + 1))
                g.tensor_tensor(f["ve"][:], f["mv"][:, :, 1], eps[:], ALU.add).then_inc(c["ve"], 1)
                pool.wait_ge(c["ve"], at(b, 2, turn + 1))
                g.tensor_tensor(f["rs"][:], f["ve"][:], half[:], ALU.pow).then_inc(c["rs"], 1)

            def vh(b, m):
                pool.wait_ge(vhh_done, at(b, KD, m + 1))
                g.tensor_tensor(vhl[:, m, :], vh32[:, m, :], vhh[:, m, :], ALU.subtract).then_inc(vhl_done, 1)

            def up(ch):
                def go(b, a, e):
                    f = F[ch]
                    for t in range(a, e):
                        if t % 2 or not t:
                            continue
                        pair = t // 2 - 1
                        pool.wait_ge(C[ch]["hh"], at(b, NPAIR, pair + 1))
                        g.tensor_tensor(f["hl"][:, pair, :], f["h32"][:, pair % 2, :], f["hh"][:, pair, :],
                                        ALU.subtract).then_inc(C[ch]["hl"], 1)
                return go

            def x_root(b):
                inv_root("X", b, 1)
                f = F["X"]
                pool.wait_ge(C["X"]["rs"], at(b, 2, 2))
                g.tensor_tensor(twice[:], f["rs"][:], f["rs"][:], ALU.add).then_inc(twice_done, 1)
                g.tensor_tensor(rx2[:], f["rs"][:], f["rs"][:], ALU.mult).then_inc(rx2_done, 1)
                pool.wait_ge(rx2_done, at(b, 1, 1))
                g.tensor_tensor(vx[:], f["mv"][:, :, 1], rx2[:], ALU.mult).then_inc(vx_done, 1)
                pool.wait_ge(vx_done, at(b, 1, 1))
                g.tensor_tensor(vx[:], vx[:], eps[:], ALU.add).then_inc(vxe_done, 1)
                pool.wait_ge(vxe_done, at(b, 1, 1))
                g.tensor_tensor(vy[:], vx[:], half[:], ALU.pow).then_inc(vy_done, 1)
                pool.wait_ge(vy_done, at(b, 1, 1))
                g.tensor_tensor(hsc[:], f["rs"][:], vy[:], ALU.mult).then_inc(hsc_done, 1)

            def x_x2(b):
                pool.wait_ge(x2_done, at(b, 1, 1))
                g.tensor_tensor(x2[:], x2[:], row["fc2b"][:].unsqueeze(1).to_broadcast([P, NT, D]), ALU.add).then_inc(
                    x2b_done, 1)

            def proj(b):
                for c in range(2):
                    exponents(b, c)

            def seg(b, c):
                if c < NT - 2:
                    exponents(b, c + 2)

            def exponents(b, c):
                for n in range(NG):
                    group = slice(n * GH, (n + 1) * GH)
                    if c >= 2:
                        filled(pool, "Y", f"seg{c - 2}_{n}", b)
                    pool.wait_ge(ah_done, at(b, 1, 1))
                    g.tensor_tensor(Rh[c % 2][:, group, :], ah[:, c, group].unsqueeze(2).to_broadcast([P, GH, P]),
                                    upto16[:].unsqueeze(1).to_broadcast([P, GH, P]), ALU.mult).then_inc(Rh_done, 1)

            def pairs(b, c):
                x3 = xbn[:, c, 0:DXB].rearrange("p (g o d) -> p g o d", g=NG, o=1).to_broadcast([P, NG, GH, HD])
                if c == 0:
                    pool.wait_ge(xbn_done, at(b, NT, NT))
                    pool.wait_ge(dt_done, at(b, 1, 1))
                if c >= 2:
                    filled(pool, "Y", f"yi{c - 2}", b)
                    pool.wait_ge(xw_done, at(b, NT - 1, c - 1))
                g.tensor_tensor(xdt[:, c % 2].rearrange("p (g j) d -> p g j d", g=NG), x3,
                                dt[:, c, :].rearrange("p (g j o) -> p g j o", g=NG, o=1).to_broadcast([P, NG, GH, HD]),
                                ALU.mult).then_inc(xdt_done, 1)
                if c >= 2:
                    filled(pool, "Y", f"ty{c - 2}", b)
                    pool.wait_ge(ss_done, at(b, NT, c - 1))
                g.tensor_tensor(yy[:, c % 2, :].rearrange("p (g j d) -> p g j d", g=NG, j=GH), x3,
                                row["dskip"][:].rearrange("p (g j o) -> p g j o", g=NG, o=1).to_broadcast(
                                    [P, NG, GH, HD]), ALU.mult).then_inc(dx_done, 1)
                if c < NT - 1:
                    if c:
                        filled(pool, "Y", f"ds{c - 1}", b)
                    pool.wait_ge(xdt_done, at(b, NT, c + 1))
                    pool.wait_ge(decs_done, at(b, 1, 1))
                    g.tensor_tensor(xw[:], xdt[:, c % 2], decs[:, 2, c, :].unsqueeze(2).to_broadcast([P, NH, HD]),
                                    ALU.mult).then_inc(xw_done, 1)

            def chunk(b, c):
                pool.wait_ge(z_done, at(b, NT, c + 1))
                if c:
                    pool.wait_ge(y_done, at(b, NT - 1, c))
                else:
                    pool.wait_ge(yi_done, at(b, NT, 1))
                g.tensor_tensor(yy[:, c % 2, :], yy[:, c % 2, :], zs[:, c, :], ALU.mult).then_inc(yg_done, 1)

            def turned(b, c):
                if c < NT - 1:
                    return
                pool.wait_ge(ss_done, at(b, NT, NT))
                g.tensor_tensor(rms[:], ss[:], ws2_di[:], ALU.mult).then_inc(rms_step, 1)
                pool.wait_ge(rms_step, at(b, 2, 1))
                g.tensor_tensor(rms[:], rms[:], ws2_eps[:], ALU.add).then_inc(rms_step, 1)
                pool.wait_ge(rms_step, at(b, 2, 2))
                g.tensor_tensor(rms[:], rms[:], half[:], ALU.pow).then_inc(rms_done, 1)

            def fc1(b):
                for t in range(KF):
                    pool.wait_ge(glh_done, at(b, KF, t + 1))
                    g.tensor_tensor(gll[:, t, :], gl32[:, t % 2, :], glh[:, t, :], ALU.subtract).then_inc(gll_done, 1)

            per_engine(pool, {
                "weight": weight, "weights at": POOL_LOW_TURN,
                ("W", "vh"): vh, ("X", "res"): lambda b: inv_root("X", b, 0), ("X", "up"): up("X"),
                ("X", "root"): x_root, ("X", "x2"): x_x2, ("Y", "proj"): proj, ("Y", "seg"): seg, ("Y", "pairs"): pairs,
                ("Y", "chunk"): chunk, ("Y", "turned"): turned, ("Y", "fc1"): fc1,
                ("Y", "out"): lambda b: inv_root("Y", b, 0),
                ("Y", "up"): up("Y"), ("Z", "down"): lambda b: inv_root("Y", b, 1)})


def ktiles(w):
    k, c = w.shape
    if k % P:
        w = np.concatenate([w, w[k // P * P:]])
    return np.ascontiguousarray(w.reshape(-1, P, c).transpose(1, 0, 2)).reshape(P, -1)


def up_order(gate, up):
    parts = []
    for t in range(NPAIR):
        parts += [gate[t * P:(t + 1) * P], up[t * P:(t + 1) * P]]
    return np.concatenate(parts + [gate[NPAIR * P:], up[NPAIR * P:]])


def columns(v):
    return np.ascontiguousarray(v.reshape(-1, P).T)


def kernel(**inputs):
    import concourse.bacc as bacc
    from concourse.bass_utils import run_bass_kernel_spmd

    a = {n: np.asarray(x) for n, x in inputs.items()}
    win = a["L1_attn_W_in"]
    z, x, bp, cp, dt_ = np.split(win, [DI, DI + DXB, DI + 2 * DXB, 2 * DI + 2 * DXB], axis=1)
    cp = cp.reshape(D, NG, GH, HD).transpose(0, 2, 1, 3).reshape(D, DI)
    arrays = {
        "x": a["L0_attn_x"], "xt": np.ascontiguousarray(a["L0_attn_x"].transpose(0, 2, 1)),
        "wqkv": ktiles(np.concatenate([a["L0_attn_Wq"].T, a["L0_attn_Wk"].T, a["L0_attn_Wv"].T], axis=1)),
        "wo": ktiles(a["L0_attn_Wo"].T),
        "up0": ktiles(up_order(a["L0_ffn_wq_gate"], a["L0_ffn_wq_up"]).T), "dn0": ktiles(a["L0_ffn_wq_down"].T),
        "win": ktiles(np.concatenate([z, x, bp, dt_, cp], axis=1)), "fc1": ktiles(a["L1_attn_fc1_w"]),
        "wout": ktiles(a["L1_attn_W_out"]), "fc2": ktiles(a["L1_attn_fc2_w"]),
        "up1": ktiles(up_order(a["L1_ffn_gate_w"], a["L1_ffn_up_w"]).T), "dn1": ktiles(a["L1_ffn_down_w"].T),
        "cols": np.concatenate([columns(a["L1_attn_ln_w"]), columns(a["L1_attn_ln_b"]), columns(a["L1_attn_fc1_b"]),
                                columns(a["L1_attn_norm_w"]), columns(up_order(a["L0_ffn_s_gate"], a["L0_ffn_s_up"])),
                                columns(up_order(a["L1_ffn_gate_s"], a["L1_ffn_up_s"]))], axis=1),
        "rows": np.concatenate([a["L1_attn_dt_bias"], a["L1_attn_A_log"], a["L1_attn_D"], a["L0_ffn_s_down"],
                                a["L1_ffn_down_s"], a["L1_attn_fc2_b"]])}
    nc = bacc.Bacc("TRN2", target_bir_lowering=False, num_devices=1, dynamic_dma_scratch_size=1024)
    ins = {n: nc.dram_tensor(f"in_{n}", v.shape, mybir.dt.from_np(v.dtype), kind="ExternalInput").ap()
           for n, v in arrays.items()}
    out = nc.dram_tensor("out", (NB, S, D), F32, kind="ExternalOutput").ap()
    build(nc, ins, out)
    r = run_bass_kernel_spmd(nc, [{f"in_{n}": np.ascontiguousarray(v) for n, v in arrays.items()}], core_ids=[0])
    return r.results[0]["out"]
```
